# Optimizing a Trainium2 kernel written in Bass

```python
import numpy as np
import jax
import jax.numpy as jnp

def _softmax(x, axis=-1):
    return jax.nn.softmax(x, axis=axis)

def _gelu(x):
    return jax.nn.gelu(x, approximate=True)

def _silu(x):
    return jax.nn.silu(x)

def _sigmoid(x):
    return jax.nn.sigmoid(x)

def _layernorm(x, axis=-1, eps=1e-05):
    m = jnp.mean(x, axis=axis, keepdims=True)
    v = jnp.var(x, axis=axis, keepdims=True)
    return (x - m) / jnp.sqrt(v + eps)

def _scatter_add(tgt, idx, src, axis=0):
    return tgt.at[idx].add(src)

def _segment_sum(src, seg, n):
    return jax.ops.segment_sum(src, seg, n)
kernel_name = 'mk_gnn_preln_d4_gnn_r8_98f856'

def setup_inputs(seed: int=0):
    np.random.seed(seed)
    _w = jnp.asarray

    def _rec_inputs():
        import jax
        import jax.numpy as jnp
        _gk = jax.random.key(seed)
        x = -0.0003713 + 1 * jax.random.normal(jax.random.fold_in(_gk, 1), (6250, 256), jnp.float32)
        src = jax.random.randint(jax.random.fold_in(_gk, 2), (100000,), 0, 6250, jnp.int32)
        dst = jax.random.randint(jax.random.fold_in(_gk, 3), (100000,), 0, 6250, jnp.int32)
        _o = jnp.argsort(dst, stable=True)
        src = src[_o]
        dst = dst[_o]
        edge_type_11 = jax.random.randint(jax.random.fold_in(_gk, 13), (100000,), 0, 11, jnp.int32)
        return (x, src, dst, edge_type_11)
    x, src, dst, edge_type_11 = _rec_inputs()

    def _L0_gnn_setup():
        import jax, jax.numpy as jnp
        import numpy as np
        N = 6250
        D = 256
        H = 4
        C = D // H
        E = 100000
        NEG_SLOPE = 0.2
        BN_EPS = 1e-05

        def _batchnorm(x, gamma, beta):
            mean = jnp.mean(x, axis=0)
            var = jnp.mean(jnp.square(x - mean), axis=0)
            return gamma * (x - mean) * jax.lax.rsqrt(var + BN_EPS) + beta
        key = jax.random.key(seed)
        ks = jax.random.split(key, 16)
        s = 0.05
        return {'x': jax.random.normal(ks[0], (N, D), dtype=jnp.float32), 'edge_index': jax.random.randint(ks[1], (2, E), 0, N, dtype=jnp.int64), 'W_l': jax.random.normal(ks[2], (D, H * C), dtype=jnp.float32) * s, 'W_r': jax.random.normal(ks[3], (D, H * C), dtype=jnp.float32) * s, 'att': jax.random.normal(ks[4], (H, C), dtype=jnp.float32) * s, 'bias': jnp.zeros((H * C,), dtype=jnp.float32), 'W1': jax.random.normal(ks[5], (D, D), dtype=jnp.float32) * s, 'b1': jnp.zeros((D,), dtype=jnp.float32), 'W2': jax.random.normal(ks[6], (D, D), dtype=jnp.float32) * s, 'b2': jnp.zeros((D,), dtype=jnp.float32), 'gamma1': jnp.ones((D,), dtype=jnp.float32), 'beta1': jnp.zeros((D,), dtype=jnp.float32), 'gamma2': jnp.ones((D,), dtype=jnp.float32), 'beta2': jnp.zeros((D,), dtype=jnp.float32)}
    _L0_gnn_all = _L0_gnn_setup()
    _L0_gnn_in = {k: v for k, v in _L0_gnn_all.items() if k in ('W_l', 'W_r', 'att', 'bias', 'W1', 'b1', 'W2', 'b2', 'gamma1', 'beta1', 'gamma2', 'beta2')}
    del _L0_gnn_all

    def _L1_gnn_setup():
        import jax, jax.numpy as jnp
        import numpy as np
        N = 12500
        E = 400000
        D_IN = 256
        D_OUT = 256
        NUM_REL = 10
        key = jax.random.key(seed)
        k1, k2, k3, k4, k5, k6 = jax.random.split(key, 6)
        x = jax.random.normal(k1, (N, D_IN), dtype=jnp.float32)
        edge_index = jax.random.randint(k2, (2, E), 0, N, dtype=jnp.int64)
        rel = jax.random.randint(k3, (E,), 0, NUM_REL + 1, dtype=jnp.int64)
        stdv = 1.0 / np.sqrt(D_OUT)
        weight = jax.random.uniform(k4, (D_IN, D_OUT), dtype=jnp.float32, minval=-stdv, maxval=stdv)
        bias = jax.random.uniform(k5, (D_OUT,), dtype=jnp.float32, minval=-stdv, maxval=stdv)
        alpha = jax.random.normal(k6, (NUM_REL + 1, 1), dtype=jnp.float32)
        alpha = alpha.at[0].set(0.0)
        return {'x': x, 'edge_index': edge_index, 'rel': rel, 'weight': weight, 'bias': bias, 'alpha': alpha}
    _L1_gnn_all = _L1_gnn_setup()
    _L1_gnn_in = {k: v for k, v in _L1_gnn_all.items() if k in ('weight', 'bias', 'alpha')}
    del _L1_gnn_all

    def _L2_gnn_setup():
        import jax, jax.numpy as jnp
        import numpy as np
        N_NODES = 6250
        N_EDGES = 100000
        D_IN = 256
        D_HID = 256
        D_OUT = 256

        def _general_conv(x, src, dst, W_msg, b_msg, W_self, b_self, n_nodes):
            msg = x[src] @ W_msg + b_msg
            agg = jax.ops.segment_sum(msg, dst, num_segments=n_nodes)
            return agg + x @ W_self + b_self
        key = jax.random.key(seed)
        ks = jax.random.split(key, 10)
        x = jax.random.normal(ks[0], (N_NODES, D_IN), dtype=jnp.float32)
        edge_index = jax.random.randint(ks[1], (2, N_EDGES), 0, N_NODES, dtype=jnp.int32)
        s_in = 1.0 / np.sqrt(D_IN)
        s_hid = 1.0 / np.sqrt(D_HID)
        return {'x': x, 'edge_index': edge_index, 'W1_msg': jax.random.normal(ks[2], (D_IN, D_HID), dtype=jnp.float32) * s_in, 'b1_msg': jax.random.normal(ks[3], (D_HID,), dtype=jnp.float32) * 0.01, 'W1_self': jax.random.normal(ks[4], (D_IN, D_HID), dtype=jnp.float32) * s_in, 'b1_self': jax.random.normal(ks[5], (D_HID,), dtype=jnp.float32) * 0.01, 'W2_msg': jax.random.normal(ks[6], (D_HID, D_OUT), dtype=jnp.float32) * s_hid, 'b2_msg': jax.random.normal(ks[7], (D_OUT,), dtype=jnp.float32) * 0.01, 'W2_self': jax.random.normal(ks[8], (D_HID, D_OUT), dtype=jnp.float32) * s_hid, 'b2_self': jax.random.normal(ks[9], (D_OUT,), dtype=jnp.float32) * 0.01}
    _L2_gnn_all = _L2_gnn_setup()
    _L2_gnn_in = {k: v for k, v in _L2_gnn_all.items() if k in ('W1_msg', 'b1_msg', 'W1_self', 'b1_self', 'W2_msg', 'b2_msg', 'W2_self', 'b2_self')}
    del _L2_gnn_all

    def _L3_gnn_setup():
        import jax, jax.numpy as jnp
        import numpy as np
        N_NODES = 6250
        N_EDGES = 100000
        DIM = 256
        NUM_HEADS = 8
        key = jax.random.key(seed)
        k_x, k_wu, k_bu, k_wv, k_src, k_dst = jax.random.split(key, 6)
        x = jax.random.normal(k_x, (N_NODES, DIM), dtype=jnp.float32)
        W_u = jax.random.normal(k_wu, (NUM_HEADS, DIM), dtype=jnp.float32) * (1.0 / np.sqrt(DIM))
        b_u = jax.random.normal(k_bu, (NUM_HEADS,), dtype=jnp.float32) * 0.01
        W_v = jax.random.normal(k_wv, (NUM_HEADS, DIM), dtype=jnp.float32) * (1.0 / np.sqrt(DIM))
        src = jax.random.randint(k_src, (N_EDGES,), 0, N_NODES, dtype=jnp.int32)
        dst = jax.random.randint(k_dst, (N_EDGES,), 0, N_NODES, dtype=jnp.int32)
        return {'x': x, 'W_u': W_u, 'b_u': b_u, 'W_v': W_v, 'src': src, 'dst': dst}
    _L3_gnn_all = _L3_gnn_setup()
    _L3_gnn_in = {k: v for k, v in _L3_gnn_all.items() if k in ('W_u', 'b_u', 'W_v')}
    del _L3_gnn_all
    return {'x': x, 'src': src, 'dst': dst, 'edge_type_11': edge_type_11, 'L0_gnn_W_l': _L0_gnn_in['W_l'], 'L0_gnn_W_r': _L0_gnn_in['W_r'], 'L0_gnn_att': _L0_gnn_in['att'], 'L0_gnn_bias': _L0_gnn_in['bias'], 'L0_gnn_W1': _L0_gnn_in['W1'], 'L0_gnn_b1': _L0_gnn_in['b1'], 'L0_gnn_W2': _L0_gnn_in['W2'], 'L0_gnn_b2': _L0_gnn_in['b2'], 'L0_gnn_gamma1': _L0_gnn_in['gamma1'], 'L0_gnn_beta1': _L0_gnn_in['beta1'], 'L0_gnn_gamma2': _L0_gnn_in['gamma2'], 'L0_gnn_beta2': _L0_gnn_in['beta2'], 'L1_gnn_weight': _L1_gnn_in['weight'], 'L1_gnn_bias': _L1_gnn_in['bias'], 'L1_gnn_alpha': _L1_gnn_in['alpha'], 'L2_gnn_W1_msg': _L2_gnn_in['W1_msg'], 'L2_gnn_b1_msg': _L2_gnn_in['b1_msg'], 'L2_gnn_W1_self': _L2_gnn_in['W1_self'], 'L2_gnn_b1_self': _L2_gnn_in['b1_self'], 'L2_gnn_W2_msg': _L2_gnn_in['W2_msg'], 'L2_gnn_b2_msg': _L2_gnn_in['b2_msg'], 'L2_gnn_W2_self': _L2_gnn_in['W2_self'], 'L2_gnn_b2_self': _L2_gnn_in['b2_self'], 'L3_gnn_W_u': _L3_gnn_in['W_u'], 'L3_gnn_b_u': _L3_gnn_in['b_u'], 'L3_gnn_W_v': _L3_gnn_in['W_v']}

def reference(x, src, dst, edge_type_11, L0_gnn_W_l, L0_gnn_W_r, L0_gnn_att, L0_gnn_bias, L0_gnn_W1, L0_gnn_b1, L0_gnn_W2, L0_gnn_b2, L0_gnn_gamma1, L0_gnn_beta1, L0_gnn_gamma2, L0_gnn_beta2, L1_gnn_weight, L1_gnn_bias, L1_gnn_alpha, L2_gnn_W1_msg, L2_gnn_b1_msg, L2_gnn_W1_self, L2_gnn_b1_self, L2_gnn_W2_msg, L2_gnn_b2_msg, L2_gnn_W2_self, L2_gnn_b2_self, L3_gnn_W_u, L3_gnn_b_u, L3_gnn_W_v):
    import jax
    import jax.numpy as jnp

    def _L0_gnn_ref(x, edge_index, W_l, W_r, att, bias, W1, b1, W2, b2, gamma1, beta1, gamma2, beta2):
        import jax, jax.numpy as jnp
        import numpy as np
        N = 6250
        D = 256
        H = 4
        C = D // H
        E = 100000
        NEG_SLOPE = 0.2
        BN_EPS = 1e-05

        def _batchnorm(x, gamma, beta):
            mean = jnp.mean(x, axis=0)
            var = jnp.mean(jnp.square(x - mean), axis=0)
            return gamma * (x - mean) * jax.lax.rsqrt(var + BN_EPS) + beta
        n = x.shape[0]
        loop = jnp.arange(n, dtype=edge_index.dtype)
        src = jnp.concatenate([edge_index[0], loop])
        dst = jnp.concatenate([edge_index[1], loop])
        xl = (x @ W_l).reshape(n, H, C)
        xr = (x @ W_r).reshape(n, H, C)
        feat = xl[src] + xr[dst]
        feat = jnp.where(feat >= 0, feat, NEG_SLOPE * feat)
        logits = jnp.einsum('ehc,hc->eh', feat, att)
        seg_max = jax.ops.segment_max(logits, dst, num_segments=n)
        ex = jnp.exp(logits - seg_max[dst])
        seg_sum = jax.ops.segment_sum(ex, dst, num_segments=n)
        alpha = ex / (seg_sum[dst] + 1e-16)
        msg = alpha[:, :, None] * xl[src]
        out = jax.ops.segment_sum(msg, dst, num_segments=n)
        x_attn = out.reshape(n, H * C) + bias
        h = _batchnorm(x_attn + x, gamma1, beta1)
        ffn = jax.nn.relu(h @ W1 + b1) @ W2 + b2
        return _batchnorm(ffn + h, gamma2, beta2)

    def _L1_gnn_ref(x, edge_index, rel, weight, bias, alpha):
        import jax, jax.numpy as jnp
        import numpy as np
        N = 12500
        E = 400000
        D_IN = 256
        D_OUT = 256
        NUM_REL = 10
        w = alpha[rel, 0]
        support = x @ weight
        row, col = (edge_index[0], edge_index[1])
        out = jax.ops.segment_sum(w[:, None] * support[col], row, num_segments=x.shape[0])
        out = out + jax.ops.segment_sum(w[:, None] * support[row], col, num_segments=x.shape[0])
        return out + bias

    def _L2_gnn_ref(x, edge_index, W1_msg, b1_msg, W1_self, b1_self, W2_msg, b2_msg, W2_self, b2_self):
        import jax, jax.numpy as jnp
        import numpy as np
        N_NODES = 6250
        N_EDGES = 100000
        D_IN = 256
        D_HID = 256
        D_OUT = 256

        def _general_conv(x, src, dst, W_msg, b_msg, W_self, b_self, n_nodes):
            msg = x[src] @ W_msg + b_msg
            agg = jax.ops.segment_sum(msg, dst, num_segments=n_nodes)
            return agg + x @ W_self + b_self
        src = edge_index[0]
        dst = edge_index[1]
        n = x.shape[0]
        h = _general_conv(x, src, dst, W1_msg, b1_msg, W1_self, b1_self, n)
        h = jax.nn.leaky_relu(h, negative_slope=0.1)
        out = _general_conv(h, src, dst, W2_msg, b2_msg, W2_self, b2_self, n)
        return out

    def _L3_gnn_ref(x, W_u, b_u, W_v, src, dst):
        import jax, jax.numpy as jnp
        import numpy as np
        N_NODES = 6250
        N_EDGES = 100000
        DIM = 256
        NUM_HEADS = 8
        n_nodes, dim = x.shape
        num_heads = W_u.shape[0]
        head_dim = dim // num_heads
        s_u = x @ W_u.T + b_u
        s_v = x @ W_v.T
        e = s_u[src] + s_v[dst]
        e = jnp.where(e >= 0, e, 0.2 * e)
        m = jax.ops.segment_max(e, dst, num_segments=n_nodes)
        e_exp = jnp.exp(e - m[dst])
        denom = jax.ops.segment_sum(e_exp, dst, num_segments=n_nodes)
        probs = e_exp / denom[dst]
        xh = x.reshape(n_nodes, head_dim, num_heads)
        msg = xh[src] * probs[:, None, :]
        out = jax.ops.segment_sum(msg, dst, num_segments=n_nodes)
        return out.reshape(n_nodes, dim)
    edge_index = jnp.stack([src, dst])
    h = jnp.maximum(_layernorm(x, axis=-1), 0.0)
    x = x + _L0_gnn_ref(h, edge_index, L0_gnn_W_l, L0_gnn_W_r, L0_gnn_att, L0_gnn_bias, L0_gnn_W1, L0_gnn_b1, L0_gnn_W2, L0_gnn_b2, L0_gnn_gamma1, L0_gnn_beta1, L0_gnn_gamma2, L0_gnn_beta2)
    h = jnp.maximum(_layernorm(x, axis=-1), 0.0)
    x = x + _L1_gnn_ref(h, edge_index, edge_type_11, L1_gnn_weight, L1_gnn_bias, L1_gnn_alpha)
    h = jnp.maximum(_layernorm(x, axis=-1), 0.0)
    x = x + _L2_gnn_ref(h, edge_index, L2_gnn_W1_msg, L2_gnn_b1_msg, L2_gnn_W1_self, L2_gnn_b1_self, L2_gnn_W2_msg, L2_gnn_b2_msg, L2_gnn_W2_self, L2_gnn_b2_self)
    h = jnp.maximum(_layernorm(x, axis=-1), 0.0)
    x = x + _L3_gnn_ref(h, L3_gnn_W_u, L3_gnn_b_u, L3_gnn_W_v, src, dst)
    return x

_drawn_inputs = setup_inputs


def setup_inputs(seed=0):
    import zlib

    import numpy as np

    out = dict(_drawn_inputs(seed))
    spreads = {'L0_gnn_bias': (0.0, 2.0),
     'L0_gnn_b1': (0.0, 2.0),
     'L0_gnn_b2': (0.0, 2.0),
     'L0_gnn_gamma1': (1.0, 0.6),
     'L0_gnn_beta1': (0.0, 2.0),
     'L0_gnn_gamma2': (1.0, 0.2),
     'L0_gnn_beta2': (0.0, 0.1)}
    factors = {'L0_gnn_W_l': 8.0,
     'L0_gnn_W_r': 8.0,
     'L0_gnn_att': 8.0,
     'L0_gnn_W1': 5.067,
     'L0_gnn_W2': 4.98,
     'L1_gnn_bias': 8.0,
     'L2_gnn_b1_msg': 3.538,
     'L2_gnn_b1_self': 49.948,
     'L2_gnn_b2_msg': 34.351,
     'L2_gnn_b2_self': 64.0,
     'L3_gnn_W_u': 64.0,
     'L3_gnn_b_u': 64.0,
     'L3_gnn_W_v': 64.0}
    for name, (base, spread) in spreads.items():
        noise = np.random.default_rng([zlib.crc32(name.encode()), seed]).standard_normal(out[name].shape)
        drawn = base * np.exp(spread * noise) if base else spread * noise
        out[name] = jnp.asarray(drawn.astype(out[name].dtype))
    for name, factor in factors.items():
        out[name] = (out[name] * factor).astype(out[name].dtype)
    return out
```

```python
from contextlib import ExitStack, contextmanager

import numpy as np

import concourse.bass as bass
from concourse import mybir

F32 = mybir.dt.float32
I32 = mybir.dt.int32
ALU = mybir.AluOpType
ACT = mybir.ActivationFunctionType
AX = mybir.AxisListType

P = 128
N, D, E = 6250, 256, 100000
NT = -(-N // P)
NP = NT * P
TAIL = N - (NT - 1) * P
ET = 784
EP = ET * P
S = ET + NT - 1
GS = 8
NG = S // GS
SB = -(-S // P)
SP_ = SB * P
HEADS0, HEADS3 = 4, 8
RELS = 11
LN_EPS = BN_EPS = 1e-5
BIG = 1e30
GT = 7
ND = NP + P
CHAINS = 4
assert S % (2 * GS) == 0 and NT == GT * GT and TAIL > 0


class Token:

    def __init__(self, sem):
        self.sem = sem

    def take(self, eng, n=1):
        eng.wait_ge(self.sem, n)
        eng.sem_inc(self.sem, -n)

    def give(self, eng, n=1):
        eng.sem_inc(self.sem, n)


class Count:

    def __init__(self, sem):
        self.sem, self.base = sem, 0

    def wait(self, eng, value):
        eng.wait_ge(self.sem, value + self.base)


class U:

    def __init__(self, val, c):
        self.val, self.c = val, c


def pipeline(eng, total, body, stages):
    maxlag = max(lag for lag, _ in stages)
    first = -(-maxlag // body) * body
    turns = max(0, (total - first) // body)

    def emit(v, c, inside):
        for lag, fn in stages:
            if inside or 0 <= c - lag < total:
                fn(U(v - lag, c - lag))

    if turns < 2:
        first, turns = total + maxlag, 0
    for v in range(first):
        emit(v, v, False)
    if turns:
        with eng.Fori(0, turns) as i:
            for k in range(body):
                emit(i * body + (first + k), first + k, True)
        for v in range(first + turns * body, total + maxlag):
            emit(v, v, False)


def build(nc, t, out):
    with ExitStack() as top:
        made = {}

        def own(name):
            made[name] = made.get(name, 0) + 1
            return name if made[name] == 1 else f"{name}_{made[name]}"

        def sb(name, shape, dt=F32, ctx=top):
            return ctx.enter_context(nc.sbuf_tensor(own(name), shape, dt))

        def bank(name, ctx):
            return ctx.enter_context(nc.psum_tensor(own(name), [P, 512], F32))

        def sem(name):
            return top.enter_context(nc.semaphore(name))

        def token(name):
            return Token(sem(name))

        A = sb("regionA", [P, NT * 264])
        B = sb("regionB", [P, NT * 265])
        C = sb("regionC", [P, NT * 264])

        def tiles(region, width, cols=None):
            return region[:, 0:NT * width].rearrange("p (t c) -> p t c", c=width)

        def part(region, at, shape):
            n = int(np.prod(shape))
            v = region[:, at:at + n]
            if len(shape) == 2:
                v = v.rearrange("p (a b) -> p a b", b=shape[1])
            elif len(shape) == 3:
                v = v.rearrange("p (a b c) -> p a b c", b=shape[1], c=shape[2])
            return v

        A256, B256, C256 = tiles(A, D), tiles(B, D), tiles(C, D)

        ident = sb("ident", [P, P])
        iota = sb("iota", [P, P])
        gidx = sb("gidx", [P, S], I32)
        rel = sb("rel", [P, S])
        wgt = sb("wgt", [P, S])
        ntab = sb("ntab", [1, SP_], I32)
        dstrow = sb("dstrow", [P, SB, P])
        eps = sb("eps", [P, 1])
        rstd = sb("rstd", [P, NT])
        nmr = sb("nmr", [P, NT])
        deg = sb("deg", [P, NT])

        def dram(name, shape, dt=F32):
            return nc.dram_tensor(name, shape, dt).ap()

        T0, T1, T2, T3 = (dram(f"table{i}", [NP, D]) for i in range(4))
        T4 = dram("table4", [NP, 264])
        srcrow_d = dram("srcrow_d", [S, P])
        Eb = dram("edge_rows", [NG, P, GS * D])
        scat = [dram(f"scatter_sum{k}", [ND, D]) for k in range(CHAINS)]

        s_in = Count(sem("s_in"))
        s_meta = sem("s_meta")
        s_tiles = sem("s_tiles")
        s_st = Count(sem("s_st"))
        s_zero = Count(sem("s_zero"))
        link = {k: token(f"s_link_{k}") for k in ("v", "a", "p", "t")}
        src_full = [token(f"s_src_full{b}") for b in (0, 1)]
        src_free = [token(f"s_src_free{b}") for b in (0, 1)]
        tr_full = [token(f"s_tr_full{b}") for b in (0, 1)]
        lhs_full = [token(f"s_lhs_full{b}") for b in (0, 1)]
        mid_full = [token(f"s_mid_full{b}") for b in (0, 1)]
        act_full = [token(f"s_act_full{b}") for b in (0, 1)]
        res_full = [token(f"s_res_full{b}") for b in (0, 1)]
        res_free = [token(f"s_res_free{b}") for b in (0, 1)]
        hot_full = [token(f"s_hot_full{b}") for b in (0, 1)]
        hot_free = [token(f"s_hot_free{b}") for b in (0, 1)]
        idx_full = [token(f"s_idx_full{b}") for b in (0, 1)]
        slot_free = [token(f"s_slot_free{b}") for b in (0, 1)]
        slot_kept = [token(f"s_slot_kept{b}") for b in (0, 1)]
        aux_full = [token(f"s_aux_full{b}") for b in (0, 1)]
        aux_free = [token(f"s_aux_free{b}") for b in (0, 1)]
        ping, pong, stats_done = token("s_ping"), token("s_pong"), token("s_stats")
        step_full = token("s_step_full")
        s_add = Count(sem("s_add"))
        s_load = [Count(sem(f"s_load{b}")) for b in (0, 1)]
        s_keep = [Count(sem(f"s_keep{b}")) for b in (0, 1)]

        def op(ins, eng, k):
            ins.then_inc(link[k].sem, 1)
            link[k].take(eng)

        def ntile(eng, u, regs):
            eng.load(regs, ntab[0:1, bass.ds(u.val * GS, GS)])
            return [eng.snap(r, min_val=0, max_val=NT - 1) for r in regs]

        def at_tile(view, v):
            return view[:, bass.ds(v, 1), :].rearrange("p a c -> p (a c)")

        def load(sp, dst, src, **kw):
            sp.dma_start(dst, src, **kw).then_inc(s_in.sem, 16)
            s_in.base += 16

        def loaded(eng):
            eng.wait_ge(s_in.sem, s_in.base)

        def store_rows(sp, table, view, width):
            for g in range(GT):
                sp.dma_start(table[g * GT * P:(g + 1) * GT * P, 0:width].rearrange("(t p) c -> p t c", p=P),
                             view[:, g * GT:(g + 1) * GT, 0:width]).then_inc(s_st.sem, 16)
                s_st.base += 16
            sp.wait_ge(s_st.sem, s_st.base)

        def phase():
            return nc.Block()

        with ExitStack() as ctx:
            pss = [bank(f"ps_m{i}", ctx) for i in range(2)]
            keys_i = part(A, 0, [ET]).bitcast(I32)
            keys = part(A, 1000, [ET])
            lane = part(A, 2000, [ET])
            below = part(A, 3000, [ET])
            zeros = part(C, 0, [10, D])
            ers = sb("edge_rows_i", [P, SB, 3 * P], I32, ctx)
            srow = part(A, 4000, [SB, P])
            typ = part(A, 5000, [SB, P])
            wrow = part(A, 6000, [SB, P])
            rrow = part(A, 7000, [SB, P])
            tmp = part(A, 8000, [SB, P])
            alpha = part(A, 9000, [RELS])
            stepno = part(A, 9100, [SB])
            et = part(A, 9200, [SB])
            et_i = part(A, 9300, [SB]).bitcast(I32)
            ntf = part(A, 9400, [SB])
            shift = part(A, 9500, [SB])
            base_in = s_in.base
            with phase() as block:
                @block.sync
                def _(sp):
                    sp.dma_start(keys_i, t["dst_last"].rearrange("(a n) -> a n", a=1).partition_broadcast(P)
                                 .rearrange("q a n -> q (a n)")).then_inc(s_meta, 16)
                    sp.dma_start(alpha, t["L1_gnn_alpha"].rearrange("r a -> a r").partition_broadcast(P)
                                 .rearrange("q a n -> q (a n)"), allow_slow_non_contiguous=True).then_inc(s_meta, 16)
                    ping.take(sp)
                    sp.dma_start(B256[:, 0:NT - 1, :], t["x"][0:(NT - 1) * P, :].rearrange("(t p) c -> p t c", p=P))\
                        .then_inc(s_in.sem, 16)
                    sp.dma_start(B256[0:TAIL, NT - 1, :], t["x"][(NT - 1) * P:N, :]).then_inc(s_in.sem, 16)
                    for k in range(CHAINS):
                        for g in range(5):
                            sp.dma_start(scat[k][g * 10 * P:(g + 1) * 10 * P, :].rearrange("(p r) c -> p r c", p=P),
                                         zeros).then_inc(s_zero.sem, 16)
                    pong.take(sp)
                    for c in range(SB):
                        n = min(P, S - c * P)
                        sp.dma_start(srcrow_d[c * P:c * P + n, :], srow[0:n, c, :]).then_inc(s_st.sem, 16)
                    s_st.base += 16 * SB
                    sp.wait_ge(s_st.sem, s_st.base)
                    sp.wait_ge(s_zero.sem, 16 * 5 * CHAINS)
                    sp.wait_ge(s_in.sem, base_in + 32)

                @block.gpsimd
                def _(g):
                    op(g.memset(ident[:, :], 0.0), g, "p")
                    g.iota(stepno, [[P, SB]], base=0, channel_multiplier=1,
                           allow_small_or_imprecise_dtypes=True)
                    g.iota(lane, [[1, ET]], base=0, channel_multiplier=0, allow_small_or_imprecise_dtypes=True)
                    g.iota(iota[:, :], [[1, P]], base=0, channel_multiplier=0, allow_small_or_imprecise_dtypes=True)
                    op(g.affine_select(out=ident[:, :], in_=ident[:, :], compare_op=ALU.not_equal, fill=1.0,
                                       base=0, pattern=[[-1, P]], channel_multiplier=1), g, "p")
                    hot_full[0].give(g)
                    idx_full[0].take(g)
                    top_edge = g.to_reg(ET - 1)
                    for c in range(SB):
                        g.indirect_dma_start(out=ers[:, c, :], out_offset=None, in_=t["edge_tiles"],
                                             in_offset=bass.IndirectOffsetOnAxis(ap=et_i[:, c:c + 1], axis=0),
                                             bounds_check=top_edge, oob_is_err=True).then_inc(s_tiles, 16)
                    g.wait_ge(s_tiles, 16 * SB)
                    hot_full[1].give(g)

                @block.vector
                def _(v):
                    op(v.memset(B256[:, NT - 1, :], 0.0), v, "v")
                    op(v.memset(zeros, 0.0), v, "v")
                    ping.give(v)
                    v.memset(eps[:, :], LN_EPS)
                    v.wait_ge(s_meta, 32)
                    hot_full[0].take(v)
                    op(v.tensor_scalar(keys_i, keys_i, 7, None, ALU.logical_shift_right), v, "v")
                    op(v.tensor_copy(keys, keys_i), v, "v")
                    op(v.tensor_tensor(keys, keys, lane, ALU.add), v, "v")
                    for c in range(SB):
                        op(v.tensor_scalar(below, keys, stepno[:, c:c + 1], 0.0, ALU.is_lt, ALU.add,
                                           accum_out=et[:, c:c + 1]), v, "v")
                    op(v.tensor_tensor(ntf, stepno, et, ALU.subtract), v, "v")
                    op(v.tensor_scalar(ntf, ntf, float(NT - 1), None, ALU.min), v, "v")
                    op(v.tensor_scalar(et, et, float(ET - 1), None, ALU.min), v, "v")
                    op(v.tensor_copy(et_i, et), v, "v")
                    op(v.tensor_scalar(shift, ntf, float(P), None, ALU.mult), v, "v")
                    idx_full[0].give(v)
                    hot_full[1].take(v)
                    v.tensor_copy(dstrow[:, :, :], ers[:, :, 0:P])
                    v.tensor_copy(srow, ers[:, :, P:2 * P])
                    op(v.tensor_copy(typ, ers[:, :, 2 * P:3 * P]), v, "v")
                    pong.give(v)
                    op(v.memset(wrow, 0.0), v, "v")
                    for c in range(SB):
                        op(v.tensor_scalar(rrow[:, c, :], dstrow[:, c, :], shift[:, c:c + 1], None, ALU.subtract), v, "v")
                    for r in range(RELS):
                        op(v.tensor_scalar(tmp, typ, float(r), alpha[:, r:r + 1], ALU.is_equal, ALU.mult), v, "v")
                        op(v.tensor_tensor(wrow, wrow, tmp, ALU.add), v, "v")
                    src_full[0].give(v)
                    for c in range(SB):
                        n = min(P, S - c * P)
                        tr_full[0].take(v)
                        v.tensor_copy(rel[:, c * P:c * P + n], pss[0][:, 0:n])
                        v.tensor_copy(gidx[:, c * P:c * P + n], pss[0][:, P:P + n])
                        v.tensor_copy(wgt[:, c * P:c * P + n], pss[0][:, 2 * P:2 * P + n])
                        op(v.tensor_copy(ntab[0:1, c * P:(c + 1) * P], pss[0][0:1, 3 * P:4 * P]), v, "v")
                        res_free[0].give(v)

                @block.tensor
                def _(te):
                    src_full[0].take(te)
                    for c in range(SB):
                        if c:
                            res_free[0].take(te)
                        te.transpose(pss[0][:, 0:P], rrow[:, c, :], ident[:, :])
                        te.transpose(pss[0][:, P:2 * P], srow[:, c, :], ident[:, :])
                        te.transpose(pss[0][:, 2 * P:3 * P], wrow[:, c, :], ident[:, :])
                        te.transpose(pss[0][0:1, 3 * P:4 * P], ntf[:, c:c + 1], ident[:, :])\
                            .then_inc(tr_full[0].sem, 1)
                    res_free[0].take(te)
            s_in.base = base_in + 32

        def ln_stats(view):
            with ExitStack() as ctx:
                st = sb("ln_parts", [P, NT, 6], F32, ctx)
                with phase() as block:
                    @block.vector
                    def _(v):
                        def stats(u):
                            v.bn_stats(st[:, bass.ds(u.val, 1), :].rearrange("p a c -> p (a c)"), at_tile(view, u.val))
                        pipeline(v, NT, GT, [(0, stats)])
                        v.drain()
                        me, qe, mo, qo = (st[:, :, k] for k in (1, 2, 4, 5))
                        op(v.tensor_tensor(qe, qe, qo, ALU.add), v, "v")
                        op(v.tensor_tensor(qo, me, mo, ALU.subtract), v, "v")
                        op(v.tensor_tensor(me, me, mo, ALU.add), v, "v")
                        op(v.tensor_tensor(qo, qo, qo, ALU.mult), v, "v")
                        op(v.tensor_scalar(qo, qo, 0.25, None, ALU.mult), v, "v")
                        op(v.scalar_tensor_tensor(out=rstd[:, :], in0=qe, scalar=1.0 / D, in1=qo,
                                                  op0=ALU.mult, op1=ALU.add), v, "v")
                        ping.give(v)
                        pong.take(v)
                        op(v.reciprocal(rstd[:, :], rstd[:, :]), v, "v")
                        op(v.scalar_tensor_tensor(out=nmr[:, :], in0=me, scalar=-0.5, in1=rstd[:, :],
                                                  op0=ALU.mult, op1=ALU.mult), v, "v")

                    @block.scalar
                    def _(a):
                        ping.take(a)
                        a.activation(rstd[:, :], rstd[:, :], ACT.Sqrt, bias=eps[:, 0:1]).then_inc(pong.sem, 1)

        def dense_loop(nsrc, ncols, wload, pre, post, mid_bias=False, nrows=0):
            with ExitStack() as ctx:
                W = sb("weights", [P, max(2 * nsrc, 4 if mid_bias else 2), ncols], F32, ctx)
                rows = sb("bias_rows", [P, 3, D], F32, ctx) if nrows else None
                mb = sb("mid_bias", [P, 2], F32, ctx) if mid_bias else None
                hs = sb("src_tile", [P, 2, nsrc, D], F32, ctx)
                hT = sb("src_tile_T", [P, 2, 2 * nsrc, P], F32, ctx)
                uT = sb("mid_T", [P, 2, 2, P], F32, ctx) if mid_bias else None
                psT = [bank(f"psT{b}", ctx) for b in (0, 1)]
                psO = [bank(f"psO{b}", ctx) for b in (0, 1)]
                psM = [bank(f"psM{b}", ctx) for b in (0, 1)]
                with phase() as block:
                    @block.sync
                    def _(sp):
                        wload(sp, W, rows, mb)
                        sp.wait_ge(s_in.sem, s_in.base)
                        src_full[0].give(sp)
                        aux_full[0].give(sp)
                        aux_full[1].give(sp)

                    @block.scalar
                    def _(a):
                        aux_full[1].take(a)

                        def fill(u):
                            b = u.c % 2
                            src_free[b].take(a)
                            pre(a, u, hs[:, b]).then_inc(hot_full[b].sem, 1)

                        def copyT(u):
                            b = u.c % 2
                            tr_full[b].take(a)
                            a.activation(hT[:, b].rearrange("p k n -> p (k n)"), psT[b][:, 0:2 * nsrc * P], ACT.Copy)\
                                .then_inc(lhs_full[b].sem, 1)

                        def mid(u):
                            b = u.c % 2
                            mid_full[b].take(a)
                            for oc in (0, 1):
                                x = a.activation(uT[:, b, oc, :], psM[b][:, oc * P:(oc + 1) * P], ACT.Relu,
                                                 bias=mb[:, oc:oc + 1])
                            x.then_inc(act_full[b].sem, 1)
                        stages = [(0, fill), (1, copyT)] + ([(2, mid)] if uT is not None else [])
                        pipeline(a, NT, 8, stages)

                    @block.tensor
                    def _(te):
                        src_full[0].take(te)
                        for b in (0, 1):
                            src_free[b].give(te)

                        def trans(u):
                            b = u.c % 2
                            hot_full[b].take(te)
                            for k in range(2 * nsrc):
                                x = te.transpose(psT[b][:, k * P:(k + 1) * P],
                                                 hs[:, b, k // 2, (k % 2) * P:(k % 2 + 1) * P], ident[:, :])
                            x.then_inc(tr_full[b].sem, 1)

                        def midmm(u):
                            b = u.c % 2
                            lhs_full[b].take(te)
                            src_free[b].give(te)
                            for oc in (0, 1):
                                for k in (0, 1):
                                    x = te.matmul(psM[b][:, oc * P:(oc + 1) * P], W[:, 2 + k, oc * P:(oc + 1) * P],
                                                  hT[:, b, k, :], start=k == 0, stop=k == 1)
                            x.then_inc(mid_full[b].sem, 1)

                        def mm(u):
                            b = u.c % 2
                            if uT is None:
                                lhs_full[b].take(te)
                                src_free[b].give(te)
                                lhs = hT
                            else:
                                act_full[b].take(te)
                                lhs = uT
                            res_free[b].take(te)
                            for k in range(2 * nsrc):
                                x = te.matmul(psO[b][:, 0:ncols], lhs[:, b, k, :], W[:, k, 0:ncols],
                                              start=k == 0, stop=k == 2 * nsrc - 1)
                            x.then_inc(res_full[b].sem, 1)
                        pipeline(te, NT, 8, [(0, trans), (1, mm)] if uT is None else [(0, trans), (1, midmm), (2, mm)])
                        for b in (0, 1):
                            src_free[b].take(te)

                    @block.vector
                    def _(v):
                        aux_full[0].take(v)
                        for b in (0, 1):
                            res_free[b].give(v)

                        def use(u):
                            b = u.c % 2
                            res_full[b].take(v)
                            post(v, u, psO[b], rows)
                            res_free[b].give(v)
                        pipeline(v, NT, 8, [(0, use)])
                        for b in (0, 1):
                            res_free[b].take(v)

        def ln_pre(view, keep=None):
            def pre(a, u, hs):
                scale, bias = rstd[:, bass.ds(u.val, 1)], nmr[:, bass.ds(u.val, 1)]
                if keep is not None:
                    a.activation(at_tile(keep, u.val), at_tile(view, u.val), ACT.Relu, bias=bias, scale=scale)
                return a.activation(hs[:, 0, :], at_tile(view, u.val), ACT.Relu, bias=bias, scale=scale)
            return pre

        def bcast_row(ap):
            return ap.rearrange("(a n) -> a n", a=1).partition_broadcast(P).rearrange("q a n -> q (a n)")

        def kchunks(w):
            return w.rearrange("(k p) n -> p k n", p=P)

        def segment_softmax(LG, logits, heads, room, last=None, peak=None):
            H = 4
            RL, FW, BW = (part(room[0], k * 3584, [H, SB, P]) for k in range(3))
            fd, bd, first, final = (part(room[1], k * SB * P, [SB, P]) for k in range(4))
            tmp = part(room[1], 4 * SB * P, [SB, P])
            ends = part(room[1], 4500, [SB, 4, H])
            lastrow = part(room[1], 4700, [SB, P])
            TR = part(room[1], 5600, [4, SP_])[0:H]
            RT = part(room[1], 9200, [4, SP_])[0:H]
            with ExitStack() as ctx:
                carry = sb("carry", [P, SB, 3, H], F32, ctx)
                ps = [bank(f"ps_s{b}", ctx) for b in (0, 1)]
                for h0 in range(0, heads, H):
                    mine = logits[:, :, h0:h0 + H]
                    with phase() as block:
                        @block.tensor
                        def _(te):
                            for c in range(SB):
                                b = c % 2
                                res_free[b].take(te)
                                for h in range(H):
                                    x = te.transpose(ps[b][:, h * P:(h + 1) * P], mine[:, c * P:(c + 1) * P, h],
                                                     ident[:, :])
                                x.then_inc(res_full[b].sem, 1)
                            hot_full[0].take(te)
                            for c in range(SB):
                                b = c % 2
                                res_free[b].take(te)
                                for k in range(4):
                                    x = te.transpose(ps[b][0:H, k * P:(k + 1) * P], ends[:, c, k, :], ident[:, :])
                                x.then_inc(res_full[b].sem, 1)
                            hot_full[1].take(te)
                            for c in range(SB):
                                b = c % 2
                                res_free[b].take(te)
                                for k in range(3):
                                    x = te.transpose(ps[b][:, k * H:(k + 1) * H], RT[:, k, c * P:(c + 1) * P],
                                                     ident[0:H, 0:H])
                                x.then_inc(res_full[b].sem, 1)
                            hot_full[0].take(te)
                            for c in range(SB):
                                b = c % 2
                                res_free[b].take(te)
                                for h in range(H):
                                    x = te.transpose(ps[b][:, h * P:(h + 1) * P], RL[:, h, c, :], ident[:, :])
                                x.then_inc(res_full[b].sem, 1)
                            if last is not None:
                                for c in range(SB):
                                    b = (c + SB) % 2
                                    res_free[b].take(te)
                                    te.transpose(ps[b][:, 0:P], lastrow[:, c, :], ident[:, :])\
                                        .then_inc(res_full[b].sem, 1)

                        @block.vector
                        def _(v):
                            for b in (0, 1):
                                res_free[b].give(v)
                            d = dstrow
                            v.memset(fd[:, :, 0:1], -BIG)
                            v.memset(bd[:, :, P - 1:P], -BIG)
                            op(v.tensor_tensor(tmp[:, :, 1:P], d[:, :, 1:P], d[:, :, 0:P - 1], ALU.not_equal), v, "v")
                            v.tensor_scalar(fd[:, :, 1:P], tmp[:, :, 1:P], -BIG, None, ALU.mult)
                            v.tensor_scalar(bd[:, :, 0:P - 1], tmp[:, :, 1:P], -BIG, None, ALU.mult)
                            op(v.tensor_copy(lastrow[:, :, 0:P - 1], tmp[:, :, 1:P]), v, "v")
                            for mask, end in ((first, 0), (final, P - 1)):
                                op(v.tensor_tensor(mask, d[:, :, :], d[:, :, end:end + 1].to_broadcast([P, SB, P]),
                                                   ALU.not_equal), v, "v")
                                op(v.tensor_scalar(mask, mask, -BIG, None, ALU.mult), v, "v")
                            for c in range(SB):
                                b = c % 2
                                res_full[b].take(v)
                                op(v.tensor_copy(RL[:, :, c, :], ps[b][:, 0:512].rearrange("p (h e) -> p h e", e=P)), v, "v")
                                res_free[b].give(v)
                            flat = lambda x: x.rearrange("p c e -> p (c e)")
                            for h in range(H):
                                v.tensor_tensor_scan(flat(FW[:, h]), flat(fd), flat(RL[:, h]), -BIG, ALU.add, ALU.max)
                                op(v.tensor_tensor_scan(flat(BW[:, h])[:, ::-1], flat(bd)[:, ::-1], flat(RL[:, h])[:, ::-1],
                                                        -BIG, ALU.add, ALU.max), v, "v")
                            for h in range(H):
                                v.tensor_copy(ends[:, :, 0, h:h + 1], FW[:, h, :, P - 1:P])
                                v.tensor_copy(ends[:, :, 1, h:h + 1], BW[:, h, :, 0:1])
                                v.tensor_copy(ends[:, :, 2, h:h + 1], d[:, :, 0:1])
                                op(v.tensor_copy(ends[:, :, 3, h:h + 1], d[:, :, P - 1:P]), v, "v")
                            hot_full[0].give(v)
                            for c in range(SB):
                                b = c % 2
                                res_full[b].take(v)
                                op(v.tensor_copy(TR[:, :, c * P:(c + 1) * P],
                                                 ps[b][0:H, 0:512].rearrange("p (k s) -> p k s", s=P)), v, "v")
                                res_free[b].give(v)
                            fend, bst, d0, d1 = (TR[:, k, :] for k in range(4))
                            cf, cb, cont = (RT[:, k, :] for k in range(3))
                            op(v.memset(cont, 0.0), v, "v")
                            op(v.tensor_tensor(cont[:, 0:SP_ - 1], d0[:, 1:SP_], d1[:, 0:SP_ - 1], ALU.is_equal), v, "v")
                            op(v.tensor_tensor(d0, d0, d1, ALU.is_equal), v, "v")
                            op(v.memset(d1[:, 0:1], 0.0), v, "v")
                            op(v.tensor_tensor(d1[:, 1:SP_], d0[:, 1:SP_], cont[:, 0:SP_ - 1], ALU.mult), v, "v")
                            op(v.tensor_scalar(d1, d1, -1.0, BIG, ALU.add, ALU.mult), v, "v")
                            op(v.tensor_tensor_scan(fend, d1, fend, -BIG, ALU.add, ALU.max), v, "v")
                            op(v.tensor_tensor(d1, d0, cont, ALU.mult), v, "v")
                            op(v.tensor_scalar(d1, d1, -1.0, BIG, ALU.add, ALU.mult), v, "v")
                            op(v.tensor_tensor_scan(bst[:, ::-1], d1[:, ::-1], bst[:, ::-1], -BIG, ALU.add, ALU.max), v, "v")
                            op(v.tensor_scalar(d1, cont, -1.0, BIG, ALU.add, ALU.mult), v, "v")
                            v.memset(cf[:, 0:1], -BIG)
                            v.memset(cb[:, SP_ - 1:SP_], -BIG)
                            op(v.tensor_tensor(cf[:, 1:SP_], fend[:, 0:SP_ - 1], d1[:, 0:SP_ - 1], ALU.add), v, "v")
                            op(v.tensor_tensor(cb[:, 0:SP_ - 1], bst[:, 1:SP_], d1[:, 0:SP_ - 1], ALU.add), v, "v")
                            hot_full[1].give(v)
                            for c in range(SB):
                                b = c % 2
                                res_full[b].take(v)
                                op(v.tensor_copy(carry[:, c, :, :], ps[b][:, 0:3 * H].rearrange("p (k h) -> p k h", h=H)), v, "v")
                                res_free[b].give(v)
                            for h in range(H):
                                op(v.tensor_tensor(RL[:, h], FW[:, h], BW[:, h], ALU.max), v, "v")
                                for k, mask in ((0, first), (1, final)):
                                    op(v.tensor_tensor(tmp, mask, carry[:, :, k, h:h + 1].to_broadcast([P, SB, P]),
                                                       ALU.add), v, "v")
                                    op(v.tensor_tensor(RL[:, h], RL[:, h], tmp, ALU.max), v, "v")
                            op(v.tensor_scalar(lastrow[:, :, P - 1:P], carry[:, :, 2, 0:1], -1.0, 1.0, ALU.mult, ALU.add), v, "v")
                            hot_full[0].give(v)
                            MX = part(room[0], 3584, [SB, P, H])
                            for c in range(SB):
                                b = c % 2
                                res_full[b].take(v)
                                op(v.tensor_copy(MX[:, c], ps[b][:, 0:512].rearrange("p (h s) -> p s h", s=P)), v, "v")
                                res_free[b].give(v)
                            mx = MX.rearrange("p c s h -> p (c s) h")
                            if last is not None:
                                for c in range(SB):
                                    b = (c + SB) % 2
                                    res_full[b].take(v)
                                    op(v.tensor_copy(last[:, c * P:(c + 1) * P], ps[b][:, 0:P]), v, "v")
                                    res_free[b].give(v)
                                v.tensor_tensor(peak[:, :, :], mx, last[:, :].unsqueeze(2).to_broadcast([P, SP_, H]), ALU.mult)
                            op(v.tensor_tensor(mine, mine, mx, ALU.subtract), v, "v")
                            ping.give(v)
                            for b in (0, 1):
                                res_free[b].take(v)

                        @block.scalar
                        def _(a):
                            ping.take(a)
                            op(a.activation(mine, mine, ACT.Exp), a, "a")


        def one_hot(v, hot, j, s, weighted):
            if weighted:
                return v.tensor_scalar(hot[:, j, :], iota[:, :], rel[:, bass.ds(s, 1)], wgt[:, bass.ds(s, 1)],
                                       ALU.is_equal, ALU.mult)
            return v.tensor_scalar(hot[:, j, :], iota[:, :], rel[:, bass.ds(s, 1)], None, ALU.is_equal)

        def rows_count(name):
            return [Count(sem(f"s_rows_{name}{b}")) for b in (0, 1)]

        def add_steps(v, u, regs, acc, ps, width, nbank):
            nt = ntile(v, u, regs)
            for j in range(GS):
                step_full.take(v)
                s_add.wait(v, u.val * GS + (j + nbank))
                dst_ = at_tile(acc, nt[j])
                v.tensor_tensor(dst_, dst_, ps[(u.c * GS + j) % nbank][:, 0:width], ALU.add).then_inc(s_add.sem, 1)

        def zero_acc(v, acc_flat, nbank):
            op(v.memset(acc_flat, 0.0), v, "v")
            s_add_start(v, nbank)

        def s_add_start(v, nbank):
            v.sem_inc(s_add.sem, nbank)

        def copy_idx(a, idx, u, b):
            return a.activation(idx[:, b, :], gidx[:, bass.ds(u.val * GS, GS)], ACT.Copy)

        def plain_pass(name, table, acc, acc_flat, width, weighted):
            NB = 4
            s_rows = rows_count(name)
            with ExitStack() as ctx:
                G = sb("rows_in", [P, 2, GS, width], F32, ctx)
                hot = sb("hot", [P, 2, GS, P], F32, ctx)
                idx = sb("idx", [P, 2, GS], I32, ctx)
                ps = [bank(f"ps_p{i}", ctx) for i in range(NB)]
                with phase() as block:
                    @block.scalar
                    def _(a):
                        def index(u):
                            b = u.c % 2
                            slot_free[b].take(a)
                            copy_idx(a, idx, u, b).then_inc(idx_full[b].sem, 1)
                        pipeline(a, NG, 2, [(0, index)])

                    @block.gpsimd
                    def _(g):
                        top_row = g.to_reg(NP - 1)

                        def fetch(u):
                            b = u.c % 2
                            idx_full[b].take(g)
                            for j in range(GS):
                                g.indirect_dma_start(out=G[:, b, j, 0:D], out_offset=None, in_=table,
                                                     in_offset=bass.IndirectOffsetOnAxis(ap=idx[:, b, j:j + 1], axis=0),
                                                     bounds_check=top_row, oob_is_err=True).then_inc(s_rows[b].sem, 16)
                        pipeline(g, NG, 2, [(0, fetch)])

                    @block.tensor
                    def _(te):
                        def multiply(u):
                            b, turn = u.c % 2, u.c // 2
                            hot_full[b].take(te)
                            s_rows[b].wait(te, (u.val - b) * (16 * GS // 2) + 16 * GS)
                            for j in range(GS):
                                s_add.wait(te, u.val * GS + (j + 1))
                                te.matmul(ps[(u.c * GS + j) % NB][:, 0:width], hot[:, b, j, :], G[:, b, j, :],
                                          start=True, stop=True).then_inc(step_full.sem, 1)
                        pipeline(te, NG, 2, [(0, multiply)])

                    @block.vector
                    def _(v):
                        regs = [v.alloc_register(f"nt_{name}{j}") for j in range(GS)]
                        if width > D:
                            op(v.memset(G[:, :, :, D:width], 1.0), v, "v")
                        for b in (0, 1):
                            slot_free[b].give(v)
                        zero_acc(v, acc_flat, NB)

                        def hots(u):
                            b = u.c % 2
                            for j in range(GS):
                                x = one_hot(v, hot[:, b], j, u.val * GS + j, weighted)
                            x.then_inc(hot_full[b].sem, 1)

                        def adds(u):
                            add_steps(v, u, regs, acc, ps, width, NB)
                            slot_free[u.c % 2].give(v)
                        pipeline(v, NG, 2, [(0, hots), (1, adds)])
                        for b in (0, 1):
                            slot_free[b].take(v)
            s_add.base += S + NB

        def attention_fetch0(LG, attc, room):
            PAIRS = S // 2
            G = part(room, 0, [2, GS * D])
            s_rows = rows_count("att0_")
            with ExitStack() as ctx:
                hot = sb("hot", [P, 2, 2, P], F32, ctx)
                hotT = sb("hotT", [P, 2, 2, P], F32, ctx)
                feat = sb("feat", [P, 2, 2 * D], F32, ctx)
                featT = sb("featT", [P, 2, 4, P], F32, ctx)
                idx = sb("idx", [P, 2, GS], I32, ctx)
                psT = [bank(f"psT{b}", ctx) for b in (0, 1)]
                psX = [bank(f"psX{b}", ctx) for b in (0, 1)]
                psF = [bank(f"psF{b}", ctx) for b in (0, 1)]
                psL = [bank(f"psL{b}", ctx) for b in (0, 1)]
                QP = GS // 2
                with phase() as block:
                    @block.sync
                    def _(sp):
                        def keep(u):
                            b = u.c % 2
                            s_rows[b].wait(sp, (u.val - b) * (16 * GS // 2) + 16 * GS)
                            sp.dma_start(Eb[bass.ds(u.val, 1), :, :].rearrange("a p c -> p (a c)"),
                                         G[:, b, :]).then_inc(s_keep[b].sem, 16)

                        def kept(u):
                            b = u.c % 2
                            s_keep[b].wait(sp, (u.val - b) * 8 + 16)
                            slot_kept[b].give(sp)
                        for b in (0, 1):
                            slot_kept[b].give(sp)
                        pipeline(sp, NG, 2, [(0, keep), (1, kept)])
                        for b in (0, 1):
                            slot_kept[b].take(sp)

                    @block.gpsimd
                    def _(g):
                        top_row = g.to_reg(NP - 1)

                        def fetch(u):
                            b = u.c % 2
                            idx_full[b].take(g)
                            for j in range(GS):
                                g.indirect_dma_start(out=G[:, b, j * D:(j + 1) * D], out_offset=None, in_=T0,
                                                     in_offset=bass.IndirectOffsetOnAxis(ap=idx[:, b, j:j + 1], axis=0),
                                                     bounds_check=top_row, oob_is_err=True).then_inc(s_rows[b].sem, 16)
                        pipeline(g, NG, 2, [(0, fetch)])

                    @block.scalar
                    def _(a):
                        def index(u):
                            if u.c % QP:
                                return
                            b = u.c // QP % 2
                            slot_free[b].take(a)
                            slot_kept[b].take(a)
                            a.activation(idx[:, b, :], gidx[:, bass.ds(u.val * 2, GS)], ACT.Copy)\
                                .then_inc(idx_full[b].sem, 1)

                        def copyT(u):
                            b = u.c % 2
                            tr_full[b].take(a)
                            a.activation(hotT[:, b].rearrange("p k n -> p (k n)"), psT[b][:, 0:2 * P], ACT.Copy)\
                                .then_inc(lhs_full[b].sem, 1)

                        def copyF(u):
                            b = u.c % 2
                            mid_full[b].take(a)
                            a.activation(featT[:, b].rearrange("p k n -> p (k n)"), psF[b][:, :], ACT.Copy)\
                                .then_inc(act_full[b].sem, 1)
                        pipeline(a, PAIRS, 2 * QP, [(0, index), (1, copyT), (3, copyF)])

                    @block.tensor
                    def _(te):
                        regs = [te.alloc_register(f"nt_att0{j}") for j in range(GS)]
                        nts = [None, None]

                        def trans(u):
                            b = u.c % 2
                            hot_full[b].take(te)
                            for k in (0, 1):
                                x = te.transpose(psT[b][:, k * P:(k + 1) * P], hot[:, b, k, :], ident[:, :])
                            x.then_inc(tr_full[b].sem, 1)

                        def fetch_xr(u):
                            b = u.c % 2
                            nt = [te.snap(r, min_val=0, max_val=NT - 1) for r in regs[0:2]]
                            lhs_full[b].take(te)
                            res_free[b].take(te)
                            for k in (0, 1):
                                x = te.matmul(psX[b][:, k * D:(k + 1) * D], hotT[:, b, k, :], at_tile(A256, nt[k]),
                                              start=True, stop=True)
                            x.then_inc(res_full[b].sem, 1)

                        def load_nt(u):
                            te.load(regs[0:2], ntab[0:1, bass.ds(u.val * 2, 2)])

                        def transF(u):
                            b = u.c % 2
                            src_full[b].take(te)
                            for k in range(4):
                                x = te.transpose(psF[b][:, k * P:(k + 1) * P], feat[:, b, k * P:(k + 1) * P], ident[:, :])
                            x.then_inc(mid_full[b].sem, 1)

                        def logit(u):
                            b, gb = u.c % 2, u.c // QP % 2
                            act_full[b].take(te)
                            if u.c % QP == 0:
                                aux_free[gb].take(te)
                            for k in (0, 1):
                                col = (u.c % QP * 2 + k) * HEADS0
                                for c in (0, 1):
                                    x = te.matmul(psL[gb][:, col:col + HEADS0], featT[:, b, 2 * k + c, :], attc[:, c, :],
                                                  start=c == 0, stop=c == 1)
                            if u.c % QP == QP - 1:
                                x.then_inc(aux_full[gb].sem, 1)
                        pipeline(te, PAIRS, 2 * QP, [(0, trans), (1, load_nt), (1, fetch_xr), (2, transF), (3, logit)])

                    @block.vector
                    def _(v):
                        for b in (0, 1):
                            slot_free[b].give(v)
                            res_free[b].give(v)
                            aux_free[b].give(v)

                        def hots(u):
                            b = u.c % 2
                            for k in (0, 1):
                                x = one_hot(v, hot[:, b], k, u.val * 2 + k, False)
                            x.then_inc(hot_full[b].sem, 1)

                        def feats(u):
                            b, gb = u.c % 2, u.c // QP % 2
                            if u.c % QP == 0:
                                s_rows[gb].wait(v, (u.val - (u.c % (2 * QP))) * (16 * GS // (2 * QP)) + 16 * GS)
                            res_full[b].take(v)
                            op(v.tensor_tensor(feat[:, b, :], G[:, gb, u.c % QP * 2 * D:(u.c % QP + 1) * 2 * D],
                                               psX[b][:, :], ALU.add), v, "v")
                            op(v.scalar_tensor_tensor(out=feat[:, b, :], in0=feat[:, b, :], scalar=0.2, in1=feat[:, b, :],
                                                      op0=ALU.mult, op1=ALU.max), v, "v")
                            src_full[b].give(v)
                            res_free[b].give(v)
                            if u.c % QP == QP - 1:
                                slot_free[gb].give(v)

                        def logits_out(u):
                            gb = u.c // QP % 2
                            if u.c % QP != QP - 1:
                                return
                            aux_full[gb].take(v)
                            op(v.tensor_copy(LG[:, bass.ds((u.val - (QP - 1)) * 2, GS), :],
                                             psL[gb][:, 0:GS * HEADS0].rearrange("p (s h) -> p s h", h=HEADS0)), v, "v")
                            aux_free[gb].give(v)
                        pipeline(v, PAIRS, 2 * QP, [(2, feats), (0, hots), (4, logits_out)])
                        for b in (0, 1):
                            slot_free[b].take(v)
                            res_free[b].take(v)
                            aux_free[b].take(v)
            for b in (0, 1):
                s_keep[b].base += 16 * NG // 2

        def attention_sum(name, LG, heads, head_major, extras, acc, acc_flat, room):
            NB = 4
            width = D + heads + sum(k for _, k in extras)
            GL = part(room, 0, [2, GS, D])
            Gs = part(room, 2 * GS * D, [2 * GS, width])
            hot = part(room, 2 * GS * (D + width), [2 * GS, P])
            with ExitStack() as ctx:
                ps = [bank(f"ps_p{i}", ctx) for i in range(NB)]
                with phase() as block:
                    @block.sync
                    def _(sp):
                        def back(u):
                            b = u.c % 2
                            src_free[b].take(sp)
                            sp.dma_start(GL[:, b].rearrange("p s c -> p (s c)"),
                                         Eb[bass.ds(u.val, 1), :, :].rearrange("a p c -> p (a c)"))\
                                .then_inc(s_load[b].sem, 16)
                        pipeline(sp, NG, 2, [(0, back)])

                    @block.gpsimd
                    def _(g):
                        for b in (0, 1):
                            src_free[b].give(g)

                        def scale(u):
                            b = u.c % 2
                            s_load[b].wait(g, (u.val - b) * 8 + 16)
                            slot_free[b].take(g)
                            w = LG[:, bass.ds(u.val * GS, GS), :]
                            out_ = Gs[:, b * GS:(b + 1) * GS, 0:D]
                            if head_major:
                                o = out_.rearrange("p s (h c) -> p s h c", h=heads)
                                i = GL[:, b].rearrange("p s (h c) -> p s h c", h=heads)
                                w = w.unsqueeze(3).to_broadcast([P, GS, heads, D // heads])
                            else:
                                o = out_.rearrange("p s (c h) -> p s c h", h=heads)
                                i = GL[:, b].rearrange("p s (c h) -> p s c h", h=heads)
                                w = w.unsqueeze(2).to_broadcast([P, GS, D // heads, heads])
                            op(g.tensor_tensor(o, i, w, ALU.mult), g, "p")
                            aux_full[b].give(g)
                            src_free[b].give(g)
                        pipeline(g, NG, 2, [(0, scale)])
                        for b in (0, 1):
                            src_free[b].take(g)

                    @block.scalar
                    def _(a):
                        def more(u):
                            b = u.c % 2
                            slot_kept[b].take(a)
                            at = D
                            for table, k in [(LG, heads)] + extras:
                                x = a.activation(Gs[:, b * GS:(b + 1) * GS, at:at + k],
                                                 table[:, bass.ds(u.val * GS, GS), :], ACT.Copy)
                                at += k
                            x.then_inc(lhs_full[b].sem, 1)
                        pipeline(a, NG, 2, [(0, more)])

                    @block.tensor
                    def _(te):
                        def multiply(u):
                            b = u.c % 2
                            hot_full[b].take(te)
                            aux_full[b].take(te)
                            lhs_full[b].take(te)
                            for j in range(GS):
                                s_add.wait(te, u.val * GS + (j + 1))
                                te.matmul(ps[(u.c * GS + j) % NB][:, 0:width], hot[:, b * GS + j, :],
                                          Gs[:, b * GS + j, :], start=True, stop=True).then_inc(step_full.sem, 1)
                        pipeline(te, NG, 2, [(0, multiply)])

                    @block.vector
                    def _(v):
                        regs = [v.alloc_register(f"nt_{name}{j}") for j in range(GS)]
                        for b in (0, 1):
                            slot_free[b].give(v)
                            slot_kept[b].give(v)
                        zero_acc(v, acc_flat, NB)

                        def hots(u):
                            b = u.c % 2
                            for j in range(GS):
                                x = one_hot(v, hot[:, b * GS:(b + 1) * GS], j, u.val * GS + j, False)
                            x.then_inc(hot_full[b].sem, 1)

                        def adds(u):
                            add_steps(v, u, regs, acc, ps, width, NB)
                            slot_free[u.c % 2].give(v)
                            slot_kept[u.c % 2].give(v)
                        pipeline(v, NG, 2, [(0, hots), (1, adds)])
                        for b in (0, 1):
                            slot_free[b].take(v)
                            slot_kept[b].take(v)
            s_add.base += S + NB
            for b in (0, 1):
                s_load[b].base += 16 * NG // 2

        def grp(view, u, n=GT):
            return view[:, bass.ds(u.val * n, n), :]

        def column_norm(Y, gamma, beta, finish):
            with ExitStack() as ctx:
                ones = sb("ones", [P, 2, P], F32, ctx)
                sq = sb("squares", [P, 2, GT, D], F32, ctx)
                gb = sb("gamma_beta", [P, 2, D], F32, ctx)
                mean = sb("mean", [P, D], F32, ctx)
                psS = bank("ps_sum", ctx)
                psQ = bank("ps_sq", ctx)
                with phase() as block:
                    @block.sync
                    def _(sp):
                        load(sp, gb[:, 0, :], bcast_row(gamma))
                        load(sp, gb[:, 1, :], bcast_row(beta))
                        sp.wait_ge(s_in.sem, s_in.base)
                        aux_full[0].give(sp)

                    @block.gpsimd
                    def _(g):
                        op(g.memset(ones[:, 0, :], 1.0), g, "p")
                        op(g.affine_select(out=ones[:, 1, :], in_=ones[:, 0, :], compare_op=ALU.is_ge, fill=0.0,
                                           base=TAIL - 1, pattern=[[0, P]], channel_multiplier=-1), g, "p")
                        hot_full[0].give(g)

                    def sums(te, rhs_of, ps, before=None):
                        def one(u):
                            if before:
                                before(u)
                            last_ = isinstance(u.val, int) and u.val == NT - 1
                            x = te.matmul(ps[:, 0:D], ones[:, 1 if last_ else 0, :], rhs_of(u),
                                          start=isinstance(u.val, int) and u.val == 0, stop=last_)
                            return x
                        return one

                    @block.tensor
                    def _(te):
                        hot_full[0].take(te)
                        one = sums(te, lambda u: at_tile(Y, u.val), psS)
                        one(U(0, 0))
                        with te.Fori(1, NT - 1) as i:
                            one(U(i, 1))
                        one(U(NT - 1, 0)).then_inc(ping.sem, 1)

                        def square_group(u):
                            b = u.c % 2
                            src_full[b].take(te)
                            for j in range(GT):
                                first = u.c == 0 and isinstance(u.val, int) and u.val == 0 and j == 0
                                last_ = isinstance(u.val, int) and u.val == GT - 1 and j == GT - 1
                                x = te.matmul(psQ[:, 0:D], ones[:, 1 if last_ else 0, :], sq[:, b, j, :],
                                              start=first, stop=last_)
                            x.then_inc(src_free[b].sem, 1)
                        square_group(U(0, 0))
                        with te.Fori(0, 2) as i:
                            square_group(U(i * 2 + 1, 1))
                            square_group(U(i * 2 + 2, 2))
                        square_group(U(GT - 2, GT - 2))
                        square_group(U(GT - 1, GT - 1))

                    @block.scalar
                    def _(a):
                        for b in (0, 1):
                            src_free[b].give(a)

                        def square(u):
                            b = u.c % 2
                            res_full[0].take(a)
                            src_free[b].take(a)
                            a.activation(sq[:, b], grp(Y, u), ACT.Square).then_inc(src_full[b].sem, 1)
                        pipeline(a, GT, 2, [(0, square)])
                        for b in (0, 1):
                            src_free[b].take(a)
                        pong.give(a)
                        stats_done.take(a)
                        a.activation(mean[:, :], mean[:, :], ACT.Sqrt, bias=eps[:, 0:1]).then_inc(mid_full[0].sem, 1)

                    @block.vector
                    def _(v):
                        ping.take(v)
                        op(v.tensor_scalar(mean[:, :], psS[:, 0:D], 1.0 / N, None, ALU.mult), v, "v")

                        def center(u):
                            y = grp(Y, u)
                            op(v.tensor_tensor(y, y, mean[:, :].unsqueeze(1).to_broadcast([P, GT, D]), ALU.subtract), v, "v")
                            res_full[0].give(v)
                        pipeline(v, GT, 2, [(0, center)])
                        pong.take(v)
                        aux_full[0].take(v)
                        v.drain()
                        op(v.tensor_scalar(mean[:, :], psQ[:, 0:D], 1.0 / N, None, ALU.mult), v, "v")
                        stats_done.give(v)
                        mid_full[0].take(v)
                        op(v.reciprocal(mean[:, :], mean[:, :]), v, "v")
                        op(v.tensor_tensor(mean[:, :], mean[:, :], gb[:, 0, :], ALU.mult), v, "v")

                        def scale(u):
                            y = grp(Y, u)
                            op(v.tensor_tensor(y, y, mean[:, :].unsqueeze(1).to_broadcast([P, GT, D]), ALU.mult), v, "v")
                            op(v.tensor_tensor(y, y, gb[:, 1, :].unsqueeze(1).to_broadcast([P, GT, D]), ALU.add), v, "v")
                            if finish:
                                finish(v, u, y)
                        pipeline(v, GT, GT, [(0, scale)])


        def scatter_pass(SUP):
            Q = 4
            NQ = S // Q
            room = 0
            with ExitStack() as ctx:
                hot = sb("hot", [P, 2, Q, P], F32, ctx)
                same = sb("same", [P, 2, Q, P], F32, ctx)
                srow = sb("src_rows", [P, 2, Q, P], F32, ctx)
                before = sb("before", [P, Q, P], F32, ctx)
                lower = sb("lower", [P, P], F32, ctx)
                pairs = sb("pairs", [P, 2, Q, P], F32, ctx)
                sums = sb("sums", [P, 2, Q, D], F32, ctx)
                dump_row = sb("dump_row", [P, 1], F32, ctx)
                cnt = sb("count", [P, Q], F32, ctx)
                away = sb("away", [P, Q], F32, ctx)
                srcs = sb("srcs", [P, Q], F32, ctx)
                idx = sb("idx", [P, 2, Q], I32, ctx)
                psC = [bank(f"psC{b}", ctx) for b in (0, 1)]
                psO = [bank(f"psO{i}", ctx) for i in range(4)]
                s_scat = [Count(sem(f"s_scat{k}")) for k in range(CHAINS)]
                with phase() as block:
                    @block.sync
                    def _(sp):
                        def rows_in(u):
                            b = u.c % 2
                            src_free[b].take(sp)
                            sp.dma_start(srow[:, b].rearrange("p q e -> p (q e)"),
                                         srcrow_d[bass.ds(u.val * Q, Q), :].rearrange("(a q) e -> a (q e)", a=1)
                                         .partition_broadcast(P).rearrange("p a e -> p (a e)")).then_inc(s_load[b].sem, 16)
                        pipeline(sp, NQ, 2, [(0, rows_in)])

                    @block.gpsimd
                    def _(g):
                        op(g.memset(lower[:, :], 1.0), g, "p")
                        g.iota(dump_row[:, :], [[0, 1]], base=NP, channel_multiplier=1,
                               allow_small_or_imprecise_dtypes=True)
                        op(g.affine_select(out=lower[:, :], in_=lower[:, :], compare_op=ALU.is_gt, fill=0.0,
                                           base=0, pattern=[[-1, P]], channel_multiplier=1), g, "p")
                        hot_free[0].give(g)
                        nought, bound = g.alloc_register("nought"), g.alloc_register("last_row")
                        g.reg_mov(nought, 0)
                        for b in (0, 1):
                            slot_free[b].give(g)

                        def scatter(u):
                            b = u.c % 2
                            idx_full[b].take(g)
                            mid_full[b].take(g)
                            for j in range(Q):
                                k = j % CHAINS
                                if not (isinstance(u.val, int) and u.val == 0):
                                    s_scat[k].wait(g, u.val * 16)
                                g.reg_add(bound, nought, ND - 1)
                                g.indirect_dma_start(out=scat[k], out_offset=bass.IndirectOffsetOnAxis(ap=idx[:, b, j:j + 1], axis=0),
                                                     in_=sums[:, b, j, :], in_offset=None, bounds_check=bound,
                                                     oob_is_err=True, compute_op=ALU.add).then_inc(s_scat[k].sem, 16)

                        def landed(u):
                            b = u.c % 2
                            for k in range(CHAINS):
                                s_scat[k].wait(g, u.val * 16 + 16)
                                g.reg_add(bound, nought, ND - 1)
                            slot_free[b].give(g)
                            slot_kept[b].give(g)
                        pipeline(g, NQ, 2, [(0, scatter), (1, landed)])
                        for b in (0, 1):
                            slot_free[b].take(g)
                            slot_kept[b].take(g)

                    @block.scalar
                    def _(a):
                        def copyC(u):
                            b = u.c % 2
                            tr_full[b].take(a)
                            a.activation(pairs[:, b].rearrange("p q e -> p (q e)"), psC[b][:, :], ACT.Copy)\
                                .then_inc(lhs_full[b].sem, 1)

                        def copyO(u):
                            b = u.c % 2
                            slot_free[b].take(a)
                            for j in range(2):
                                res_full[j].take(a)
                                op(a.activation(sums[:, b, 2 * j:2 * j + 2, :].rearrange("p q c -> p (q c)"),
                                                psO[2 * b + j][:, :], ACT.Copy), a, "a")
                                res_free[j].give(a)
                            mid_full[b].give(a)
                        for j in (0, 1):
                            res_free[j].give(a)
                            res_free[j].give(a)
                        pipeline(a, NQ, 2, [(0, copyC), (1, copyO)])
                        for j in (0, 1):
                            res_free[j].take(a, 2)

                    @block.tensor
                    def _(te):
                        regs = [te.alloc_register(f"nt_sc{j}") for j in range(Q)]

                        def pairmm(u):
                            b = u.c % 2
                            hot_full[b].take(te)
                            for j in range(Q):
                                x = te.matmul(psC[b][:, j * P:(j + 1) * P], hot[:, b, j, :], same[:, b, j, :],
                                              start=True, stop=True)
                            x.then_inc(tr_full[b].sem, 1)

                        def summm(u):
                            b = u.c % 2
                            te.load(regs, ntab[0:1, bass.ds(u.val * Q, Q)])
                            nt = [te.snap(r, min_val=0, max_val=NT - 1) for r in regs]
                            lhs_full[b].take(te)
                            for j in range(Q):
                                if j % 2 == 0:
                                    res_free[j // 2].take(te)
                                x = te.matmul(psO[2 * b + j // 2][:, j % 2 * D:(j % 2 + 1) * D], pairs[:, b, j, :],
                                              at_tile(SUP, nt[j]), start=True, stop=True)
                                if j % 2:
                                    x.then_inc(res_full[j // 2].sem, 1)
                            te.sem_inc(hot_free[1].sem, 1)
                        pipeline(te, NQ, 2, [(0, pairmm), (1, summm)])

                    @block.vector
                    def _(v):
                        for b in (0, 1):
                            src_free[b].give(v)
                            slot_kept[b].give(v)
                        hot_free[0].take(v)

                        def marks(u):
                            b = u.c % 2
                            s_ = u.val * Q
                            hot_free[1].take(v)
                            for j in range(Q):
                                one_hot(v, hot[:, b], j, s_ + j, True)
                            op(v.tensor_copy(srcs[:, :], gidx[:, bass.ds(s_, Q)]), v, "v")
                            s_load[b].wait(v, (u.val - b) * 8 + 16)
                            for j in range(Q):
                                x = v.tensor_scalar(same[:, b, j, :], srow[:, b, j, :], srcs[:, j:j + 1], None, ALU.is_equal)
                            op(x, v, "v")
                            v.drain()
                            hot_full[b].give(v)
                            src_free[b].give(v)
                            op(v.tensor_tensor(before[:, :, :], same[:, b], lower[:, :].unsqueeze(1).to_broadcast([P, Q, P]),
                                               ALU.mult), v, "v")
                            op(v.tensor_reduce(cnt[:, :], before[:, :, :], AX.X, ALU.add), v, "v")
                            v.tensor_scalar(away[:, :], srcs[:, :], -1.0, dump_row[:, 0:1], ALU.mult, ALU.add)
                            op(v.tensor_scalar(cnt[:, :], cnt[:, :], 0.0, None, ALU.is_gt), v, "v")
                            op(v.tensor_tensor(cnt[:, :], cnt[:, :], away[:, :], ALU.mult), v, "v")
                            slot_kept[b].take(v)
                            op(v.tensor_tensor(idx[:, b, :], cnt[:, :], srcs[:, :], ALU.add), v, "v")
                            idx_full[b].give(v)
                        hot_free[1].give(v, 2)
                        pipeline(v, NQ, 2, [(0, marks)])
                        for b in (0, 1):
                            src_free[b].take(v)
                        hot_free[1].take(v, 2)
            for b in (0, 1):
                s_load[b].base += 16 * NQ // 2

        def attention_fetch3(LG, SV, rows_room, T_room, WT):
            G = part(rows_room, 0, [2, GS, WT])
            s_rows = rows_count("att3_")
            with ExitStack() as ctx:
                hot = part(T_room, 0, [2 * GS, P])
                hotT = part(T_room, 2 * GS * P, [2 * GS, P])
                raw = sb("raw_logits", [P, GS, HEADS3], F32, ctx)
                idx = sb("idx", [P, 2, GS], I32, ctx)
                psT = [[bank(f"psT{b}{k}", ctx) for k in (0, 1)] for b in (0, 1)]
                psS = [bank(f"psS{b}", ctx) for b in (0, 1)]
                with phase() as block:
                    @block.sync
                    def _(sp):
                        def keep(u):
                            b = u.c % 2
                            s_rows[b].wait(sp, (u.val - b) * (16 * GS // 2) + 16 * GS)
                            sp.dma_start(Eb[bass.ds(u.val, 1), :, :].rearrange("a p (s c) -> p (a s) c", c=D),
                                         G[:, b, :, 0:D]).then_inc(s_keep[b].sem, 16)

                        def kept(u):
                            b = u.c % 2
                            s_keep[b].wait(sp, (u.val - b) * 8 + 16)
                            slot_kept[b].give(sp)
                        for b in (0, 1):
                            slot_kept[b].give(sp)
                        pipeline(sp, NG, 2, [(0, keep), (1, kept)])
                        for b in (0, 1):
                            slot_kept[b].take(sp)

                    @block.gpsimd
                    def _(g):
                        top_row = g.to_reg(NP - 1)

                        def fetch(u):
                            b = u.c % 2
                            idx_full[b].take(g)
                            for j in range(GS):
                                g.indirect_dma_start(out=G[:, b, j, :], out_offset=None, in_=T4,
                                                     in_offset=bass.IndirectOffsetOnAxis(ap=idx[:, b, j:j + 1], axis=0),
                                                     bounds_check=top_row, oob_is_err=True).then_inc(s_rows[b].sem, 16)
                        pipeline(g, NG, 2, [(0, fetch)])

                    @block.scalar
                    def _(a):
                        def index(u):
                            b = u.c % 2
                            slot_free[b].take(a)
                            slot_kept[b].take(a)
                            a.activation(idx[:, b, :], gidx[:, bass.ds(u.val * GS, GS)], ACT.Copy)\
                                .then_inc(idx_full[b].sem, 1)

                        def copyT(u):
                            b = u.c % 2
                            tr_full[b].take(a)
                            for k in (0, 1):
                                x = a.activation(hotT[:, b * GS + 4 * k:b * GS + 4 * k + 4, :].rearrange("p j n -> p (j n)"),
                                                 psT[b][k][:, :], ACT.Copy)
                            x.then_inc(lhs_full[b].sem, 1)
                        pipeline(a, NG, 2, [(0, index), (0, copyT)])

                    @block.tensor
                    def _(te):
                        regs = [te.alloc_register(f"nt_att3{j}") for j in range(GS)]

                        def trans(u):
                            b = u.c % 2
                            hot_full[b].take(te)
                            for j in range(GS):
                                x = te.transpose(psT[b][j // 4][:, j % 4 * P:(j % 4 + 1) * P], hot[:, b * GS + j, :], ident[:, :])
                            x.then_inc(tr_full[b].sem, 1)

                        def scores(u):
                            b = u.c % 2
                            nt = ntile(te, u, regs)
                            lhs_full[b].take(te)
                            res_free[b].take(te)
                            for j in range(GS):
                                x = te.matmul(psS[b][:, j * HEADS3:(j + 1) * HEADS3], hotT[:, b * GS + j, :],
                                              at_tile(SV, nt[j]), start=True, stop=True)
                            x.then_inc(res_full[b].sem, 1)
                        pipeline(te, NG, 2, [(0, trans), (1, scores)])

                    @block.vector
                    def _(v):
                        for b in (0, 1):
                            slot_free[b].give(v)
                            res_free[b].give(v)

                        def hots(u):
                            b = u.c % 2
                            for j in range(GS):
                                x = one_hot(v, hot[:, b * GS:(b + 1) * GS], j, u.val * GS + j, False)
                            x.then_inc(hot_full[b].sem, 1)

                        def logits(u):
                            b = u.c % 2
                            s_rows[b].wait(v, (u.val - b) * (16 * GS // 2) + 16 * GS)
                            res_full[b].take(v)
                            op(v.tensor_tensor(raw[:, :, :], G[:, b, :, D:WT],
                                               psS[b][:, 0:GS * HEADS3].rearrange("p (s h) -> p s h", h=HEADS3), ALU.add), v, "v")
                            slot_free[b].give(v)
                            res_free[b].give(v)
                            op(v.scalar_tensor_tensor(out=LG[:, bass.ds(u.val * GS, GS), :], in0=raw[:, :, :], scalar=0.2,
                                                      in1=raw[:, :, :], op0=ALU.mult, op1=ALU.max), v, "v")
                        pipeline(v, NG, 2, [(2, logits), (0, hots)])
                        for b in (0, 1):
                            slot_free[b].take(v)
                            res_free[b].take(v)
            for b in (0, 1):
                s_keep[b].base += 16 * NG // 2

        ln_stats(B256)
        XR, H0 = A256, C256

        def w0(sp, W, rows, mb):
            load(sp, W[:, 0:2, 0:D], kchunks(t["L0_gnn_W_l"]))
            load(sp, W[:, 0:2, D:2 * D], kchunks(t["L0_gnn_W_r"]))

        def post0(v, u, ps, rows):
            v.tensor_copy(at_tile(B256, u.val), ps[:, 0:D])
            op(v.tensor_copy(at_tile(XR, u.val), ps[:, D:2 * D]), v, "v")

        dense_loop(1, 2 * D, w0, ln_pre(B256, H0), post0)
        with phase() as block:
            @block.sync
            def _(sp):
                store_rows(sp, T0, B256, D)


        def bc(ap, shape):
            return ap.to_broadcast(shape)

        with ExitStack() as L0:
            LG = sb("logits0", [P, SP_, HEADS0], F32, L0)
            SL = sb("self_logits", [P, NT, HEADS0], F32, L0)
            attc = sb("att_cols", [P, 2, HEADS0], F32, L0)
            with ExitStack() as ctx:
                f = sb("self_feat", [P, GT, D], F32, ctx)
                attr = sb("att_row", [P, D], F32, ctx)
                with phase() as block:
                    @block.sync
                    def _(sp):
                        load(sp, attr[:, :], bcast_row(t["L0_gnn_att"].rearrange("h c -> (h c)")))
                        ping.take(sp)
                        for h in range(HEADS0):
                            load(sp, attc[h % 2 * 64:h % 2 * 64 + 64, h // 2, h:h + 1],
                                 t["L0_gnn_att"][h:h + 1, :].rearrange("a c -> c a"), allow_slow_non_contiguous=True)
                        sp.wait_ge(s_in.sem, s_in.base)
                        aux_full[0].give(sp)

                    @block.vector
                    def _(v):
                        op(v.memset(attc[:, :, :], 0.0), v, "v")
                        ping.give(v)
                        op(v.memset(LG[:, :, :], 0.0), v, "v")
                        aux_full[0].take(v)

                        def self_logit(u):
                            op(v.tensor_tensor(f[:, :, :], grp(B256, u), grp(A256, u), ALU.add), v, "v")
                            op(v.scalar_tensor_tensor(out=f[:, :, :], in0=f[:, :, :], scalar=0.2, in1=f[:, :, :],
                                                      op0=ALU.mult, op1=ALU.max), v, "v")
                            op(v.tensor_tensor(f[:, :, :], f[:, :, :], attr[:, :].unsqueeze(1).to_broadcast([P, GT, D]),
                                               ALU.mult), v, "v")
                            op(v.tensor_reduce(grp(SL, u).rearrange("p t h -> p (t h)"),
                                               f[:, :, :].rearrange("p t (h c) -> p (t h) c", h=HEADS0), AX.X, ALU.add), v, "v")
                        pipeline(v, GT, GT, [(0, self_logit)])
            attention_fetch0(LG, attc, B)
            PK = sb("peaks", [P, SP_, HEADS0], F32, L0)
            LS = sb("last_marks", [P, SP_], F32, L0)
            segment_softmax(LG, LG[:, :, :], HEADS0, (A, B), last=LS[:, :], peak=PK)
            WB = D + 2 * HEADS0 + 1
            ACCB = tiles(B, WB)
            attention_sum("a0", LG, HEADS0, True, [(PK, HEADS0), (LS[:, :].unsqueeze(2), 1)],
                          ACCB, B[:, 0:NT * WB], A)
            with ExitStack() as ctx:
                xl = part(A, 0, [GT, D])
                biasr = sb("bias_row", [P, D], F32, ctx)
                sm = [sb(f"small{k}", [P, GT, HEADS0], F32, ctx) for k in range(4)]
                with phase() as block:
                    @block.sync
                    def _(sp):
                        load(sp, biasr[:, :], bcast_row(t["L0_gnn_bias"]))
                        sp.wait_ge(s_in.sem, s_in.base)
                        aux_full[0].give(sp)

                        def group(u):
                            src_free[0].take(sp)
                            sp.dma_start(xl[:, :, :], T0[bass.ds(u.val * (GT * P), GT * P), :].rearrange("(t p) c -> p t c", p=P))\
                                .then_inc(s_load[0].sem, 16)
                        pipeline(sp, GT, GT, [(0, group)])

                    @block.scalar
                    def _(a):
                        def exps(u):
                            src_full[0].take(a)
                            op(a.activation(sm[0][:, :, :], sm[0][:, :, :], ACT.Exp), a, "a")
                            a.activation(sm[1][:, :, :], sm[1][:, :, :], ACT.Exp).then_inc(src_full[1].sem, 1)
                        pipeline(a, GT, GT, [(0, exps)])

                    @block.vector
                    def _(v):
                        aux_full[0].take(v)
                        src_free[0].give(v)

                        def join(u):
                            acc = ACCB[:, bass.ds(u.val * GT, GT), :]
                            wsum, peak, hit = acc[:, :, D:D + 4], acc[:, :, D + 4:D + 8], acc[:, :, D + 8:D + 9]
                            e, s_, x2, x3 = (k[:, :, :] for k in sm)
                            sl = SL[:, bass.ds(u.val * GT, GT), :]
                            bw = [P, GT, HEADS0]
                            op(v.tensor_scalar(x2[:, :, 0:1], hit, -1.0, BIG, ALU.add, ALU.mult), v, "v")
                            op(v.tensor_tensor(e, peak, x2[:, :, 0:1].to_broadcast(bw), ALU.add), v, "v")
                            op(v.tensor_tensor(x3, e, sl, ALU.max), v, "v")
                            op(v.tensor_tensor(e, e, x3, ALU.subtract), v, "v")
                            op(v.tensor_tensor(s_, sl, x3, ALU.subtract), v, "v")
                            src_full[0].give(v)
                            src_full[1].take(v)
                            op(v.tensor_tensor(x2, wsum, e, ALU.mult), v, "v")
                            op(v.tensor_tensor(x2, x2, s_, ALU.add), v, "v")
                            op(v.tensor_scalar(x2, x2, 1e-16, None, ALU.add), v, "v")
                            op(v.reciprocal(x2, x2), v, "v")
                            op(v.tensor_tensor(e, e, x2, ALU.mult), v, "v")
                            op(v.tensor_tensor(s_, s_, x2, ALU.mult), v, "v")
                            heads_of = lambda z: z.rearrange("p t (h c) -> p t h c", h=HEADS0)
                            wide = [P, GT, HEADS0, D // HEADS0]
                            rows_ = acc[:, :, 0:D]
                            op(v.tensor_tensor(heads_of(rows_), heads_of(rows_), e.unsqueeze(3).to_broadcast(wide), ALU.mult), v, "v")
                            s_load[0].wait(v, u.val * 16 + 16)
                            op(v.tensor_tensor(heads_of(xl[:, :, :]), heads_of(xl[:, :, :]), s_.unsqueeze(3).to_broadcast(wide),
                                               ALU.mult), v, "v")
                            op(v.tensor_tensor(rows_, rows_, xl[:, :, :], ALU.add), v, "v")
                            src_free[0].give(v)
                            h = grp(C256, u)
                            op(v.tensor_tensor(h, h, rows_, ALU.add), v, "v")
                            op(v.tensor_tensor(h, h, biasr[:, :].unsqueeze(1).to_broadcast([P, GT, D]), ALU.add), v, "v")
                        pipeline(v, GT, GT, [(0, join)])
                        src_free[0].take(v)
                s_load[0].base += 16 * GT

        column_norm(C256, t["L0_gnn_gamma1"], t["L0_gnn_beta1"], None)

        def w_ffn(sp, W, rows, mb):
            load(sp, W[:, 2:4, :], kchunks(t["L0_gnn_W1"]))
            load(sp, W[:, 0:2, :], kchunks(t["L0_gnn_W2"]))
            load(sp, rows[:, 0, :], bcast_row(t["L0_gnn_b2"]))
            load(sp, mb[:, :], t["L0_gnn_b1"].rearrange("(k p) -> p k", p=P), allow_slow_non_contiguous=True)

        def copy_pre(a, u, hs):
            return a.activation(hs[:, 0, :], at_tile(C256, u.val), ACT.Copy)

        def post_ffn(v, u, ps, rows):
            y = at_tile(C256, u.val)
            op(v.tensor_tensor(y, y, ps[:, 0:D], ALU.add), v, "v")
            op(v.tensor_tensor(y, y, rows[:, 0, :], ALU.add), v, "v")

        dense_loop(1, D, w_ffn, copy_pre, post_ffn, mid_bias=True, nrows=1)
        with phase() as block:
            @block.vector
            def _(v):
                op(v.memset(B256[:, NT - 1, :], 0.0), v, "v")
                ping.give(v)

            @block.sync
            def _(sp):
                ping.take(sp)
                load(sp, B256[:, 0:NT - 1, :], t["x"][0:(NT - 1) * P, :].rearrange("(t p) c -> p t c", p=P))
                load(sp, B256[0:TAIL, NT - 1, :], t["x"][(NT - 1) * P:N, :])
                loaded(sp)

        def add_residual(v, u, y):
            x = grp(B256, u)
            op(v.tensor_tensor(x, x, y, ALU.add), v, "v")

        column_norm(C256, t["L0_gnn_gamma2"], t["L0_gnn_beta2"], add_residual)

        ln_stats(B256)

        def w_one(name):
            def w(sp, W, rows, mb):
                load(sp, W[:, 0:2, :], kchunks(t[name]))
            return w

        def post_support(v, u, ps, rows):
            op(v.tensor_copy(at_tile(A256, u.val), ps[:, 0:D]), v, "v")

        dense_loop(1, D, w_one("L1_gnn_weight"), ln_pre(B256), post_support)
        with phase() as block:
            @block.sync
            def _(sp):
                store_rows(sp, T1, A256, D)
        plain_pass("l1", T1, C256, C[:, 0:NT * D], D, True)

        scatter_pass(A256)

        with ExitStack() as ctx:
            parts = sb("scatter_parts", [P, 2, GT, D], F32, ctx)
            biasr = sb("bias_row", [P, D], F32, ctx)
            with phase() as block:
                @block.sync
                def _(sp):
                    load(sp, biasr[:, :], bcast_row(t["L1_gnn_bias"]))
                    loaded(sp)
                    aux_full[0].give(sp)

                    def group(u):
                        b = u.c % 2
                        src_free[b].take(sp)
                        k = u.c % CHAINS
                        g7 = (u.val - k) * (GT * P // CHAINS) if k or not isinstance(u.val, int) else u.val * (GT * P // CHAINS)
                        sp.dma_start(parts[:, b], scat[k][bass.ds(g7, GT * P), :].rearrange("(t p) c -> p t c", p=P))\
                            .then_inc(s_load[b].sem, 16)
                    pipeline(sp, GT * CHAINS, CHAINS, [(0, group)])

                @block.vector
                def _(v):
                    aux_full[0].take(v)
                    for b in (0, 1):
                        src_free[b].give(v)

                    def add(u):
                        b, k = u.c % 2, u.c % CHAINS
                        x = B256[:, bass.ds((u.val - k) * GT // CHAINS if isinstance(u.val, int)
                                            else (u.val - k) // CHAINS * GT, GT), :]
                        if k == 0:
                            y = C256[:, bass.ds(u.val * GT // CHAINS if isinstance(u.val, int)
                                                else u.val // CHAINS * GT, GT), :]
                            op(v.tensor_tensor(x, x, y, ALU.add), v, "v")
                            op(v.tensor_tensor(x, x, biasr[:, :].unsqueeze(1).to_broadcast([P, GT, D]), ALU.add), v, "v")
                        s_load[b].wait(v, (u.val - b) * 8 + 16)
                        op(v.tensor_tensor(x, x, parts[:, b], ALU.add), v, "v")
                        src_free[b].give(v)
                    pipeline(v, GT * CHAINS, CHAINS, [(0, add)])
                    for b in (0, 1):
                        src_free[b].take(v)
            for b in (0, 1):
                s_load[b].base += 16 * GT * CHAINS // 2

        ln_stats(B256)
        with phase() as block:
            @block.scalar
            def _(a):
                def norm(u):
                    a.activation(at_tile(A256, u.val), at_tile(B256, u.val), ACT.Relu,
                                 bias=nmr[:, bass.ds(u.val, 1)], scale=rstd[:, bass.ds(u.val, 1)])
                pipeline(a, NT, GT, [(0, norm)])
                a.drain()
                ping.give(a)

            @block.sync
            def _(sp):
                ping.take(sp)
                store_rows(sp, T2, A256, D)
        WC = D + 1
        ACC1 = tiles(C, WC)
        plain_pass("l2a", T2, ACC1, C[:, 0:NT * WC], WC, False)

        def conv_weights(k):
            def w(sp, W, rows, mb):
                load(sp, W[:, 0:2, :], kchunks(t[f"L2_gnn_W{k}_msg"]))
                load(sp, W[:, 2:4, :], kchunks(t[f"L2_gnn_W{k}_self"]))
                load(sp, rows[:, 0, :], bcast_row(t[f"L2_gnn_b{k}_msg"]))
                load(sp, rows[:, 1, :], bcast_row(t[f"L2_gnn_b{k}_self"]))
            return w

        def conv_pre(acc):
            def pre(a, u, hs):
                a.activation(hs[:, 0, :], acc[:, bass.ds(u.val, 1), 0:D].rearrange("p a c -> p (a c)"), ACT.Copy)
                return a.activation(hs[:, 1, :], at_tile(A256, u.val), ACT.Copy)
            return pre

        def post_conv1(v, u, ps, rows):
            y = at_tile(A256, u.val)
            dg = deg[:, bass.ds(u.val, 1)]
            op(v.tensor_copy(dg, ACC1[:, bass.ds(u.val, 1), D:D + 1].rearrange("p a c -> p (a c)")), v, "v")
            op(v.scalar_tensor_tensor(out=y, in0=rows[:, 0, :], scalar=dg, in1=ps[:, 0:D], op0=ALU.mult, op1=ALU.add), v, "v")
            op(v.tensor_tensor(y, y, rows[:, 1, :], ALU.add), v, "v")
            op(v.scalar_tensor_tensor(out=y, in0=y, scalar=0.1, in1=y, op0=ALU.mult, op1=ALU.max), v, "v")

        dense_loop(2, D, conv_weights(1), conv_pre(ACC1), post_conv1, nrows=2)
        with phase() as block:
            @block.sync
            def _(sp):
                store_rows(sp, T3, A256, D)
        plain_pass("l2b", T3, C256, C[:, 0:NT * D], D, False)

        def post_conv2(v, u, ps, rows):
            y, x = at_tile(C256, u.val), at_tile(B256, u.val)
            op(v.scalar_tensor_tensor(out=y, in0=rows[:, 0, :], scalar=deg[:, bass.ds(u.val, 1)], in1=ps[:, 0:D],
                                      op0=ALU.mult, op1=ALU.add), v, "v")
            op(v.tensor_tensor(y, y, rows[:, 1, :], ALU.add), v, "v")
            op(v.tensor_tensor(x, x, y, ALU.add), v, "v")

        dense_loop(2, D, conv_weights(2), conv_pre(C256), post_conv2, nrows=2)

        ln_stats(B256)
        WT = D + HEADS3
        H4 = tiles(A, WT)
        with ExitStack() as L3:
            LG3 = sb("logits3", [P, SP_, HEADS3], F32, L3)
            with ExitStack() as SVX:
                SV = sb("dst_scores", [P, NT, HEADS3], F32, SVX)

                def w_uv(sp, W, rows, mb):
                    load(sp, W[:, 0:2, 0:2 * HEADS3], kchunks(t["W_uv"]))
                    load(sp, rows[:, 0, 0:HEADS3], bcast_row(t["L3_gnn_b_u"]))

                def pre_uv(a, u, hs):
                    scale, bias = rstd[:, bass.ds(u.val, 1)], nmr[:, bass.ds(u.val, 1)]
                    a.activation(H4[:, bass.ds(u.val, 1), 0:D].rearrange("p a c -> p (a c)"), at_tile(B256, u.val),
                                 ACT.Relu, bias=bias, scale=scale)
                    return a.activation(hs[:, 0, :], at_tile(B256, u.val), ACT.Relu, bias=bias, scale=scale)

                def post_uv(v, u, ps, rows):
                    v.tensor_tensor(H4[:, bass.ds(u.val, 1), D:WT].rearrange("p a c -> p (a c)"), ps[:, 0:HEADS3],
                                    rows[:, 0, 0:HEADS3], ALU.add)
                    op(v.tensor_copy(at_tile(SV, u.val), ps[:, HEADS3:2 * HEADS3]), v, "v")

                dense_loop(1, 2 * HEADS3, w_uv, pre_uv, post_uv, nrows=1)
                with phase() as block:
                    @block.sync
                    def _(sp):
                        store_rows(sp, T4, H4, WT)

                    @block.vector
                    def _(v):
                        op(v.memset(LG3[:, :, :], 0.0), v, "v")
                attention_fetch3(LG3, SV, C, A, WT)
            segment_softmax(LG3, LG3[:, :, :], HEADS3, (A, C))
            ACC3 = tiles(C, WT)
            attention_sum("a3", LG3, HEADS3, False, [], ACC3, C[:, 0:NT * WT], A)
            with ExitStack() as ctx:
                rd = sb("denominators", [P, GT, HEADS3], F32, ctx)
                with phase() as block:
                    @block.vector
                    def _(v):
                        def final(u):
                            acc = ACC3[:, bass.ds(u.val * GT, GT), :]
                            op(v.tensor_scalar(rd[:, :, :], acc[:, :, D:WT], 0.5, None, ALU.max), v, "v")
                            op(v.reciprocal(rd[:, :, :], rd[:, :, :]), v, "v")
                            rows_ = acc[:, :, 0:D].rearrange("p t (c h) -> p t c h", h=HEADS3)
                            op(v.tensor_tensor(rows_, rows_, rd[:, :, :].unsqueeze(2).to_broadcast([P, GT, D // HEADS3, HEADS3]),
                                               ALU.mult), v, "v")
                            x = grp(B256, u)
                            op(v.tensor_tensor(x, x, acc[:, :, 0:D], ALU.add), v, "v")
                            res_full[0].give(v)
                        pipeline(v, GT, GT, [(0, final)])

                    @block.sync
                    def _(sp):
                        for g in range(GT - 1):
                            res_full[0].take(sp)
                            sp.dma_start(out[g * GT * P:(g + 1) * GT * P, :].rearrange("(t p) c -> p t c", p=P),
                                         B256[:, g * GT:(g + 1) * GT, :]).then_inc(s_st.sem, 16)
                        res_full[0].take(sp)
                        g = GT - 1
                        sp.dma_start(out[g * GT * P:(NT - 1) * P, :].rearrange("(t p) c -> p t c", p=P),
                                     B256[:, g * GT:NT - 1, :]).then_inc(s_st.sem, 16)
                        sp.dma_start(out[(NT - 1) * P:N, :], B256[0:TAIL, NT - 1, :]).then_inc(s_st.sem, 16)
                        s_st.base += 16 * (GT + 1)
                        sp.wait_ge(s_st.sem, s_st.base)


_INS = ['x', 'L0_gnn_W_l', 'L0_gnn_W_r', 'L0_gnn_att', 'L0_gnn_bias', 'L0_gnn_W1', 'L0_gnn_b1', 'L0_gnn_W2',
        'L0_gnn_b2', 'L0_gnn_gamma1', 'L0_gnn_beta1', 'L0_gnn_gamma2', 'L0_gnn_beta2', 'L1_gnn_weight',
        'L1_gnn_bias', 'L1_gnn_alpha', 'L2_gnn_W1_msg', 'L2_gnn_b1_msg', 'L2_gnn_W1_self', 'L2_gnn_b1_self',
        'L2_gnn_W2_msg', 'L2_gnn_b2_msg', 'L2_gnn_W2_self', 'L2_gnn_b2_self', 'L3_gnn_b_u']


def kernel(**inputs):
    import concourse.bacc as bacc
    from concourse.bass_utils import run_bass_kernel_spmd as run

    nc = bacc.Bacc("TRN2", target_bir_lowering=False, num_devices=1)
    arrays, t = {}, {}

    def give(name, a):
        a = np.ascontiguousarray(a)
        arrays[f"in_{name}"] = a
        t[name] = nc.dram_tensor(f"in_{name}", a.shape, mybir.dt.from_np(a.dtype), kind="ExternalInput").ap()

    for name in _INS:
        give(name, inputs[name])
    pad = EP - E
    dst = np.pad(np.asarray(inputs["dst"]), (0, pad), constant_values=N).reshape(ET, P)
    src = np.pad(np.asarray(inputs["src"]), (0, pad)).reshape(ET, P)
    typ = np.pad(np.asarray(inputs["edge_type_11"]), (0, pad), constant_values=RELS).reshape(ET, P)
    give("edge_tiles", np.concatenate([dst, src, typ], axis=1))
    give("dst_last", dst[:, P - 1])
    give("W_uv", np.concatenate([np.asarray(inputs["L3_gnn_W_u"]).T, np.asarray(inputs["L3_gnn_W_v"]).T], axis=1))
    out = nc.dram_tensor("out0", (N, D), F32, kind="ExternalOutput").ap()
    build(nc, t, out)
    r = run(nc, [arrays], core_ids=[0])
    return r.results[0]["out0"]
```

```python
from contextlib import ExitStack, contextmanager

import numpy as np

import concourse.bass as bass
from concourse import mybir

F32 = mybir.dt.float32
I32 = mybir.dt.int32
ALU = mybir.AluOpType
ACT = mybir.ActivationFunctionType
AX = mybir.AxisListType

P = 128
N, D, E = 6250, 256, 100000
NT = -(-N // P)
NP = NT * P
TAIL = N - (NT - 1) * P
ET = 784
EP = ET * P
S = ET + NT - 1
GS = 8
NG = S // GS
SB = -(-S // P)
SP_ = SB * P
HEADS0, HEADS3 = 4, 8
W0 = D + HEADS0
RELS = 11
LN_EPS = BN_EPS = 1e-5
BIG = 1e30
GT = 7
ND = NP + P
RING = 4
CHAINS = 8
assert S % (RING * GS) == 0 and NT == GT * GT and TAIL > 0


class Token:

    def __init__(self, sem):
        self.sem = sem

    def take(self, eng, n=1):
        eng.wait_ge(self.sem, n)
        eng.sem_inc(self.sem, -n)

    def give(self, eng, n=1):
        eng.sem_inc(self.sem, n)


class Count:

    def __init__(self, sem):
        self.sem, self.base = sem, 0

    def wait(self, eng, value):
        eng.wait_ge(self.sem, value + self.base)


class U:

    def __init__(self, val, c):
        self.val, self.c = val, c


def pipeline(eng, total, body, stages, steady=None):
    maxlag = max(lag for lag, _ in stages)
    first = -(-maxlag // body) * body
    turns = max(0, ((steady or total) - first) // body)

    def emit(v, c, inside):
        for lag, fn in stages:
            if inside or 0 <= c - lag < total:
                fn(U(v - lag, c - lag))

    if turns < 2:
        first, turns = total + maxlag, 0
    for v in range(first):
        emit(v, v, False)
    if turns:
        with eng.Fori(0, turns) as i:
            for k in range(body):
                emit(i * body + (first + k), first + k, True)
        for v in range(first + turns * body, total + maxlag):
            emit(v, v, False)


def build(nc, t, out):
    with ExitStack() as top:
        made = {}

        def own(name):
            made[name] = made.get(name, 0) + 1
            return name if made[name] == 1 else f"{name}_{made[name]}"

        def sb(name, shape, dt=F32, ctx=top):
            return ctx.enter_context(nc.sbuf_tensor(own(name), shape, dt))

        def bank(name, ctx):
            return ctx.enter_context(nc.psum_tensor(own(name), [P, 512], F32))

        def sem(name):
            return top.enter_context(nc.semaphore(name))

        def token(name):
            return Token(sem(name))

        A = sb("regionA", [P, NT * 264])
        B = sb("regionB", [P, NT * 265])
        C = sb("regionC", [P, NT * 264])

        def tiles(region, width, cols=None):
            return region[:, 0:NT * width].rearrange("p (t c) -> p t c", c=width)

        def part(region, at, shape):
            n = int(np.prod(shape))
            v = region[:, at:at + n]
            if len(shape) == 2:
                v = v.rearrange("p (a b) -> p a b", b=shape[1])
            elif len(shape) == 3:
                v = v.rearrange("p (a b c) -> p a b c", b=shape[1], c=shape[2])
            return v

        A256, B256, C256 = tiles(A, D), tiles(B, D), tiles(C, D)

        ident = sb("ident", [P, P])
        iota = sb("iota", [P, P])
        gidx = sb("gidx", [P, S], I32)
        rel = sb("rel", [P, S])
        wgt = sb("wgt", [P, S])
        ntab = sb("ntab", [1, SP_], I32)
        dstrow = sb("dstrow", [P, SB, P])
        eps = sb("eps", [P, 1])
        rstd = sb("rstd", [P, NT])
        nmr = sb("nmr", [P, NT])
        deg = sb("deg", [P, NT])
        zero_rows = sb("zero_rows", [P, 1, D])
        node_scores = sb("node_scores", [P, NT, 8])

        def dram(name, shape, dt=F32):
            return nc.dram_tensor(name, shape, dt).ap()

        T0 = dram("table0", [NP, W0])
        T1, T2, T3 = (dram(f"table{i}", [NP, D]) for i in (1, 2, 3))
        T4 = dram("table4", [NP, 264])
        srcrow_d = dram("srcrow_d", [S, P])
        Eb = dram("edge_rows", [NG, P, GS * D])
        scat = dram("scatter_sums", [CHAINS * ND, D])

        s_in = Count(sem("s_in"))
        s_meta = sem("s_meta")
        s_tiles = sem("s_tiles")
        s_st = Count(sem("s_st"))
        s_back = Count(sem("s_back"))
        s_zero = Count(sem("s_zero"))
        link = {k: token(f"s_link_{k}") for k in ("v", "a", "p", "t")}
        src_full = [token(f"s_src_full{b}") for b in (0, 1)]
        src_free = [token(f"s_src_free{b}") for b in (0, 1)]
        tr_full = [token(f"s_tr_full{b}") for b in (0, 1)]
        lhs_full = [token(f"s_lhs_full{b}") for b in (0, 1)]
        mid_full = [token(f"s_mid_full{b}") for b in (0, 1)]
        act_full = [token(f"s_act_full{b}") for b in (0, 1)]
        res_full = [token(f"s_res_full{b}") for b in (0, 1)]
        res_free = [token(f"s_res_free{b}") for b in (0, 1)]
        hot_full = [token(f"s_hot_full{b}") for b in (0, 1)]
        hot_free = [token(f"s_hot_free{b}") for b in (0, 1)]
        idx_full = [token(f"s_idx_full{b}") for b in range(RING)]
        slot_free = [token(f"s_slot_free{b}") for b in range(RING)]
        slot_kept = [token(f"s_slot_kept{b}") for b in range(RING)]
        aux_full = [token(f"s_aux_full{b}") for b in (0, 1)]
        aux_free = [token(f"s_aux_free{b}") for b in (0, 1)]
        ping, pong, stats_done = token("s_ping"), token("s_pong"), token("s_stats")
        step_full = token("s_step_full")
        s_add = Count(sem("s_add"))
        s_load = [Count(sem(f"s_load{b}")) for b in (0, 1)]
        s_keep = [Count(sem(f"s_keep{b}")) for b in range(RING)]

        def op(ins, eng, k):
            ins.then_inc(link[k].sem, 1)
            link[k].take(eng)

        def ntile(eng, u, regs):
            eng.load(regs, ntab[0:1, bass.ds(u.val * GS, GS)])
            return [eng.snap(r, min_val=0, max_val=NT - 1) for r in regs]

        def at_tile(view, v):
            return view[:, bass.ds(v, 1), :].rearrange("p a c -> p (a c)")

        def load(sp, dst, src, **kw):
            sp.dma_start(dst, src, **kw).then_inc(s_in.sem, 16)
            s_in.base += 16

        def loaded(eng):
            eng.wait_ge(s_in.sem, s_in.base)

        def phase():
            return nc.Block()

        with ExitStack() as ctx:
            pss = [bank(f"ps_m{i}", ctx) for i in range(2)]
            keys_i = part(A, 0, [ET]).bitcast(I32)
            keys = part(A, 1000, [ET])
            lane = part(A, 2000, [ET])
            below = part(A, 3000, [ET])
            ers = sb("edge_rows_i", [P, SB, 3 * P], I32, ctx)
            srow = part(A, 4000, [SB, P])
            typ = part(A, 5000, [SB, P])
            wrow = part(A, 6000, [SB, P])
            rrow = part(A, 7000, [SB, P])
            tmp = part(A, 8000, [SB, P])
            alpha = part(A, 9000, [RELS])
            stepno = part(A, 9100, [SB])
            et = part(A, 9200, [SB])
            et_i = part(A, 9300, [SB]).bitcast(I32)
            ntf = part(A, 9400, [SB])
            shift = part(A, 9500, [SB])
            base_in = s_in.base
            with phase() as block:
                @block.sync
                def _(sp):
                    sp.dma_start(keys_i, t["dst_last"].rearrange("(a n) -> a n", a=1).partition_broadcast(P)
                                 .rearrange("q a n -> q (a n)")).then_inc(s_meta, 16)
                    sp.dma_start(alpha, t["L1_gnn_alpha"].rearrange("r a -> a r").partition_broadcast(P)
                                 .rearrange("q a n -> q (a n)"), allow_slow_non_contiguous=True).then_inc(s_meta, 16)
                    ping.take(sp)
                    sp.dma_start(B256[:, 0:NT - 1, :], t["x"][0:(NT - 1) * P, :].rearrange("(t p) c -> p t c", p=P))\
                        .then_inc(s_in.sem, 16)
                    sp.dma_start(B256[0:TAIL, NT - 1, :], t["x"][(NT - 1) * P:N, :]).then_inc(s_in.sem, 16)
                    pong.take(sp)
                    for c in range(SB):
                        n = min(P, S - c * P)
                        sp.dma_start(srcrow_d[c * P:c * P + n, :], srow[0:n, c, :]).then_inc(s_st.sem, 16)
                    s_st.base += 16 * SB
                    sp.wait_ge(s_st.sem, s_st.base)
                    sp.wait_ge(s_in.sem, base_in + 32)

                @block.gpsimd
                def _(g):
                    op(g.memset(ident[:, :], 0.0), g, "p")
                    g.iota(stepno, [[P, SB]], base=0, channel_multiplier=1,
                           allow_small_or_imprecise_dtypes=True)
                    g.iota(lane, [[1, ET]], base=0, channel_multiplier=0, allow_small_or_imprecise_dtypes=True)
                    g.iota(iota[:, :], [[1, P]], base=0, channel_multiplier=0, allow_small_or_imprecise_dtypes=True)
                    op(g.affine_select(out=ident[:, :], in_=ident[:, :], compare_op=ALU.not_equal, fill=1.0,
                                       base=0, pattern=[[-1, P]], channel_multiplier=1), g, "p")
                    hot_full[0].give(g)
                    idx_full[0].take(g)
                    top_edge = g.to_reg(ET - 1)
                    for c in range(SB):
                        g.indirect_dma_start(out=ers[:, c, :], out_offset=None, in_=t["edge_tiles"],
                                             in_offset=bass.IndirectOffsetOnAxis(ap=et_i[:, c:c + 1], axis=0),
                                             bounds_check=top_edge, oob_is_err=True).then_inc(s_tiles, 16)
                    g.wait_ge(s_tiles, 16 * SB)
                    hot_full[1].give(g)

                @block.vector
                def _(v):
                    op(v.memset(B256[:, NT - 1, :], 0.0), v, "v")
                    ping.give(v)
                    v.memset(eps[:, :], LN_EPS)
                    v.wait_ge(s_meta, 32)
                    hot_full[0].take(v)
                    op(v.tensor_scalar(keys_i, keys_i, 7, None, ALU.logical_shift_right), v, "v")
                    op(v.tensor_copy(keys, keys_i), v, "v")
                    op(v.tensor_tensor(keys, keys, lane, ALU.add), v, "v")
                    for c in range(SB):
                        op(v.tensor_scalar(below, keys, stepno[:, c:c + 1], 0.0, ALU.is_lt, ALU.add,
                                           accum_out=et[:, c:c + 1]), v, "v")
                    op(v.tensor_tensor(ntf, stepno, et, ALU.subtract), v, "v")
                    op(v.tensor_scalar(ntf, ntf, float(NT - 1), None, ALU.min), v, "v")
                    op(v.tensor_scalar(et, et, float(ET - 1), None, ALU.min), v, "v")
                    op(v.tensor_copy(et_i, et), v, "v")
                    op(v.tensor_scalar(shift, ntf, float(P), None, ALU.mult), v, "v")
                    idx_full[0].give(v)
                    hot_full[1].take(v)
                    v.tensor_copy(dstrow[:, :, :], ers[:, :, 0:P])
                    v.tensor_copy(srow, ers[:, :, P:2 * P])
                    op(v.tensor_copy(typ, ers[:, :, 2 * P:3 * P]), v, "v")
                    pong.give(v)
                    op(v.memset(wrow, 0.0), v, "v")
                    for c in range(SB):
                        op(v.tensor_scalar(rrow[:, c, :], dstrow[:, c, :], shift[:, c:c + 1], None, ALU.subtract), v, "v")
                    for r in range(RELS):
                        op(v.tensor_scalar(tmp, typ, float(r), alpha[:, r:r + 1], ALU.is_equal, ALU.mult), v, "v")
                        op(v.tensor_tensor(wrow, wrow, tmp, ALU.add), v, "v")
                    src_full[0].give(v)
                    for c in range(SB):
                        n = min(P, S - c * P)
                        tr_full[0].take(v)
                        v.tensor_copy(rel[:, c * P:c * P + n], pss[0][:, 0:n])
                        v.tensor_copy(gidx[:, c * P:c * P + n], pss[0][:, P:P + n])
                        v.tensor_copy(wgt[:, c * P:c * P + n], pss[0][:, 2 * P:2 * P + n])
                        op(v.tensor_copy(ntab[0:1, c * P:(c + 1) * P], pss[0][0:1, 3 * P:4 * P]), v, "v")
                        res_free[0].give(v)

                @block.tensor
                def _(te):
                    src_full[0].take(te)
                    for c in range(SB):
                        if c:
                            res_free[0].take(te)
                        te.transpose(pss[0][:, 0:P], rrow[:, c, :], ident[:, :])
                        te.transpose(pss[0][:, P:2 * P], srow[:, c, :], ident[:, :])
                        te.transpose(pss[0][:, 2 * P:3 * P], wrow[:, c, :], ident[:, :])
                        te.transpose(pss[0][0:1, 3 * P:4 * P], ntf[:, c:c + 1], ident[:, :])\
                            .then_inc(tr_full[0].sem, 1)
                    res_free[0].take(te)
            s_in.base = base_in + 32

        def ln_stats(view):
            with ExitStack() as ctx:
                st = sb("ln_parts", [P, NT, 6], F32, ctx)
                with phase() as block:
                    @block.vector
                    def _(v):
                        def stats(u):
                            v.bn_stats(st[:, bass.ds(u.val, 1), :].rearrange("p a c -> p (a c)"), at_tile(view, u.val))
                        pipeline(v, NT, GT, [(0, stats)])
                        v.drain()
                        me, qe, mo, qo = (st[:, :, k] for k in (1, 2, 4, 5))
                        op(v.tensor_tensor(qe, qe, qo, ALU.add), v, "v")
                        op(v.tensor_tensor(qo, me, mo, ALU.subtract), v, "v")
                        op(v.tensor_tensor(me, me, mo, ALU.add), v, "v")
                        op(v.tensor_tensor(qo, qo, qo, ALU.mult), v, "v")
                        op(v.tensor_scalar(qo, qo, 0.25, None, ALU.mult), v, "v")
                        op(v.scalar_tensor_tensor(out=rstd[:, :], in0=qe, scalar=1.0 / D, in1=qo,
                                                  op0=ALU.mult, op1=ALU.add), v, "v")
                        ping.give(v)
                        pong.take(v)
                        op(v.reciprocal(rstd[:, :], rstd[:, :]), v, "v")
                        op(v.scalar_tensor_tensor(out=nmr[:, :], in0=me, scalar=-0.5, in1=rstd[:, :],
                                                  op0=ALU.mult, op1=ALU.mult), v, "v")

                    @block.scalar
                    def _(a):
                        ping.take(a)
                        a.activation(rstd[:, :], rstd[:, :], ACT.Sqrt, bias=eps[:, 0:1]).then_inc(pong.sem, 1)

        def dense_loop(nsrc, ncols, wload, pre, post, mid_bias=False, nrows=0, side=None, save=None):
            with ExitStack() as ctx:
                W = sb("weights", [P, max(2 * nsrc, 4 if mid_bias else 2), ncols], F32, ctx)
                rows = sb("bias_rows", [P, nrows, D], F32, ctx) if nrows else None
                mb = sb("mid_bias", [P, 2], F32, ctx) if mid_bias else None
                hs = sb("src_tile", [P, 2, nsrc, D], F32, ctx)
                hT = sb("src_tile_T", [P, 2, 2 * nsrc, P], F32, ctx)
                uT = sb("mid_T", [P, 2, 2, P], F32, ctx) if mid_bias else None
                psT = [bank(f"psT{b}", ctx) for b in (0, 1)]
                psO = [bank(f"psO{b}", ctx) for b in (0, 1)]
                psM = [bank(f"psM{b}", ctx) for b in (0, 1)]
                WS = sb("side_weights", [P, 2, side[1]], F32, ctx) if side else None
                with phase() as block:
                    @block.sync
                    def _(sp):
                        wload(sp, W, rows, mb)
                        sp.wait_ge(s_in.sem, s_in.base)
                        if not side:
                            src_full[0].give(sp)
                        aux_full[0].give(sp)
                        aux_full[1].give(sp)
                        if save:
                            for g in range(GT):
                                s_add.wait(sp, 2 + (g + 1) * GT)
                                for table, view in save:
                                    sp.dma_start(table[g * GT * P:(g + 1) * GT * P, :].rearrange("(t p) c -> p t c", p=P),
                                                 view[:, g * GT:(g + 1) * GT, :]).then_inc(s_st.sem, 16)
                                    s_st.base += 16
                            sp.wait_ge(s_st.sem, s_st.base)

                    @block.scalar
                    def _(a):
                        aux_full[1].take(a)

                        def fill(u):
                            b = u.c % 2
                            src_free[b].take(a)
                            pre(a, u, hs[:, b]).then_inc(hot_full[b].sem, 1)

                        def copyT(u):
                            b = u.c % 2
                            tr_full[b].take(a)
                            a.activation(hT[:, b].rearrange("p k n -> p (k n)"), psT[b][:, 0:2 * nsrc * P], ACT.Copy)\
                                .then_inc(lhs_full[b].sem, 1)

                        def mid(u):
                            b = u.c % 2
                            mid_full[b].take(a)
                            for oc in (0, 1):
                                x = a.activation(uT[:, b, oc, :], psM[b][:, oc * P:(oc + 1) * P], ACT.Relu,
                                                 bias=mb[:, oc:oc + 1])
                            x.then_inc(act_full[b].sem, 1)
                        stages = [(0, fill), (1, copyT)] + ([(2, mid)] if uT is not None else [])
                        pipeline(a, NT, 8, stages)

                    @block.tensor
                    def _(te):
                        src_full[0].take(te)
                        for b in (0, 1):
                            src_free[b].give(te)

                        def trans(u):
                            b = u.c % 2
                            hot_full[b].take(te)
                            for k in range(2 * nsrc):
                                x = te.transpose(psT[b][:, k * P:(k + 1) * P],
                                                 hs[:, b, k // 2, (k % 2) * P:(k % 2 + 1) * P], ident[:, :])
                            x.then_inc(tr_full[b].sem, 1)

                        def midmm(u):
                            b = u.c % 2
                            lhs_full[b].take(te)
                            src_free[b].give(te)
                            for oc in (0, 1):
                                for k in (0, 1):
                                    x = te.matmul(psM[b][:, oc * P:(oc + 1) * P], W[:, 2 + k, oc * P:(oc + 1) * P],
                                                  hT[:, b, k, :], start=k == 0, stop=k == 1)
                            x.then_inc(mid_full[b].sem, 1)

                        def mm(u):
                            b = u.c % 2
                            if uT is None:
                                lhs_full[b].take(te)
                                src_free[b].give(te)
                                lhs = hT
                            else:
                                act_full[b].take(te)
                                lhs = uT
                            s_add.wait(te, u.val + 1)
                            if side:
                                for k in (0, 1):
                                    te.matmul(psM[b][:, 0:side[1]], lhs[:, b, k, :], WS[:, k, :], start=k == 0, stop=k == 1)
                            for k in range(2 * nsrc):
                                x = te.matmul(psO[b][:, 0:ncols], lhs[:, b, k, :], W[:, k, 0:ncols],
                                              start=k == 0, stop=k == 2 * nsrc - 1)
                            x.then_inc(res_full[b].sem, 1)
                        pipeline(te, NT, 8, [(0, trans), (1, mm)] if uT is None else [(0, trans), (1, midmm), (2, mm)])
                        for b in (0, 1):
                            src_free[b].take(te)

                    @block.vector
                    def _(v):
                        aux_full[0].take(v)
                        v.sem_inc(s_add.sem, 2)
                        if side:
                            side[0](v, W, rows, WS)
                            src_full[0].give(v)

                        def use(u):
                            b = u.c % 2
                            res_full[b].take(v)
                            if side:
                                v.tensor_copy(side[2](u), psM[b][:, 0:side[1]])
                            post(v, u, psO[b], rows).then_inc(s_add.sem, 1)
                        pipeline(v, NT, 8, [(0, use)])
                s_add.base += NT + 2

        def ln_pre(view, keep=None):
            def pre(a, u, hs):
                scale, bias = rstd[:, bass.ds(u.val, 1)], nmr[:, bass.ds(u.val, 1)]
                if keep is not None:
                    a.activation(at_tile(keep, u.val), at_tile(view, u.val), ACT.Relu, bias=bias, scale=scale)
                return a.activation(hs[:, 0, :], at_tile(view, u.val), ACT.Relu, bias=bias, scale=scale)
            return pre

        def bcast_row(ap):
            return ap.rearrange("(a n) -> a n", a=1).partition_broadcast(P).rearrange("q a n -> q (a n)")

        def kchunks(w):
            return w.rearrange("(k p) n -> p k n", p=P)

        def segment_softmax(LG, logits, heads, room, last=None, peak=None):
            H = 4
            RL, FW, BW = (part(room[0], k * 3584, [H, SB, P]) for k in range(3))
            fd, bd, first, final = (part(room[1], k * SB * P, [SB, P]) for k in range(4))
            tmp = part(room[1], 4 * SB * P, [SB, P])
            ends = part(room[1], 4500, [SB, 4, H])
            lastrow = part(room[1], 4700, [SB, P])
            TR = part(room[1], 5600, [4, SP_])[0:H]
            RT = part(room[1], 9200, [4, SP_])[0:H]
            with ExitStack() as ctx:
                carry = sb("carry", [P, SB, 3, H], F32, ctx)
                ps = [bank(f"ps_s{b}", ctx) for b in (0, 1)]
                for h0 in range(0, heads, H):
                    mine = logits[:, :, h0:h0 + H]
                    with phase() as block:
                        @block.tensor
                        def _(te):
                            for c in range(SB):
                                b = c % 2
                                res_free[b].take(te)
                                for h in range(H):
                                    x = te.transpose(ps[b][:, h * P:(h + 1) * P], mine[:, c * P:(c + 1) * P, h],
                                                     ident[:, :])
                                x.then_inc(res_full[b].sem, 1)
                            hot_full[0].take(te)
                            for c in range(SB):
                                b = c % 2
                                res_free[b].take(te)
                                for k in range(4):
                                    x = te.transpose(ps[b][0:H, k * P:(k + 1) * P], ends[:, c, k, :], ident[:, :])
                                x.then_inc(res_full[b].sem, 1)
                            hot_full[1].take(te)
                            for c in range(SB):
                                b = c % 2
                                res_free[b].take(te)
                                for k in range(3):
                                    x = te.transpose(ps[b][:, k * H:(k + 1) * H], RT[:, k, c * P:(c + 1) * P],
                                                     ident[0:H, 0:H])
                                x.then_inc(res_full[b].sem, 1)
                            hot_full[0].take(te)
                            for c in range(SB):
                                b = c % 2
                                res_free[b].take(te)
                                for h in range(H):
                                    x = te.transpose(ps[b][:, h * P:(h + 1) * P], RL[:, h, c, :], ident[:, :])
                                x.then_inc(res_full[b].sem, 1)
                            if last is not None:
                                for c in range(SB):
                                    b = (c + SB) % 2
                                    res_free[b].take(te)
                                    te.transpose(ps[b][:, 0:P], lastrow[:, c, :], ident[:, :])\
                                        .then_inc(res_full[b].sem, 1)

                        @block.vector
                        def _(v):
                            for b in (0, 1):
                                res_free[b].give(v)
                            d = dstrow
                            v.memset(fd[:, :, 0:1], -BIG)
                            v.memset(bd[:, :, P - 1:P], -BIG)
                            op(v.tensor_tensor(tmp[:, :, 1:P], d[:, :, 1:P], d[:, :, 0:P - 1], ALU.not_equal), v, "v")
                            v.tensor_scalar(fd[:, :, 1:P], tmp[:, :, 1:P], -BIG, None, ALU.mult)
                            v.tensor_scalar(bd[:, :, 0:P - 1], tmp[:, :, 1:P], -BIG, None, ALU.mult)
                            op(v.tensor_copy(lastrow[:, :, 0:P - 1], tmp[:, :, 1:P]), v, "v")
                            for mask, end in ((first, 0), (final, P - 1)):
                                op(v.tensor_tensor(mask, d[:, :, :], d[:, :, end:end + 1].to_broadcast([P, SB, P]),
                                                   ALU.not_equal), v, "v")
                                op(v.tensor_scalar(mask, mask, -BIG, None, ALU.mult), v, "v")
                            for c in range(SB):
                                b = c % 2
                                res_full[b].take(v)
                                op(v.tensor_copy(RL[:, :, c, :], ps[b][:, 0:512].rearrange("p (h e) -> p h e", e=P)), v, "v")
                                res_free[b].give(v)
                            flat = lambda x: x.rearrange("p c e -> p (c e)")
                            for h in range(H):
                                v.tensor_tensor_scan(flat(FW[:, h]), flat(fd), flat(RL[:, h]), -BIG, ALU.add, ALU.max)
                                op(v.tensor_tensor_scan(flat(BW[:, h])[:, ::-1], flat(bd)[:, ::-1], flat(RL[:, h])[:, ::-1],
                                                        -BIG, ALU.add, ALU.max), v, "v")
                            for h in range(H):
                                v.tensor_copy(ends[:, :, 0, h:h + 1], FW[:, h, :, P - 1:P])
                                v.tensor_copy(ends[:, :, 1, h:h + 1], BW[:, h, :, 0:1])
                                v.tensor_copy(ends[:, :, 2, h:h + 1], d[:, :, 0:1])
                                op(v.tensor_copy(ends[:, :, 3, h:h + 1], d[:, :, P - 1:P]), v, "v")
                            hot_full[0].give(v)
                            for c in range(SB):
                                b = c % 2
                                res_full[b].take(v)
                                op(v.tensor_copy(TR[:, :, c * P:(c + 1) * P],
                                                 ps[b][0:H, 0:512].rearrange("p (k s) -> p k s", s=P)), v, "v")
                                res_free[b].give(v)
                            fend, bst, d0, d1 = (TR[:, k, :] for k in range(4))
                            cf, cb, cont = (RT[:, k, :] for k in range(3))
                            op(v.memset(cont, 0.0), v, "v")
                            op(v.tensor_tensor(cont[:, 0:SP_ - 1], d0[:, 1:SP_], d1[:, 0:SP_ - 1], ALU.is_equal), v, "v")
                            op(v.tensor_tensor(d0, d0, d1, ALU.is_equal), v, "v")
                            op(v.memset(d1[:, 0:1], 0.0), v, "v")
                            op(v.tensor_tensor(d1[:, 1:SP_], d0[:, 1:SP_], cont[:, 0:SP_ - 1], ALU.mult), v, "v")
                            op(v.tensor_scalar(d1, d1, -1.0, BIG, ALU.add, ALU.mult), v, "v")
                            op(v.tensor_tensor_scan(fend, d1, fend, -BIG, ALU.add, ALU.max), v, "v")
                            op(v.tensor_tensor(d1, d0, cont, ALU.mult), v, "v")
                            op(v.tensor_scalar(d1, d1, -1.0, BIG, ALU.add, ALU.mult), v, "v")
                            op(v.tensor_tensor_scan(bst[:, ::-1], d1[:, ::-1], bst[:, ::-1], -BIG, ALU.add, ALU.max), v, "v")
                            op(v.tensor_scalar(d1, cont, -1.0, BIG, ALU.add, ALU.mult), v, "v")
                            v.memset(cf[:, 0:1], -BIG)
                            v.memset(cb[:, SP_ - 1:SP_], -BIG)
                            op(v.tensor_tensor(cf[:, 1:SP_], fend[:, 0:SP_ - 1], d1[:, 0:SP_ - 1], ALU.add), v, "v")
                            op(v.tensor_tensor(cb[:, 0:SP_ - 1], bst[:, 1:SP_], d1[:, 0:SP_ - 1], ALU.add), v, "v")
                            hot_full[1].give(v)
                            for c in range(SB):
                                b = c % 2
                                res_full[b].take(v)
                                op(v.tensor_copy(carry[:, c, :, :], ps[b][:, 0:3 * H].rearrange("p (k h) -> p k h", h=H)), v, "v")
                                res_free[b].give(v)
                            for h in range(H):
                                op(v.tensor_tensor(RL[:, h], FW[:, h], BW[:, h], ALU.max), v, "v")
                                for k, mask in ((0, first), (1, final)):
                                    op(v.tensor_tensor(tmp, mask, carry[:, :, k, h:h + 1].to_broadcast([P, SB, P]),
                                                       ALU.add), v, "v")
                                    op(v.tensor_tensor(RL[:, h], RL[:, h], tmp, ALU.max), v, "v")
                            op(v.tensor_scalar(lastrow[:, :, P - 1:P], carry[:, :, 2, 0:1], -1.0, 1.0, ALU.mult, ALU.add), v, "v")
                            hot_full[0].give(v)
                            MX = part(room[0], 3584, [SB, P, H])
                            for c in range(SB):
                                b = c % 2
                                res_full[b].take(v)
                                op(v.tensor_copy(MX[:, c], ps[b][:, 0:512].rearrange("p (h s) -> p s h", s=P)), v, "v")
                                res_free[b].give(v)
                            mx = MX.rearrange("p c s h -> p (c s) h")
                            if last is not None:
                                for c in range(SB):
                                    b = (c + SB) % 2
                                    res_full[b].take(v)
                                    op(v.tensor_copy(last[:, c * P:(c + 1) * P], ps[b][:, 0:P]), v, "v")
                                    res_free[b].give(v)
                                v.tensor_tensor(peak[:, :, :], mx, last[:, :].unsqueeze(2).to_broadcast([P, SP_, H]), ALU.mult)
                            op(v.tensor_tensor(mine, mine, mx, ALU.subtract), v, "v")
                            ping.give(v)
                            for b in (0, 1):
                                res_free[b].take(v)

                        @block.scalar
                        def _(a):
                            ping.take(a)
                            op(a.activation(mine, mine, ACT.Exp), a, "a")


        def one_hot(v, hot, j, s, weighted):
            if weighted:
                return v.tensor_scalar(hot[:, j, :], iota[:, :], rel[:, bass.ds(s, 1)], wgt[:, bass.ds(s, 1)],
                                       ALU.is_equal, ALU.mult)
            return v.tensor_scalar(hot[:, j, :], iota[:, :], rel[:, bass.ds(s, 1)], None, ALU.is_equal)

        def rows_count(name, n=2):
            return [Count(sem(f"s_rows_{name}{b}")) for b in range(n)]

        def add_steps(v, u, regs, acc, ps, width, nbank):
            nt = ntile(v, u, regs)
            for j in range(GS):
                step_full.take(v)
                s_add.wait(v, u.val * GS + (j + nbank))
                dst_ = at_tile(acc, nt[j])
                v.tensor_tensor(dst_, dst_, ps[(u.c * GS + j) % nbank][:, 0:width], ALU.add).then_inc(s_add.sem, 1)

        def zero_acc(v, acc_flat, nbank):
            op(v.memset(acc_flat, 0.0), v, "v")
            s_add_start(v, nbank)

        def s_add_start(v, nbank):
            v.sem_inc(s_add.sem, nbank)

        def copy_idx(a, idx, u, b):
            return a.activation(idx[:, b, :], gidx[:, bass.ds(u.val * GS, GS)], ACT.Copy)

        def plain_pass(name, table, acc, acc_flat, width, weighted, fold=None):
            NB = 4
            s_rows = rows_count(name)
            with ExitStack() as ctx:
                G = sb("rows_in", [P, 2, GS, width], F32, ctx)
                hot = sb("hot", [P, 2, GS, P], F32, ctx)
                idx = sb("idx", [P, 2, GS], I32, ctx)
                ps = [bank(f"ps_p{i}", ctx) for i in range(NB)]
                if fold:
                    parts = part(fold[1], 0, [2, CHAINS, D])
                    total = part(fold[1], 2 * CHAINS * D, [D])
                with phase() as block:
                    if fold:
                        @block.sync
                        def _(sp):
                            def sums_in(u):
                                b = u.c % 2
                                src_free[b].take(sp)
                                sp.dma_start(parts[:, b], scat.rearrange("(k n) c -> n k c", k=CHAINS)
                                             [bass.ds(u.val * P, P), :, :]).then_inc(s_load[b].sem, 16)
                            pipeline(sp, NT, 2, [(0, sums_in)])

                    @block.scalar
                    def _(a):
                        def index(u):
                            b = u.c % 2
                            slot_free[b].take(a)
                            copy_idx(a, idx, u, b).then_inc(idx_full[b].sem, 1)
                        pipeline(a, NG, 2, [(0, index)])

                    @block.gpsimd
                    def _(g):
                        top_row = g.to_reg(NP - 1)

                        def fetch(u):
                            b = u.c % 2
                            idx_full[b].take(g)
                            for j in range(GS):
                                g.indirect_dma_start(out=G[:, b, j, 0:D], out_offset=None, in_=table,
                                                     in_offset=bass.IndirectOffsetOnAxis(ap=idx[:, b, j:j + 1], axis=0),
                                                     bounds_check=top_row, oob_is_err=True).then_inc(s_rows[b].sem, 16)
                        pipeline(g, NG, 2, [(0, fetch)])

                    @block.tensor
                    def _(te):
                        def multiply(u):
                            b, turn = u.c % 2, u.c // 2
                            hot_full[b].take(te)
                            s_rows[b].wait(te, (u.val - b) * (16 * GS // 2) + 16 * GS)
                            for j in range(GS):
                                s_add.wait(te, u.val * GS + (j + 1))
                                te.matmul(ps[(u.c * GS + j) % NB][:, 0:width], hot[:, b, j, :], G[:, b, j, :],
                                          start=True, stop=True).then_inc(step_full.sem, 1)
                        pipeline(te, NG, 2, [(0, multiply)])

                    @block.vector
                    def _(v):
                        regs = [v.alloc_register(f"nt_{name}{j}") for j in range(GS)]
                        if width > D:
                            op(v.memset(G[:, :, :, D:width], 1.0), v, "v")
                        for b in (0, 1):
                            slot_free[b].give(v)
                        zero_acc(v, acc_flat, NB)

                        def hots(u):
                            b = u.c % 2
                            for j in range(GS):
                                x = one_hot(v, hot[:, b], j, u.val * GS + j, weighted)
                            x.then_inc(hot_full[b].sem, 1)

                        def adds(u):
                            add_steps(v, u, regs, acc, ps, width, NB)
                            slot_free[u.c % 2].give(v)

                        def folds(u):
                            return u.c % 2 == 0 and (not isinstance(u.val, int) or u.val // 2 < NT)

                        def fold_sum(u):
                            b = u.c // 2 % 2
                            if folds(u):
                                s_load[b].wait(v, u.val // 4 * 16 + 16)
                                v.tensor_reduce(total, parts[:, b].rearrange("p k c -> p c k"), AX.X, ALU.add)\
                                    .then_inc(link["v"].sem, 1)

                        def fold_add(u):
                            if folds(u):
                                link["v"].take(v)
                                src_free[u.c // 2 % 2].give(v)
                                x = at_tile(fold[0], u.val // 2)
                                v.tensor_tensor(x, x, total, ALU.add)
                        if fold:
                            for b in (0, 1):
                                src_free[b].give(v)
                            pipeline(v, NG, 4, [(0, hots), (0, fold_sum), (1, adds), (0, fold_add)], steady=2 * (NT - 1))
                            for b in (0, 1):
                                src_free[b].take(v)
                        else:
                            pipeline(v, NG, 2, [(0, hots), (1, adds)])
                        for b in (0, 1):
                            slot_free[b].take(v)
            s_add.base += S + NB
            if fold:
                for b in (0, 1):
                    s_load[b].base += 16 * len(range(b, NT, 2))

        def attention_fetch0(LG, attc, SCR, room):
            PAIRS = S // 2
            G = part(room, 0, [RING, GS, W0])
            s_rows = rows_count("att0_", RING)
            with ExitStack() as ctx:
                hot = sb("hot", [P, 2, 2, P], F32, ctx)
                hotT = sb("hotT", [P, 2, 2, P], F32, ctx)
                dscore = sb("dst_src_scores", [P, GS, HEADS0], F32, ctx)
                feat = sb("feat", [P, 2, 2 * D], F32, ctx)
                featT = sb("featT", [P, 2, 4, P], F32, ctx)
                idx = sb("idx", [P, RING, GS], I32, ctx)
                psT = [bank(f"psT{b}", ctx) for b in (0, 1)]
                psX = [bank(f"psX{b}", ctx) for b in (0, 1)]
                psF = [bank(f"psF{b}", ctx) for b in (0, 1)]
                psL = [bank(f"psL{b}", ctx) for b in (0, 1)]
                QP = GS // 2
                with phase() as block:
                    @block.sync
                    def _(sp):
                        def keep(u):
                            b = u.c % RING
                            s_rows[b].wait(sp, (u.val - b) * (16 * GS // RING) + 16 * GS)
                            sp.dma_start(Eb[bass.ds(u.val, 1), :, :].rearrange("a p (s c) -> p (a s) c", c=D),
                                         G[:, b, :, 0:D]).then_inc(s_keep[b].sem, 16)
                            s_keep[b].wait(sp, (u.val - b) * (16 // RING) + 16)
                            slot_kept[b].give(sp)
                        for b in range(RING):
                            slot_kept[b].give(sp)
                        pipeline(sp, NG, RING, [(0, keep)])
                        for b in range(RING):
                            slot_kept[b].take(sp)

                    @block.gpsimd
                    def _(g):
                        top_row = g.to_reg(NP - 1)

                        def fetch(u):
                            b = u.c % RING
                            idx_full[b].take(g)
                            for j in range(GS):
                                g.indirect_dma_start(out=G[:, b, j, :], out_offset=None, in_=T0,
                                                     in_offset=bass.IndirectOffsetOnAxis(ap=idx[:, b, j:j + 1], axis=0),
                                                     bounds_check=top_row, oob_is_err=True).then_inc(s_rows[b].sem, 16)
                        pipeline(g, NG, RING, [(0, fetch)])

                    @block.scalar
                    def _(a):
                        def index(u):
                            if u.c % QP:
                                return
                            b = u.c // QP % RING
                            slot_free[b].take(a)
                            slot_kept[b].take(a)
                            a.activation(idx[:, b, :], gidx[:, bass.ds(u.val * 2, GS)], ACT.Copy)\
                                .then_inc(idx_full[b].sem, 1)

                        def copyT(u):
                            b = u.c % 2
                            tr_full[b].take(a)
                            hot_free[b].give(a)
                            a.activation(hotT[:, b].rearrange("p k n -> p (k n)"), psT[b][:, 0:2 * P], ACT.Copy)\
                                .then_inc(lhs_full[b].sem, 1)

                        def copyF(u):
                            b = u.c % 2
                            mid_full[b].take(a)
                            a.activation(featT[:, b].rearrange("p k n -> p (k n)"), psF[b][:, :], ACT.Relu)\
                                .then_inc(act_full[b].sem, 1)
                        pipeline(a, PAIRS, RING * QP, [(0, index), (1, copyT), (4, copyF)])

                    @block.tensor
                    def _(te):
                        regs = [te.alloc_register(f"nt_att0{j}") for j in range(GS)]

                        def trans(u):
                            b = u.c % 2
                            hot_full[b].take(te)
                            for k in (0, 1):
                                x = te.transpose(psT[b][:, k * P:(k + 1) * P], hot[:, b, k, :], ident[:, :])
                            x.then_inc(tr_full[b].sem, 1)

                        def fetch_xr(u):
                            b = u.c % 2
                            q = u.c % QP * 2
                            nt = [te.snap(r, min_val=0, max_val=NT - 1) for r in regs[q:q + 2]]
                            gb = u.c // QP % 2
                            lhs_full[b].take(te)
                            if u.c % QP == 0:
                                aux_free[gb].take(te)
                            for k in (0, 1):
                                col = (GS + q + k) * HEADS0
                                te.matmul(psL[gb][:, col:col + HEADS0], hotT[:, b, k, :],
                                          SCR[:, bass.ds(nt[k], 1), HEADS0:2 * HEADS0].rearrange("p a h -> p (a h)"),
                                          start=True, stop=True)
                            for k in (0, 1):
                                x = te.matmul(psX[b][:, k * D:(k + 1) * D], hotT[:, b, k, :], at_tile(A256, nt[k]),
                                              start=True, stop=True)
                            x.then_inc(res_full[b].sem, 1)

                        def load_nt(u):
                            if u.c % QP == 0:
                                te.load(regs, ntab[0:1, bass.ds(u.val * 2, GS)])

                        def transF(u):
                            b = u.c % 2
                            src_full[b].take(te)
                            for k in range(4):
                                x = te.transpose(psF[b][:, k * P:(k + 1) * P], feat[:, b, k * P:(k + 1) * P], ident[:, :])
                            x.then_inc(mid_full[b].sem, 1)

                        def logit(u):
                            b, gb = u.c % 2, u.c // QP % 2
                            act_full[b].take(te)
                            for k in (0, 1):
                                col = (u.c % QP * 2 + k) * HEADS0
                                for c in (0, 1):
                                    x = te.matmul(psL[gb][:, col:col + HEADS0], featT[:, b, 2 * k + c, :], attc[:, c, :],
                                                  start=c == 0, stop=c == 1)
                            if u.c % QP == QP - 1:
                                x.then_inc(aux_full[gb].sem, 1)
                        pipeline(te, PAIRS, RING * QP, [(1, trans), (4, transF), (2, load_nt), (2, fetch_xr), (5, logit)])

                    @block.vector
                    def _(v):
                        for b in range(RING):
                            slot_free[b].give(v)
                        for b in (0, 1):
                            aux_free[b].give(v)
                            hot_free[b].give(v)

                        def hots(u):
                            b = u.c % 2
                            hot_free[b].take(v)
                            for k in (0, 1):
                                x = one_hot(v, hot[:, b], k, u.val * 2 + k, False)
                            x.then_inc(hot_full[b].sem, 1)

                        def feats(u):
                            b, gb = u.c % 2, u.c // QP % RING
                            if u.c % QP == 0:
                                s_rows[gb].wait(v, (u.val - (u.c % (RING * QP))) * (16 * GS // (RING * QP)) + 16 * GS)
                            res_full[b].take(v)
                            q = u.c % QP * 2
                            v.tensor_tensor(feat[:, b, :].rearrange("p (k c) -> p k c", c=D), G[:, gb, q:q + 2, 0:D],
                                            psX[b][:, :].rearrange("p (k c) -> p k c", c=D), ALU.add)\
                                .then_inc(src_full[b].sem, 1)

                        def logits_out(u):
                            gb, rb = u.c // QP % 2, u.c // QP % RING
                            if u.c % QP != QP - 1:
                                return
                            aux_full[gb].take(v)
                            of_steps = lambda k: psL[gb][:, k * GS * HEADS0:(k + 1) * GS * HEADS0]\
                                .rearrange("p (s h) -> p s h", h=HEADS0)
                            op(v.tensor_tensor(dscore[:, :, :], G[:, rb, :, D:W0], of_steps(1), ALU.add), v, "v")
                            slot_free[rb].give(v)
                            op(v.tensor_tensor(LG[:, bass.ds((u.val - (QP - 1)) * 2, GS), :], dscore[:, :, :],
                                               of_steps(0), ALU.add), v, "v")
                            aux_free[gb].give(v)
                        pipeline(v, PAIRS, RING * QP, [(3, feats), (0, hots), (6, logits_out)])
                        for b in range(RING):
                            slot_free[b].take(v)
                        for b in (0, 1):
                            aux_free[b].take(v)
                            hot_free[b].take(v)
            for b in range(RING):
                s_keep[b].base += 16 * NG // RING

        def attention_sum(name, LG, heads, head_major, extras, acc, acc_flat, room):
            NB = 4
            width = D + heads + sum(k for _, k in extras)
            GL = part(room, 0, [2, GS, D])
            Gs = part(room, 2 * GS * D, [2 * GS, width])
            hot = part(room, 2 * GS * (D + width), [2 * GS, P])
            with ExitStack() as ctx:
                ps = [bank(f"ps_p{i}", ctx) for i in range(NB)]
                with phase() as block:
                    @block.sync
                    def _(sp):
                        def back(u):
                            b = u.c % 2
                            src_free[b].take(sp)
                            sp.dma_start(GL[:, b].rearrange("p s c -> p (s c)"),
                                         Eb[bass.ds(u.val, 1), :, :].rearrange("a p c -> p (a c)"))\
                                .then_inc(s_load[b].sem, 16)
                        pipeline(sp, NG, 2, [(0, back)])

                    @block.gpsimd
                    def _(g):
                        for b in (0, 1):
                            src_free[b].give(g)

                        def scale(u):
                            b = u.c % 2
                            s_load[b].wait(g, (u.val - b) * 8 + 16)
                            slot_free[b].take(g)
                            w = LG[:, bass.ds(u.val * GS, GS), :]
                            out_ = Gs[:, b * GS:(b + 1) * GS, 0:D]
                            if head_major:
                                o = out_.rearrange("p s (h c) -> p s h c", h=heads)
                                i = GL[:, b].rearrange("p s (h c) -> p s h c", h=heads)
                                w = w.unsqueeze(3).to_broadcast([P, GS, heads, D // heads])
                            else:
                                o = out_.rearrange("p s (c h) -> p s c h", h=heads)
                                i = GL[:, b].rearrange("p s (c h) -> p s c h", h=heads)
                                w = w.unsqueeze(2).to_broadcast([P, GS, D // heads, heads])
                            op(g.tensor_tensor(o, i, w, ALU.mult), g, "p")
                            aux_full[b].give(g)
                            src_free[b].give(g)
                        pipeline(g, NG, 2, [(0, scale)])
                        for b in (0, 1):
                            src_free[b].take(g)

                    @block.scalar
                    def _(a):
                        def more(u):
                            b = u.c % 2
                            slot_kept[b].take(a)
                            at = D
                            for table, k in [(LG, heads)] + extras:
                                x = a.activation(Gs[:, b * GS:(b + 1) * GS, at:at + k],
                                                 table[:, bass.ds(u.val * GS, GS), :], ACT.Copy)
                                at += k
                            x.then_inc(lhs_full[b].sem, 1)
                        pipeline(a, NG, 2, [(0, more)])

                    @block.tensor
                    def _(te):
                        def multiply(u):
                            b = u.c % 2
                            hot_full[b].take(te)
                            aux_full[b].take(te)
                            lhs_full[b].take(te)
                            for j in range(GS):
                                s_add.wait(te, u.val * GS + (j + 1))
                                te.matmul(ps[(u.c * GS + j) % NB][:, 0:width], hot[:, b * GS + j, :],
                                          Gs[:, b * GS + j, :], start=True, stop=True).then_inc(step_full.sem, 1)
                        pipeline(te, NG, 2, [(0, multiply)])

                    @block.vector
                    def _(v):
                        regs = [v.alloc_register(f"nt_{name}{j}") for j in range(GS)]
                        for b in (0, 1):
                            slot_free[b].give(v)
                            slot_kept[b].give(v)
                        zero_acc(v, acc_flat, NB)

                        def hots(u):
                            b = u.c % 2
                            for j in range(GS):
                                x = one_hot(v, hot[:, b * GS:(b + 1) * GS], j, u.val * GS + j, False)
                            x.then_inc(hot_full[b].sem, 1)

                        def adds(u):
                            add_steps(v, u, regs, acc, ps, width, NB)
                            slot_free[u.c % 2].give(v)
                            slot_kept[u.c % 2].give(v)
                        pipeline(v, NG, 2, [(0, hots), (1, adds)])
                        for b in (0, 1):
                            slot_free[b].take(v)
                            slot_kept[b].take(v)
            s_add.base += S + NB
            for b in (0, 1):
                s_load[b].base += 16 * NG // 2

        def grp(view, u, n=GT):
            return view[:, bass.ds(u.val * n, n), :]

        def column_norm(Y, gamma, beta, finish, beside=None):
            with ExitStack() as ctx:
                ones = sb("ones", [P, 2, P], F32, ctx)
                sq = sb("squares", [P, 2, GT, D], F32, ctx)
                gb = sb("gamma_beta", [P, 2, D], F32, ctx)
                mean = sb("mean", [P, D], F32, ctx)
                psS = bank("ps_sum", ctx)
                psQ = bank("ps_sq", ctx)
                with phase() as block:
                    @block.sync
                    def _(sp):
                        load(sp, gb[:, 0, :], bcast_row(gamma))
                        load(sp, gb[:, 1, :], bcast_row(beta))
                        if beside:
                            beside(sp)
                        sp.wait_ge(s_in.sem, s_in.base)
                        aux_full[0].give(sp)

                    @block.gpsimd
                    def _(g):
                        op(g.memset(ones[:, 0, :], 1.0), g, "p")
                        op(g.affine_select(out=ones[:, 1, :], in_=ones[:, 0, :], compare_op=ALU.is_ge, fill=0.0,
                                           base=TAIL - 1, pattern=[[0, P]], channel_multiplier=-1), g, "p")
                        hot_full[0].give(g)

                    def sums(te, rhs_of, ps, before=None):
                        def one(u):
                            if before:
                                before(u)
                            last_ = isinstance(u.val, int) and u.val == NT - 1
                            x = te.matmul(ps[:, 0:D], ones[:, 1 if last_ else 0, :], rhs_of(u),
                                          start=isinstance(u.val, int) and u.val == 0, stop=last_)
                            return x
                        return one

                    @block.tensor
                    def _(te):
                        hot_full[0].take(te)
                        one = sums(te, lambda u: at_tile(Y, u.val), psS)
                        one(U(0, 0))
                        with te.Fori(1, NT - 1) as i:
                            one(U(i, 1))
                        one(U(NT - 1, 0)).then_inc(ping.sem, 1)

                        def square_group(u):
                            b = u.c % 2
                            src_full[b].take(te)
                            for j in range(GT):
                                first = u.c == 0 and isinstance(u.val, int) and u.val == 0 and j == 0
                                last_ = isinstance(u.val, int) and u.val == GT - 1 and j == GT - 1
                                x = te.matmul(psQ[:, 0:D], ones[:, 1 if last_ else 0, :], sq[:, b, j, :],
                                              start=first, stop=last_)
                            x.then_inc(src_free[b].sem, 1)
                        square_group(U(0, 0))
                        with te.Fori(0, 2) as i:
                            square_group(U(i * 2 + 1, 1))
                            square_group(U(i * 2 + 2, 2))
                        square_group(U(GT - 2, GT - 2))
                        square_group(U(GT - 1, GT - 1))

                    @block.scalar
                    def _(a):
                        for b in (0, 1):
                            src_free[b].give(a)

                        def square(u):
                            b = u.c % 2
                            res_full[0].take(a)
                            src_free[b].take(a)
                            a.activation(sq[:, b], grp(Y, u), ACT.Square).then_inc(src_full[b].sem, 1)
                        pipeline(a, GT, 2, [(0, square)])
                        for b in (0, 1):
                            src_free[b].take(a)
                        pong.give(a)
                        stats_done.take(a)
                        a.activation(mean[:, :], mean[:, :], ACT.Sqrt, bias=eps[:, 0:1]).then_inc(mid_full[0].sem, 1)

                    @block.vector
                    def _(v):
                        ping.take(v)
                        op(v.tensor_scalar(mean[:, :], psS[:, 0:D], 1.0 / N, None, ALU.mult), v, "v")

                        def center(u):
                            y = grp(Y, u)
                            op(v.tensor_tensor(y, y, mean[:, :].unsqueeze(1).to_broadcast([P, GT, D]), ALU.subtract), v, "v")
                            res_full[0].give(v)
                        pipeline(v, GT, 2, [(0, center)])
                        pong.take(v)
                        aux_full[0].take(v)
                        v.drain()
                        op(v.tensor_scalar(mean[:, :], psQ[:, 0:D], 1.0 / N, None, ALU.mult), v, "v")
                        stats_done.give(v)
                        mid_full[0].take(v)
                        op(v.reciprocal(mean[:, :], mean[:, :]), v, "v")
                        op(v.tensor_tensor(mean[:, :], mean[:, :], gb[:, 0, :], ALU.mult), v, "v")

                        def scale(u):
                            y = grp(Y, u)
                            op(v.tensor_tensor(y, y, mean[:, :].unsqueeze(1).to_broadcast([P, GT, D]), ALU.mult), v, "v")
                            op(v.tensor_tensor(y, y, gb[:, 1, :].unsqueeze(1).to_broadcast([P, GT, D]), ALU.add), v, "v")
                            if finish:
                                finish(v, u, y)
                        pipeline(v, GT, GT, [(0, scale)])


        def scatter_pass(SUP, room, table):
            Q = 4
            NQ = S // Q
            RB = 4
            at = 0

            def take(shape):
                nonlocal at
                v = part(room, at, shape)
                at += int(np.prod(shape))
                return v
            hot, same, srow, pairs = (take([2 * Q, P]) for _ in range(4))
            sums = take([RB, Q, D])
            source, row, away = (take([S]) for _ in range(3))
            lower, marked = take([P]), take([Q, P])
            with ExitStack() as ctx:
                dump_row = sb("dump_row", [P, 1], F32, ctx)
                start = sb("accumulator_start", [P, CHAINS], F32, ctx)
                earlier = sb("earlier", [P, 2, Q], F32, ctx)
                idx = sb("idx", [P, RB, Q], I32, ctx)
                psC = [bank(f"psC{b}", ctx) for b in (0, 1)]
                psO = [bank(f"psO{i}", ctx) for i in range(4)]
                s_scat = [Count(sem(f"s_scat{k}")) for k in range(CHAINS)]
                sums_full = [token(f"s_sums_full{b}") for b in range(RB)]
                with phase() as block:
                    @block.sync
                    def _(sp):
                        for g in range(GT):
                            sp.dma_start(table[g * GT * P:(g + 1) * GT * P, :].rearrange("(t p) c -> p t c", p=P),
                                         SUP[:, g * GT:(g + 1) * GT, :]).then_inc(s_st.sem, 16)
                            s_st.base += 16

                        def rows_in(u):
                            b = u.c % 2
                            src_free[b].take(sp)
                            sp.dma_start(srow[:, b * Q:(b + 1) * Q, :].rearrange("p q e -> p (q e)"),
                                         srcrow_d[bass.ds(u.val * Q, Q), :].rearrange("(a q) e -> a (q e)", a=1)
                                         .partition_broadcast(P).rearrange("p a e -> p (a e)")).then_inc(s_load[b].sem, 16)
                        pipeline(sp, NQ, 2, [(0, rows_in)])
                        sp.wait_ge(s_st.sem, s_st.base)

                    @block.gpsimd
                    def _(g):
                        op(g.memset(lower, 1.0), g, "p")
                        g.iota(dump_row[:, :], [[0, 1]], base=NP, channel_multiplier=1,
                               allow_small_or_imprecise_dtypes=True)
                        g.iota(start[:, :], [[ND, CHAINS]], base=0, channel_multiplier=0,
                               allow_small_or_imprecise_dtypes=True)
                        op(g.affine_select(out=lower, in_=lower, compare_op=ALU.is_gt, fill=0.0,
                                           base=0, pattern=[[-1, P]], channel_multiplier=1), g, "p")
                        aux_full[0].give(g)
                        g.wait_ge(s_zero.sem, s_zero.base)
                        nought, bound = g.alloc_register("nought"), g.alloc_register("last_row")
                        g.reg_mov(nought, 0)

                        def scatter(u):
                            b, half = u.c % RB, u.c % 2
                            idx_full[b].take(g)
                            sums_full[b].take(g)
                            for j in range(Q):
                                k = half * Q + j
                                if not isinstance(u.val, int) or u.val >= 2:
                                    s_scat[k].wait(g, (u.val - half) * (16 // 2))
                                g.reg_add(bound, nought, CHAINS * ND - 1)
                                g.indirect_dma_start(out=scat, out_offset=bass.IndirectOffsetOnAxis(ap=idx[:, b, j:j + 1], axis=0),
                                                     in_=sums[:, b, j, :], in_offset=None, bounds_check=bound,
                                                     oob_is_err=True, compute_op=ALU.add).then_inc(s_scat[k].sem, 16)

                        def landed(u):
                            b, half = u.c % RB, u.c % 2
                            if isinstance(u.val, int) and u.val >= NQ - 2:
                                for k in range(half * Q, half * Q + Q):
                                    s_scat[k].wait(g, NQ // 2 * 16)
                            slot_free[b].give(g)
                            slot_kept[b].give(g)
                        for b in range(RB):
                            slot_free[b].give(g)
                            slot_kept[b].give(g)
                        pipeline(g, NQ, RB, [(0, scatter), (2, landed)])
                        for b in range(RB):
                            slot_free[b].take(g)
                            slot_kept[b].take(g)

                    @block.scalar
                    def _(a):
                        def copyC(u):
                            b = u.c % 2
                            tr_full[b].take(a)
                            hot_free[b].give(a)
                            src_free[b].give(a)
                            a.activation(pairs[:, b * Q:(b + 1) * Q, :].rearrange("p q e -> p (q e)"), psC[b][:, :], ACT.Copy)\
                                .then_inc(lhs_full[b].sem, 1)

                        def copyO(u):
                            b = u.c % 2
                            slot_free[u.c % RB].take(a)
                            for j in range(2):
                                res_full[j].take(a)
                                op(a.activation(sums[:, u.c % RB, 2 * j:2 * j + 2, :].rearrange("p q c -> p (q c)"),
                                                psO[2 * b + j][:, :], ACT.Copy), a, "a")
                                res_free[j].give(a)
                            sums_full[u.c % RB].give(a)
                        for b in (0, 1):
                            hot_free[b].give(a)
                            src_free[b].give(a)
                            res_free[b].give(a)
                            res_free[b].give(a)
                        pipeline(a, NQ, RB, [(0, copyC), (1, copyO)])
                        for b in (0, 1):
                            hot_free[b].take(a)
                            src_free[b].take(a)
                            res_free[b].take(a, 2)

                    @block.tensor
                    def _(te):
                        regs = [te.alloc_register(f"nt_sc{j}") for j in range(Q)]

                        def pairmm(u):
                            b = u.c % 2
                            hot_full[b].take(te)
                            for j in range(Q):
                                x = te.matmul(psC[b][:, j * P:(j + 1) * P], hot[:, b * Q + j, :], same[:, b * Q + j, :],
                                              start=True, stop=True)
                            x.then_inc(tr_full[b].sem, 1)

                        def summm(u):
                            b = u.c % 2
                            te.load(regs, ntab[0:1, bass.ds(u.val * Q, Q)])
                            nt = [te.snap(r, min_val=0, max_val=NT - 1) for r in regs]
                            lhs_full[b].take(te)
                            for j in range(Q):
                                if j % 2 == 0:
                                    res_free[j // 2].take(te)
                                x = te.matmul(psO[2 * b + j // 2][:, j % 2 * D:(j % 2 + 1) * D], pairs[:, b * Q + j, :],
                                              at_tile(SUP, nt[j]), start=True, stop=True)
                                if j % 2:
                                    x.then_inc(res_full[j // 2].sem, 1)
                        pipeline(te, NQ, 2, [(0, pairmm), (1, summm)])

                    @block.vector
                    def _(v):
                        aux_full[0].take(v)
                        op(v.tensor_copy(source, gidx[:, :]), v, "v")
                        v.tensor_tensor(row.rearrange("p (n k) -> p n k", k=CHAINS),
                                        source.rearrange("p (n k) -> p n k", k=CHAINS),
                                        start[:, :].unsqueeze(1).to_broadcast([P, S // CHAINS, CHAINS]), ALU.add)
                        op(v.tensor_scalar(away, source, -1.0, dump_row[:, 0:1], ALU.mult, ALU.add), v, "v")

                        def marks(u):
                            b, rb = u.c % 2, u.c % RB
                            hot_free[b].take(v)
                            src = [source[:, bass.ds(u.val * Q + j, 1)] for j in range(Q)]
                            steps = bass.ds(u.val * Q, Q)
                            for j in range(Q):
                                one_hot(v, hot[:, b * Q:(b + 1) * Q], j, u.val * Q + j, True)
                            s_load[b].wait(v, (u.val - b) * (16 // 2) + 16)
                            for j in range(Q):
                                x = v.scalar_tensor_tensor(out=marked[:, j, :], in0=srow[:, b * Q + j, :], scalar=src[j], in1=lower,
                                                           op0=ALU.is_equal, op1=ALU.mult, accum_out=earlier[:, b, j:j + 1])
                            x.then_inc(link["v"].sem, 1)
                            for j in range(Q):
                                x = v.tensor_scalar(same[:, b * Q + j, :], srow[:, b * Q + j, :], src[j], None, ALU.is_equal)
                            x.then_inc(hot_full[b].sem, 1)
                            link["v"].take(v)
                            op(v.scalar_tensor_tensor(out=earlier[:, b, :], in0=earlier[:, b, :], scalar=0.0, in1=away[:, steps],
                                                      op0=ALU.is_gt, op1=ALU.mult), v, "v")
                            slot_kept[rb].take(v)
                            v.tensor_tensor(idx[:, rb, :], earlier[:, b, :], row[:, steps], ALU.add)\
                                .then_inc(idx_full[rb].sem, 1)
                        pipeline(v, NQ, RB, [(0, marks)])
            for b in (0, 1):
                s_load[b].base += 16 * NQ // 2

        def attention_fetch3(LG, SV, rows_room, T_room, WT):
            G = part(rows_room, 0, [RING, GS, WT])
            s_rows = rows_count("att3_", RING)
            with ExitStack() as ctx:
                hot = part(T_room, 0, [2 * GS, P])
                hotT = part(T_room, 2 * GS * P, [2 * GS, P])
                raw = sb("raw_logits", [P, GS, HEADS3], F32, ctx)
                idx = sb("idx", [P, RING, GS], I32, ctx)
                psT = [[bank(f"psT{b}{k}", ctx) for k in (0, 1)] for b in (0, 1)]
                psS = [bank(f"psS{b}", ctx) for b in (0, 1)]
                with phase() as block:
                    @block.sync
                    def _(sp):
                        def keep(u):
                            b = u.c % RING
                            s_rows[b].wait(sp, (u.val - b) * (16 * GS // RING) + 16 * GS)
                            sp.dma_start(Eb[bass.ds(u.val, 1), :, :].rearrange("a p (s c) -> p (a s) c", c=D),
                                         G[:, b, :, 0:D]).then_inc(s_keep[b].sem, 16)
                            s_keep[b].wait(sp, (u.val - b) * (16 // RING) + 16)
                            slot_kept[b].give(sp)
                        for b in range(RING):
                            slot_kept[b].give(sp)
                        pipeline(sp, NG, RING, [(0, keep)])
                        for b in range(RING):
                            slot_kept[b].take(sp)

                    @block.gpsimd
                    def _(g):
                        top_row = g.to_reg(NP - 1)

                        def fetch(u):
                            b = u.c % RING
                            idx_full[b].take(g)
                            for j in range(GS):
                                g.indirect_dma_start(out=G[:, b, j, :], out_offset=None, in_=T4,
                                                     in_offset=bass.IndirectOffsetOnAxis(ap=idx[:, b, j:j + 1], axis=0),
                                                     bounds_check=top_row, oob_is_err=True).then_inc(s_rows[b].sem, 16)
                        pipeline(g, NG, RING, [(0, fetch)])

                    @block.scalar
                    def _(a):
                        def index(u):
                            b = u.c % RING
                            slot_free[b].take(a)
                            slot_kept[b].take(a)
                            a.activation(idx[:, b, :], gidx[:, bass.ds(u.val * GS, GS)], ACT.Copy)\
                                .then_inc(idx_full[b].sem, 1)

                        def copyT(u):
                            b = u.c % 2
                            tr_full[b].take(a)
                            for k in (0, 1):
                                x = a.activation(hotT[:, b * GS + 4 * k:b * GS + 4 * k + 4, :].rearrange("p j n -> p (j n)"),
                                                 psT[b][k][:, :], ACT.Copy)
                            x.then_inc(lhs_full[b].sem, 1)
                        pipeline(a, NG, RING, [(0, index), (2, copyT)])

                    @block.tensor
                    def _(te):
                        regs = [te.alloc_register(f"nt_att3{j}") for j in range(GS)]

                        def trans(u):
                            b = u.c % 2
                            hot_full[b].take(te)
                            for j in range(GS):
                                x = te.transpose(psT[b][j // 4][:, j % 4 * P:(j % 4 + 1) * P], hot[:, b * GS + j, :], ident[:, :])
                            x.then_inc(tr_full[b].sem, 1)

                        def scores(u):
                            b = u.c % 2
                            nt = ntile(te, u, regs)
                            lhs_full[b].take(te)
                            res_free[b].take(te)
                            for j in range(GS):
                                x = te.matmul(psS[b][:, j * HEADS3:(j + 1) * HEADS3], hotT[:, b * GS + j, :],
                                              at_tile(SV, nt[j]), start=True, stop=True)
                            x.then_inc(res_full[b].sem, 1)
                        pipeline(te, NG, RING, [(2, trans), (3, scores)])

                    @block.vector
                    def _(v):
                        op(v.memset(LG[:, :, :], 0.0), v, "v")
                        for b in range(RING):
                            slot_free[b].give(v)
                        for b in (0, 1):
                            res_free[b].give(v)

                        def hots(u):
                            b = u.c % 2
                            for j in range(GS):
                                x = one_hot(v, hot[:, b * GS:(b + 1) * GS], j, u.val * GS + j, False)
                            x.then_inc(hot_full[b].sem, 1)

                        def logits(u):
                            b, gb = u.c % 2, u.c % RING
                            s_rows[gb].wait(v, (u.val - gb) * (16 * GS // RING) + 16 * GS)
                            res_full[b].take(v)
                            op(v.tensor_tensor(raw[:, :, :], G[:, gb, :, D:WT],
                                               psS[b][:, 0:GS * HEADS3].rearrange("p (s h) -> p s h", h=HEADS3), ALU.add), v, "v")
                            slot_free[gb].give(v)
                            res_free[b].give(v)
                            op(v.scalar_tensor_tensor(out=LG[:, bass.ds(u.val * GS, GS), :], in0=raw[:, :, :], scalar=0.2,
                                                      in1=raw[:, :, :], op0=ALU.mult, op1=ALU.max), v, "v")
                        pipeline(v, NG, RING, [(2, logits), (0, hots)])
                        for b in range(RING):
                            slot_free[b].take(v)
                        for b in (0, 1):
                            res_free[b].take(v)
            for b in range(RING):
                s_keep[b].base += 16 * NG // RING

        ln_stats(B256)
        XL, XR, H0 = B256, A256, C256

        def w0(sp, W, rows, mb):
            load(sp, W[:, 0:2, 0:D], kchunks(t["L0_gnn_W_l"]))
            load(sp, W[:, 0:2, D:2 * D], kchunks(t["L0_gnn_W_r"]))
            load(sp, rows[:, 0, :], bcast_row(t["L0_gnn_att"].rearrange("h c -> (h c)")))

        def score_weights(v, W, rows, WS):
            prod = part(A, 0, [2, 2, D])
            op(v.tensor_tensor(prod, W[:, 0:2, 0:2 * D].rearrange("p k (w n) -> p k w n", w=2),
                               rows[:, 0, :].unsqueeze(1).unsqueeze(1).to_broadcast([P, 2, 2, D]), ALU.mult), v, "v")
            op(v.tensor_reduce(WS.rearrange("p k h -> p (k h)"), part(A, 0, [4 * HEADS0, D // HEADS0]), AX.X, ALU.add), v, "v")
            op(v.tensor_scalar(WS[:, :, :], WS[:, :, :], 0.2, None, ALU.mult), v, "v")

        def post0(v, u, ps, rows):
            v.tensor_copy(at_tile(XL, u.val), ps[:, 0:D])
            return v.tensor_copy(at_tile(XR, u.val), ps[:, D:2 * D])

        SCR = node_scores
        dense_loop(1, 2 * D, w0, ln_pre(B256, H0), post0, nrows=1,
                   side=(score_weights, 2 * HEADS0, lambda u: at_tile(SCR, u.val)),
                   save=[(T0[:, 0:D], XL), (T0[:, D:W0], SCR[:, :, 0:HEADS0])])

        def bc(ap, shape):
            return ap.to_broadcast(shape)

        with ExitStack() as L0:
            LG = sb("logits0", [P, SP_, HEADS0], F32, L0)
            SL = sb("self_logits", [P, NT, HEADS0], F32, L0)
            attc = sb("att_cols", [P, 2, HEADS0], F32, L0)
            with ExitStack() as ctx:
                f = sb("self_feat", [P, GT, D], F32, ctx)
                attr = sb("att_row", [P, D], F32, ctx)
                with phase() as block:
                    @block.sync
                    def _(sp):
                        load(sp, attr[:, :], bcast_row(t["L0_gnn_att"].rearrange("h c -> (h c)")))
                        ping.take(sp)
                        for h in range(HEADS0):
                            load(sp, attc[h % 2 * 64:h % 2 * 64 + 64, h // 2, h:h + 1],
                                 t["L0_gnn_att"][h:h + 1, :].rearrange("a c -> c a"), allow_slow_non_contiguous=True)
                        sp.wait_ge(s_in.sem, s_in.base)
                        aux_full[0].give(sp)

                    @block.vector
                    def _(v):
                        op(v.memset(attc[:, :, :], 0.0), v, "v")
                        ping.give(v)
                        op(v.memset(LG[:, :, :], 0.0), v, "v")
                        aux_full[0].take(v)
                        op(v.tensor_scalar(attc[:, :, :], attc[:, :, :], 0.8, None, ALU.mult), v, "v")

                        def self_logit(u):
                            op(v.tensor_tensor(f[:, :, :], grp(B256, u), grp(A256, u), ALU.add), v, "v")
                            op(v.scalar_tensor_tensor(out=f[:, :, :], in0=f[:, :, :], scalar=0.2, in1=f[:, :, :],
                                                      op0=ALU.mult, op1=ALU.max), v, "v")
                            op(v.tensor_tensor(f[:, :, :], f[:, :, :], attr[:, :].unsqueeze(1).to_broadcast([P, GT, D]),
                                               ALU.mult), v, "v")
                            op(v.tensor_reduce(grp(SL, u).rearrange("p t h -> p (t h)"),
                                               f[:, :, :].rearrange("p t (h c) -> p (t h) c", h=HEADS0), AX.X, ALU.add), v, "v")
                        pipeline(v, GT, GT, [(0, self_logit)])
            attention_fetch0(LG, attc, SCR, B)
            PK = sb("peaks", [P, SP_, HEADS0], F32, L0)
            LS = sb("last_marks", [P, SP_], F32, L0)
            segment_softmax(LG, LG[:, :, :], HEADS0, (A, B), last=LS[:, :], peak=PK)
            WB = D + 2 * HEADS0 + 1
            ACCB = tiles(B, WB)
            attention_sum("a0", LG, HEADS0, True, [(PK, HEADS0), (LS[:, :].unsqueeze(2), 1)],
                          ACCB, B[:, 0:NT * WB], A)
            with ExitStack() as ctx:
                xl = part(A, 0, [GT, D])
                biasr = sb("bias_row", [P, D], F32, ctx)
                sm = [sb(f"small{k}", [P, GT, HEADS0], F32, ctx) for k in range(4)]
                with phase() as block:
                    @block.sync
                    def _(sp):
                        load(sp, biasr[:, :], bcast_row(t["L0_gnn_bias"]))
                        sp.wait_ge(s_in.sem, s_in.base)
                        aux_full[0].give(sp)

                        def group(u):
                            src_free[0].take(sp)
                            sp.dma_start(xl[:, :, :], T0[bass.ds(u.val * (GT * P), GT * P), 0:D].rearrange("(t p) c -> p t c", p=P))\
                                .then_inc(s_load[0].sem, 16)
                        pipeline(sp, GT, GT, [(0, group)])

                    @block.scalar
                    def _(a):
                        def exps(u):
                            src_full[0].take(a)
                            op(a.activation(sm[0][:, :, :], sm[0][:, :, :], ACT.Exp), a, "a")
                            a.activation(sm[1][:, :, :], sm[1][:, :, :], ACT.Exp).then_inc(src_full[1].sem, 1)
                        pipeline(a, GT, GT, [(0, exps)])

                    @block.vector
                    def _(v):
                        aux_full[0].take(v)
                        src_free[0].give(v)

                        def join(u):
                            acc = ACCB[:, bass.ds(u.val * GT, GT), :]
                            wsum, peak, hit = acc[:, :, D:D + 4], acc[:, :, D + 4:D + 8], acc[:, :, D + 8:D + 9]
                            e, s_, x2, x3 = (k[:, :, :] for k in sm)
                            sl = SL[:, bass.ds(u.val * GT, GT), :]
                            bw = [P, GT, HEADS0]
                            op(v.tensor_scalar(x2[:, :, 0:1], hit, -1.0, BIG, ALU.add, ALU.mult), v, "v")
                            op(v.tensor_tensor(e, peak, x2[:, :, 0:1].to_broadcast(bw), ALU.add), v, "v")
                            op(v.tensor_tensor(x3, e, sl, ALU.max), v, "v")
                            op(v.tensor_tensor(e, e, x3, ALU.subtract), v, "v")
                            op(v.tensor_tensor(s_, sl, x3, ALU.subtract), v, "v")
                            src_full[0].give(v)
                            src_full[1].take(v)
                            op(v.tensor_tensor(x2, wsum, e, ALU.mult), v, "v")
                            op(v.tensor_tensor(x2, x2, s_, ALU.add), v, "v")
                            op(v.tensor_scalar(x2, x2, 1e-16, None, ALU.add), v, "v")
                            op(v.reciprocal(x2, x2), v, "v")
                            op(v.tensor_tensor(e, e, x2, ALU.mult), v, "v")
                            op(v.tensor_tensor(s_, s_, x2, ALU.mult), v, "v")
                            heads_of = lambda z: z.rearrange("p t (h c) -> p t h c", h=HEADS0)
                            wide = [P, GT, HEADS0, D // HEADS0]
                            rows_ = acc[:, :, 0:D]
                            op(v.tensor_tensor(heads_of(rows_), heads_of(rows_), e.unsqueeze(3).to_broadcast(wide), ALU.mult), v, "v")
                            s_load[0].wait(v, u.val * 16 + 16)
                            op(v.tensor_tensor(heads_of(xl[:, :, :]), heads_of(xl[:, :, :]), s_.unsqueeze(3).to_broadcast(wide),
                                               ALU.mult), v, "v")
                            op(v.tensor_tensor(rows_, rows_, xl[:, :, :], ALU.add), v, "v")
                            src_free[0].give(v)
                            h = grp(C256, u)
                            op(v.tensor_tensor(h, h, rows_, ALU.add), v, "v")
                            op(v.tensor_tensor(h, h, biasr[:, :].unsqueeze(1).to_broadcast([P, GT, D]), ALU.add), v, "v")
                        pipeline(v, GT, GT, [(0, join)])
                        src_free[0].take(v)
                        v.memset(B256[:, NT - 1, :], 0.0)
                        v.memset(zero_rows[:, :, :], 0.0)
                s_load[0].base += 16 * GT

        def beside_norm(sp):
            sp.dma_start(B256[:, 0:NT - 1, :], t["x"][0:(NT - 1) * P, :].rearrange("(t p) c -> p t c", p=P))\
                .then_inc(s_back.sem, 16)
            sp.dma_start(B256[0:TAIL, NT - 1, :], t["x"][(NT - 1) * P:N, :]).then_inc(s_back.sem, 16)
            s_back.base += 32
            per = ND // P
            for k in range(CHAINS):
                sp.dma_start(scat[k * ND:(k + 1) * ND, :].rearrange("(p r) c -> p r c", p=P),
                             zero_rows[:, :, :].to_broadcast([P, per, D])).then_inc(s_zero.sem, 16)
                s_zero.base += 16

        column_norm(C256, t["L0_gnn_gamma1"], t["L0_gnn_beta1"], None, beside_norm)

        def w_ffn(sp, W, rows, mb):
            load(sp, W[:, 2:4, :], kchunks(t["L0_gnn_W1"]))
            load(sp, W[:, 0:2, :], kchunks(t["L0_gnn_W2"]))
            load(sp, rows[:, 0, :], bcast_row(t["L0_gnn_b2"]))
            load(sp, mb[:, :], t["L0_gnn_b1"].rearrange("(k p) -> p k", p=P), allow_slow_non_contiguous=True)

        def copy_pre(a, u, hs):
            return a.activation(hs[:, 0, :], at_tile(C256, u.val), ACT.Copy)

        def post_ffn(v, u, ps, rows):
            y = at_tile(C256, u.val)
            op(v.tensor_tensor(y, y, ps[:, 0:D], ALU.add), v, "v")
            return v.tensor_tensor(y, y, rows[:, 0, :], ALU.add)

        dense_loop(1, D, w_ffn, copy_pre, post_ffn, mid_bias=True, nrows=1)
        def add_residual(v, u, y):
            x = grp(B256, u)
            if isinstance(u.val, int) and u.val == 0:
                v.wait_ge(s_back.sem, s_back.base)
            op(v.tensor_tensor(x, x, y, ALU.add), v, "v")

        column_norm(C256, t["L0_gnn_gamma2"], t["L0_gnn_beta2"], add_residual)

        ln_stats(B256)

        def w_one(name):
            def w(sp, W, rows, mb):
                load(sp, W[:, 0:2, :], kchunks(t[name]))
            return w

        def post_support(v, u, ps, rows):
            return v.tensor_copy(at_tile(A256, u.val), ps[:, 0:D])

        dense_loop(1, D, w_one("L1_gnn_weight"), ln_pre(B256), post_support)
        scatter_pass(A256, C, T1)
        plain_pass("l1", T1, C256, C[:, 0:NT * D], D, True, fold=(B256, A))

        with ExitStack() as ctx:
            biasr = sb("bias_row", [P, D], F32, ctx)
            with phase() as block:
                @block.sync
                def _(sp):
                    load(sp, biasr[:, :], bcast_row(t["L1_gnn_bias"]))
                    loaded(sp)
                    aux_full[0].give(sp)

                @block.vector
                def _(v):
                    aux_full[0].take(v)

                    def add(u):
                        x = grp(B256, u)
                        op(v.tensor_tensor(x, x, grp(C256, u), ALU.add), v, "v")
                        v.tensor_tensor(x, x, biasr[:, :].unsqueeze(1).to_broadcast([P, GT, D]), ALU.add)
                    pipeline(v, GT, GT, [(0, add)])

        ln_stats(B256)
        with phase() as block:
            @block.scalar
            def _(a):
                def norm(u):
                    x = a.activation(at_tile(A256, u.val), at_tile(B256, u.val), ACT.Relu,
                                     bias=nmr[:, bass.ds(u.val, 1)], scale=rstd[:, bass.ds(u.val, 1)])
                    if u.c % GT == GT - 1:
                        x.then_inc(res_full[0].sem, 1)
                pipeline(a, NT, GT, [(0, norm)])

            @block.sync
            def _(sp):
                for g in range(GT):
                    res_full[0].take(sp)
                    sp.dma_start(T2[g * GT * P:(g + 1) * GT * P, :].rearrange("(t p) c -> p t c", p=P),
                                 A256[:, g * GT:(g + 1) * GT, :]).then_inc(s_st.sem, 16)
                    s_st.base += 16
                sp.wait_ge(s_st.sem, s_st.base)
        WC = D + 1
        ACC1 = tiles(C, WC)
        plain_pass("l2a", T2, ACC1, C[:, 0:NT * WC], WC, False)

        def conv_weights(k):
            def w(sp, W, rows, mb):
                load(sp, W[:, 0:2, :], kchunks(t[f"L2_gnn_W{k}_msg"]))
                load(sp, W[:, 2:4, :], kchunks(t[f"L2_gnn_W{k}_self"]))
                load(sp, rows[:, 0, :], bcast_row(t[f"L2_gnn_b{k}_msg"]))
                load(sp, rows[:, 1, :], bcast_row(t[f"L2_gnn_b{k}_self"]))
            return w

        def conv_pre(acc):
            def pre(a, u, hs):
                a.activation(hs[:, 0, :], acc[:, bass.ds(u.val, 1), 0:D].rearrange("p a c -> p (a c)"), ACT.Copy)
                return a.activation(hs[:, 1, :], at_tile(A256, u.val), ACT.Copy)
            return pre

        def post_conv1(v, u, ps, rows):
            y = at_tile(A256, u.val)
            dg = ACC1[:, bass.ds(u.val, 1), D:D + 1].rearrange("p a c -> p (a c)")
            v.tensor_copy(deg[:, bass.ds(u.val, 1)], dg)
            op(v.scalar_tensor_tensor(out=y, in0=rows[:, 0, :], scalar=dg, in1=ps[:, 0:D], op0=ALU.mult, op1=ALU.add), v, "v")
            op(v.tensor_tensor(y, y, rows[:, 1, :], ALU.add), v, "v")
            return v.scalar_tensor_tensor(out=y, in0=y, scalar=0.1, in1=y, op0=ALU.mult, op1=ALU.max)

        dense_loop(2, D, conv_weights(1), conv_pre(ACC1), post_conv1, nrows=2, save=[(T3, A256)])
        plain_pass("l2b", T3, C256, C[:, 0:NT * D], D, False)

        def post_conv2(v, u, ps, rows):
            y, x = at_tile(C256, u.val), at_tile(B256, u.val)
            op(v.scalar_tensor_tensor(out=y, in0=rows[:, 0, :], scalar=deg[:, bass.ds(u.val, 1)], in1=ps[:, 0:D],
                                      op0=ALU.mult, op1=ALU.add), v, "v")
            op(v.tensor_tensor(y, y, rows[:, 1, :], ALU.add), v, "v")
            return v.tensor_tensor(x, x, y, ALU.add)

        dense_loop(2, D, conv_weights(2), conv_pre(C256), post_conv2, nrows=2)

        ln_stats(B256)
        WT = D + HEADS3
        H4 = tiles(A, WT)
        with ExitStack() as L3:
            LG3 = sb("logits3", [P, SP_, HEADS3], F32, L3)
            SV = node_scores

            def w_uv(sp, W, rows, mb):
                load(sp, W[:, 0:2, 0:2 * HEADS3], kchunks(t["W_uv"]))
                load(sp, rows[:, 0, 0:HEADS3], bcast_row(t["L3_gnn_b_u"]))

            def pre_uv(a, u, hs):
                scale, bias = rstd[:, bass.ds(u.val, 1)], nmr[:, bass.ds(u.val, 1)]
                a.activation(H4[:, bass.ds(u.val, 1), 0:D].rearrange("p a c -> p (a c)"), at_tile(B256, u.val),
                             ACT.Relu, bias=bias, scale=scale)
                return a.activation(hs[:, 0, :], at_tile(B256, u.val), ACT.Relu, bias=bias, scale=scale)

            def post_uv(v, u, ps, rows):
                v.tensor_tensor(H4[:, bass.ds(u.val, 1), D:WT].rearrange("p a c -> p (a c)"), ps[:, 0:HEADS3],
                                rows[:, 0, 0:HEADS3], ALU.add)
                return v.tensor_copy(at_tile(SV, u.val), ps[:, HEADS3:2 * HEADS3])

            dense_loop(1, 2 * HEADS3, w_uv, pre_uv, post_uv, nrows=1, save=[(T4, H4)])
            attention_fetch3(LG3, SV, C, A, WT)
            segment_softmax(LG3, LG3[:, :, :], HEADS3, (A, C))
            ACC3 = tiles(C, WT)
            attention_sum("a3", LG3, HEADS3, False, [], ACC3, C[:, 0:NT * WT], A)
            with ExitStack() as ctx:
                rd = sb("denominators", [P, GT, HEADS3], F32, ctx)
                with phase() as block:
                    @block.vector
                    def _(v):
                        def final(u):
                            acc = ACC3[:, bass.ds(u.val * GT, GT), :]
                            op(v.tensor_scalar(rd[:, :, :], acc[:, :, D:WT], 0.5, None, ALU.max), v, "v")
                            op(v.reciprocal(rd[:, :, :], rd[:, :, :]), v, "v")
                            rows_ = acc[:, :, 0:D].rearrange("p t (c h) -> p t c h", h=HEADS3)
                            op(v.tensor_tensor(rows_, rows_, rd[:, :, :].unsqueeze(2).to_broadcast([P, GT, D // HEADS3, HEADS3]),
                                               ALU.mult), v, "v")
                            x = grp(B256, u)
                            op(v.tensor_tensor(x, x, acc[:, :, 0:D], ALU.add), v, "v")
                            res_full[0].give(v)
                        pipeline(v, GT, GT, [(0, final)])

                    @block.sync
                    def _(sp):
                        for g in range(GT - 1):
                            res_full[0].take(sp)
                            sp.dma_start(out[g * GT * P:(g + 1) * GT * P, :].rearrange("(t p) c -> p t c", p=P),
                                         B256[:, g * GT:(g + 1) * GT, :]).then_inc(s_st.sem, 16)
                        res_full[0].take(sp)
                        g = GT - 1
                        sp.dma_start(out[g * GT * P:(NT - 1) * P, :].rearrange("(t p) c -> p t c", p=P),
                                     B256[:, g * GT:NT - 1, :]).then_inc(s_st.sem, 16)
                        sp.dma_start(out[(NT - 1) * P:N, :], B256[0:TAIL, NT - 1, :]).then_inc(s_st.sem, 16)
                        s_st.base += 16 * (GT + 1)
                        sp.wait_ge(s_st.sem, s_st.base)


_INS = ['x', 'L0_gnn_W_l', 'L0_gnn_W_r', 'L0_gnn_att', 'L0_gnn_bias', 'L0_gnn_W1', 'L0_gnn_b1', 'L0_gnn_W2',
        'L0_gnn_b2', 'L0_gnn_gamma1', 'L0_gnn_beta1', 'L0_gnn_gamma2', 'L0_gnn_beta2', 'L1_gnn_weight',
        'L1_gnn_bias', 'L1_gnn_alpha', 'L2_gnn_W1_msg', 'L2_gnn_b1_msg', 'L2_gnn_W1_self', 'L2_gnn_b1_self',
        'L2_gnn_W2_msg', 'L2_gnn_b2_msg', 'L2_gnn_W2_self', 'L2_gnn_b2_self', 'L3_gnn_b_u']


def kernel(**inputs):
    import concourse.bacc as bacc
    from concourse.bass_utils import run_bass_kernel_spmd as run

    nc = bacc.Bacc("TRN2", target_bir_lowering=False, num_devices=1)
    arrays, t = {}, {}

    def give(name, a):
        a = np.ascontiguousarray(a)
        arrays[f"in_{name}"] = a
        t[name] = nc.dram_tensor(f"in_{name}", a.shape, mybir.dt.from_np(a.dtype), kind="ExternalInput").ap()

    for name in _INS:
        give(name, inputs[name])
    pad = EP - E
    dst = np.pad(np.asarray(inputs["dst"]), (0, pad), constant_values=N).reshape(ET, P)
    src = np.pad(np.asarray(inputs["src"]), (0, pad)).reshape(ET, P)
    typ = np.pad(np.asarray(inputs["edge_type_11"]), (0, pad), constant_values=RELS).reshape(ET, P)
    give("edge_tiles", np.concatenate([dst, src, typ], axis=1))
    give("dst_last", dst[:, P - 1])
    give("W_uv", np.concatenate([np.asarray(inputs["L3_gnn_W_u"]).T, np.asarray(inputs["L3_gnn_W_v"]).T], axis=1))
    out = nc.dram_tensor("out0", (N, D), F32, kind="ExternalOutput").ap()
    build(nc, t, out)
    r = run(nc, [arrays], core_ids=[0])
    return r.results[0]["out0"]
```

```python
from contextlib import ExitStack

import numpy as np

import concourse.bass as bass
from concourse import mybir

F32 = mybir.dt.float32
I32 = mybir.dt.int32
ALU = mybir.AluOpType
ACT = mybir.ActivationFunctionType
AX = mybir.AxisListType

P = 128
N, D, E = 6250, 256, 100000
NT = -(-N // P)
NP = NT * P
TAIL = N - (NT - 1) * P
ET = 784
EP = ET * P
S = ET + NT - 1
GS = 8
NG = S // GS
SB = -(-S // P)
SP_ = SB * P
HEADS0, HEADS3 = 4, 8
WT = D + HEADS3
RELS = 11
LN_EPS = BN_EPS = 1e-5
BIG = 1e30
GT = 7
ND = NP + P
RING = 4
CHAINS = 8
assert S % (RING * GS) == 0 and NT == GT * GT and TAIL > 0


class Token:

    def __init__(self, sem):
        self.sem = sem

    def take(self, eng, n=1):
        eng.wait_ge(self.sem, n)
        eng.sem_inc(self.sem, -n)

    def give(self, eng, n=1):
        eng.sem_inc(self.sem, n)


class Count:

    def __init__(self, sem):
        self.sem, self.base = sem, 0

    def wait(self, eng, value):
        eng.wait_ge(self.sem, value + self.base)


class U:

    def __init__(self, val, c):
        self.val, self.c = val, c


def pipeline(eng, total, body, stages, steady=None):
    maxlag = max(lag for lag, _ in stages)
    first = -(-maxlag // body) * body
    turns = max(0, ((steady or total) - first) // body)

    def emit(v, c, inside):
        for lag, fn in stages:
            if inside or 0 <= c - lag < total:
                fn(U(v - lag, c - lag))

    if turns < 2:
        first, turns = total + maxlag, 0
    for v in range(first):
        emit(v, v, False)
    if turns:
        with eng.Fori(0, turns) as i:
            for k in range(body):
                emit(i * body + (first + k), first + k, True)
        for v in range(first + turns * body, total + maxlag):
            emit(v, v, False)


def build(nc, t, out):
    with ExitStack() as top:
        made = {}

        def own(name):
            made[name] = made.get(name, 0) + 1
            return name if made[name] == 1 else f"{name}_{made[name]}"

        def sb(name, shape, dt=F32, ctx=top):
            return ctx.enter_context(nc.sbuf_tensor(own(name), shape, dt))

        def bank(name, ctx):
            return ctx.enter_context(nc.psum_tensor(own(name), [P, 512], F32))

        def sem(name):
            return top.enter_context(nc.semaphore(name))

        def token(name):
            return Token(sem(name))

        A = sb("regionA", [P, NT * 264])
        B = sb("regionB", [P, NT * 265])
        C = sb("regionC", [P, NT * 264])

        def tiles(region, width, cols=None):
            return region[:, 0:NT * width].rearrange("p (t c) -> p t c", c=width)

        def part(region, at, shape):
            n = int(np.prod(shape))
            v = region[:, at:at + n]
            if len(shape) == 2:
                v = v.rearrange("p (a b) -> p a b", b=shape[1])
            elif len(shape) == 3:
                v = v.rearrange("p (a b c) -> p a b c", b=shape[1], c=shape[2])
            return v

        A256, B256, C256 = tiles(A, D), tiles(B, D), tiles(C, D)

        ident = sb("ident", [P, P])
        iota = sb("iota", [P, P])
        gidx = sb("gidx", [P, S], I32)
        rel = sb("rel", [P, S])
        wgt = sb("wgt", [P, S])
        ntab = sb("ntab", [1, SP_], I32)
        dstrow = sb("dstrow", [P, SB, P])
        eps = sb("eps", [P, 1])
        rstd = sb("rstd", [P, NT])
        nmr = sb("nmr", [P, NT])
        deg = sb("deg", [P, NT])
        zero_rows = sb("zero_rows", [P, 1, D])

        def dram(name, shape, dt=F32):
            return nc.dram_tensor(name, shape, dt).ap()

        T0, T1, T2, T3 = (dram(f"table{i}", [NP, D]) for i in range(4))
        T4 = dram("table4", [NP, WT])
        srcrow_d = dram("srcrow_d", [S, P])
        Eb = dram("edge_rows", [NG, P, GS * D])
        scat = dram("scatter_sums", [CHAINS * ND, D])

        s_in = Count(sem("s_in"))
        s_meta = sem("s_meta")
        s_tiles = sem("s_tiles")
        s_st = Count(sem("s_st"))
        s_back = Count(sem("s_back"))
        s_zero = Count(sem("s_zero"))
        link = {k: token(f"s_link_{k}") for k in ("v", "a", "p", "t")}
        src_full = [token(f"s_src_full{b}") for b in (0, 1)]
        src_free = [token(f"s_src_free{b}") for b in (0, 1)]
        tr_full = [token(f"s_tr_full{b}") for b in (0, 1)]
        lhs_full = [token(f"s_lhs_full{b}") for b in (0, 1)]
        mid_full = [token(f"s_mid_full{b}") for b in (0, 1)]
        act_full = [token(f"s_act_full{b}") for b in (0, 1)]
        res_full = [token(f"s_res_full{b}") for b in (0, 1)]
        res_free = [token(f"s_res_free{b}") for b in (0, 1)]
        hot_full = [token(f"s_hot_full{b}") for b in (0, 1)]
        hot_free = [token(f"s_hot_free{b}") for b in (0, 1)]
        idx_full = [token(f"s_idx_full{b}") for b in range(RING)]
        slot_free = [token(f"s_slot_free{b}") for b in range(RING)]
        slot_kept = [token(f"s_slot_kept{b}") for b in range(RING)]
        aux_full = [token(f"s_aux_full{b}") for b in (0, 1)]
        aux_free = [token(f"s_aux_free{b}") for b in (0, 1)]
        ping, pong, stats_done = token("s_ping"), token("s_pong"), token("s_stats")
        step_full = token("s_step_full")
        s_add = Count(sem("s_add"))
        s_load = [Count(sem(f"s_load{b}")) for b in (0, 1)]
        s_keep = [Count(sem(f"s_keep{b}")) for b in range(RING)]

        def op(ins, eng, k):
            ins.then_inc(link[k].sem, 1)
            link[k].take(eng)

        def ntile(eng, u, regs):
            eng.load(regs, ntab[0:1, bass.ds(u.val * GS, GS)])
            return [eng.snap(r, min_val=0, max_val=NT - 1) for r in regs]

        def at_tile(view, v):
            return view[:, bass.ds(v, 1), :].rearrange("p a c -> p (a c)")

        def load(sp, dst, src, **kw):
            sp.dma_start(dst, src, **kw).then_inc(s_in.sem, 16)
            s_in.base += 16

        def loaded(eng):
            eng.wait_ge(s_in.sem, s_in.base)

        def phase():
            return nc.Block()

        def zero_sums(a, chains):
            for k in chains:
                a.dma_start(scat[k * ND:(k + 1) * ND, :].rearrange("(p r) c -> p r c", p=P),
                            zero_rows[:, :, :].to_broadcast([P, ND // P, D])).then_inc(s_zero.sem, 16)
                s_zero.base += 16

        with ExitStack() as ctx:
            pss = [bank(f"ps_m{i}", ctx) for i in range(2)]
            keys_i = part(A, 0, [ET]).bitcast(I32)
            keys = part(A, 1000, [ET])
            lane = part(A, 2000, [ET])
            below = part(A, 3000, [ET])
            ers = sb("edge_rows_i", [P, SB, 3 * P], I32, ctx)
            srow = part(A, 4000, [SB, P])
            typ = part(A, 5000, [SB, P])
            wrow = part(A, 6000, [SB, P])
            rrow = part(A, 7000, [SB, P])
            tmp = part(A, 8000, [SB, P])
            alpha = part(A, 9000, [RELS])
            stepno = part(A, 9100, [SB])
            et = part(A, 9200, [SB])
            et_i = part(A, 9300, [SB]).bitcast(I32)
            ntf = part(A, 9400, [SB])
            shift = part(A, 9500, [SB])
            base_in = s_in.base
            with phase() as block:
                @block.sync
                def _(sp):
                    sp.dma_start(keys_i, t["dst_last"].rearrange("(a n) -> a n", a=1).partition_broadcast(P)
                                 .rearrange("q a n -> q (a n)")).then_inc(s_meta, 16)
                    sp.dma_start(alpha, t["L1_gnn_alpha"].rearrange("r a -> a r").partition_broadcast(P)
                                 .rearrange("q a n -> q (a n)"), allow_slow_non_contiguous=True).then_inc(s_meta, 16)
                    ping.take(sp)
                    sp.dma_start(B256[:, 0:NT - 1, :], t["x"][0:(NT - 1) * P, :].rearrange("(t p) c -> p t c", p=P))\
                        .then_inc(s_in.sem, 16)
                    sp.dma_start(B256[0:TAIL, NT - 1, :], t["x"][(NT - 1) * P:N, :]).then_inc(s_in.sem, 16)
                    pong.take(sp)
                    for c in range(SB):
                        n = min(P, S - c * P)
                        sp.dma_start(srcrow_d[c * P:c * P + n, :], srow[0:n, c, :]).then_inc(s_st.sem, 16)
                    s_st.base += 16 * SB
                    sp.wait_ge(s_st.sem, s_st.base)
                    sp.wait_ge(s_in.sem, base_in + 32)

                @block.gpsimd
                def _(g):
                    op(g.memset(ident[:, :], 0.0), g, "p")
                    g.iota(stepno, [[P, SB]], base=0, channel_multiplier=1,
                           allow_small_or_imprecise_dtypes=True)
                    g.iota(lane, [[1, ET]], base=0, channel_multiplier=0, allow_small_or_imprecise_dtypes=True)
                    g.iota(iota[:, :], [[1, P]], base=0, channel_multiplier=0, allow_small_or_imprecise_dtypes=True)
                    op(g.affine_select(out=ident[:, :], in_=ident[:, :], compare_op=ALU.not_equal, fill=1.0,
                                       base=0, pattern=[[-1, P]], channel_multiplier=1), g, "p")
                    hot_full[0].give(g)
                    idx_full[0].take(g)
                    top_edge = g.to_reg(ET - 1)
                    for c in range(SB):
                        g.indirect_dma_start(out=ers[:, c, :], out_offset=None, in_=t["edge_tiles"],
                                             in_offset=bass.IndirectOffsetOnAxis(ap=et_i[:, c:c + 1], axis=0),
                                             bounds_check=top_edge, oob_is_err=True).then_inc(s_tiles, 16)
                    g.wait_ge(s_tiles, 16 * SB)
                    hot_full[1].give(g)

                @block.vector
                def _(v):
                    op(v.memset(B256[:, NT - 1, :], 0.0), v, "v")
                    ping.give(v)
                    v.memset(zero_rows[:, :, :], 0.0)
                    v.memset(eps[:, :], LN_EPS)
                    v.wait_ge(s_meta, 32)
                    hot_full[0].take(v)
                    op(v.tensor_scalar(keys_i, keys_i, 7, None, ALU.logical_shift_right), v, "v")
                    op(v.tensor_copy(keys, keys_i), v, "v")
                    op(v.tensor_tensor(keys, keys, lane, ALU.add), v, "v")
                    for c in range(SB):
                        op(v.tensor_scalar(below, keys, stepno[:, c:c + 1], 0.0, ALU.is_lt, ALU.add,
                                           accum_out=et[:, c:c + 1]), v, "v")
                    op(v.tensor_tensor(ntf, stepno, et, ALU.subtract), v, "v")
                    op(v.tensor_scalar(ntf, ntf, float(NT - 1), None, ALU.min), v, "v")
                    op(v.tensor_scalar(et, et, float(ET - 1), None, ALU.min), v, "v")
                    op(v.tensor_copy(et_i, et), v, "v")
                    op(v.tensor_scalar(shift, ntf, float(P), None, ALU.mult), v, "v")
                    idx_full[0].give(v)
                    hot_full[1].take(v)
                    v.tensor_copy(dstrow[:, :, :], ers[:, :, 0:P])
                    v.tensor_copy(srow, ers[:, :, P:2 * P])
                    op(v.tensor_copy(typ, ers[:, :, 2 * P:3 * P]), v, "v")
                    pong.give(v)
                    op(v.memset(wrow, 0.0), v, "v")
                    for c in range(SB):
                        op(v.tensor_scalar(rrow[:, c, :], dstrow[:, c, :], shift[:, c:c + 1], None, ALU.subtract), v, "v")
                    for r in range(RELS):
                        op(v.tensor_scalar(tmp, typ, float(r), alpha[:, r:r + 1], ALU.is_equal, ALU.mult), v, "v")
                        op(v.tensor_tensor(wrow, wrow, tmp, ALU.add), v, "v")
                    src_full[0].give(v)
                    for c in range(SB):
                        n = min(P, S - c * P)
                        tr_full[0].take(v)
                        v.tensor_copy(rel[:, c * P:c * P + n], pss[0][:, 0:n])
                        v.tensor_copy(gidx[:, c * P:c * P + n], pss[0][:, P:P + n])
                        v.tensor_copy(wgt[:, c * P:c * P + n], pss[0][:, 2 * P:2 * P + n])
                        op(v.tensor_copy(ntab[0:1, c * P:(c + 1) * P], pss[0][0:1, 3 * P:4 * P]), v, "v")
                        res_free[0].give(v)

                @block.tensor
                def _(te):
                    src_full[0].take(te)
                    for c in range(SB):
                        if c:
                            res_free[0].take(te)
                        te.transpose(pss[0][:, 0:P], rrow[:, c, :], ident[:, :])
                        te.transpose(pss[0][:, P:2 * P], srow[:, c, :], ident[:, :])
                        te.transpose(pss[0][:, 2 * P:3 * P], wrow[:, c, :], ident[:, :])
                        te.transpose(pss[0][0:1, 3 * P:4 * P], ntf[:, c:c + 1], ident[:, :])\
                            .then_inc(tr_full[0].sem, 1)
                    res_free[0].take(te)
            s_in.base = base_in + 32

        def ln_stats(view):
            with ExitStack() as ctx:
                st = sb("ln_parts", [P, NT, 6], F32, ctx)
                with phase() as block:
                    @block.vector
                    def _(v):
                        def stats(u):
                            v.bn_stats(st[:, bass.ds(u.val, 1), :].rearrange("p a c -> p (a c)"), at_tile(view, u.val))
                        pipeline(v, NT, GT, [(0, stats)])
                        v.drain()
                        me, qe, mo, qo = (st[:, :, k] for k in (1, 2, 4, 5))
                        op(v.tensor_tensor(qe, qe, qo, ALU.add), v, "v")
                        op(v.tensor_tensor(qo, me, mo, ALU.subtract), v, "v")
                        op(v.tensor_tensor(me, me, mo, ALU.add), v, "v")
                        op(v.tensor_tensor(qo, qo, qo, ALU.mult), v, "v")
                        op(v.tensor_scalar(qo, qo, 0.25, None, ALU.mult), v, "v")
                        op(v.scalar_tensor_tensor(out=rstd[:, :], in0=qe, scalar=1.0 / D, in1=qo,
                                                  op0=ALU.mult, op1=ALU.add), v, "v")
                        ping.give(v)
                        pong.take(v)
                        op(v.reciprocal(rstd[:, :], rstd[:, :]), v, "v")
                        op(v.scalar_tensor_tensor(out=nmr[:, :], in0=me, scalar=-0.5, in1=rstd[:, :],
                                                  op0=ALU.mult, op1=ALU.mult), v, "v")

                    @block.scalar
                    def _(a):
                        ping.take(a)
                        a.activation(rstd[:, :], rstd[:, :], ACT.Sqrt, bias=eps[:, 0:1]).then_inc(pong.sem, 1)

        def dense_loop(nsrc, ncols, wload, pre, post, mid_bias=False, nrows=0, save=None,
                       beside=None, vector_stages=(), gpsimd=None, prepare=None):
            with ExitStack() as ctx:
                W = sb("weights", [P, max(2 * nsrc, 4 if mid_bias else 2), ncols], F32, ctx)
                rows = sb("bias_rows", [P, nrows, D], F32, ctx) if nrows else None
                mb = sb("mid_bias", [P, 2], F32, ctx) if mid_bias else None
                hs = sb("src_tile", [P, 2, nsrc, D], F32, ctx)
                hT = sb("src_tile_T", [P, 2, 2 * nsrc, P], F32, ctx)
                uT = sb("mid_T", [P, 2, 2, P], F32, ctx) if mid_bias else None
                psT = [bank(f"psT{b}", ctx) for b in (0, 1)]
                psO = [bank(f"psO{b}", ctx) for b in (0, 1)]
                psM = [bank(f"psM{b}", ctx) for b in (0, 1)]
                with phase() as block:
                    @block.sync
                    def _(sp):
                        wload(sp, W, rows, mb)
                        sp.wait_ge(s_in.sem, s_in.base)
                        src_full[0].give(sp)
                        aux_full[0].give(sp)
                        aux_full[1].give(sp)
                        if save:
                            for g in range(GT):
                                s_add.wait(sp, 2 + (g + 1) * GT)
                                for table, view in save:
                                    sp.dma_start(table[g * GT * P:(g + 1) * GT * P, :].rearrange("(t p) c -> p t c", p=P),
                                                 view[:, g * GT:(g + 1) * GT, :]).then_inc(s_st.sem, 16)
                                    s_st.base += 16
                            sp.wait_ge(s_st.sem, s_st.base)

                    @block.scalar
                    def _(a):
                        aux_full[1].take(a)
                        if beside:
                            beside(a)

                        def fill(u):
                            b = u.c % 2
                            src_free[b].take(a)
                            if prepare:
                                aux_free[0].take(a)
                            pre(a, u, hs[:, b]).then_inc(hot_full[b].sem, 1)

                        def copyT(u):
                            b = u.c % 2
                            tr_full[b].take(a)
                            a.activation(hT[:, b].rearrange("p k n -> p (k n)"), psT[b][:, 0:2 * nsrc * P], ACT.Copy)\
                                .then_inc(lhs_full[b].sem, 1)

                        def mid(u):
                            b = u.c % 2
                            mid_full[b].take(a)
                            for oc in (0, 1):
                                x = a.activation(uT[:, b, oc, :], psM[b][:, oc * P:(oc + 1) * P], ACT.Relu,
                                                 bias=mb[:, oc:oc + 1])
                            x.then_inc(act_full[b].sem, 1)
                        stages = [(0, fill), (1, copyT)] + ([(2, mid)] if uT is not None else [])
                        pipeline(a, NT, 8, stages)

                    @block.tensor
                    def _(te):
                        src_full[0].take(te)
                        for b in (0, 1):
                            src_free[b].give(te)

                        def trans(u):
                            b = u.c % 2
                            hot_full[b].take(te)
                            for k in range(2 * nsrc):
                                x = te.transpose(psT[b][:, k * P:(k + 1) * P],
                                                 hs[:, b, k // 2, (k % 2) * P:(k % 2 + 1) * P], ident[:, :])
                            x.then_inc(tr_full[b].sem, 1)

                        def midmm(u):
                            b = u.c % 2
                            lhs_full[b].take(te)
                            src_free[b].give(te)
                            for oc in (0, 1):
                                for k in (0, 1):
                                    x = te.matmul(psM[b][:, oc * P:(oc + 1) * P], W[:, 2 + k, oc * P:(oc + 1) * P],
                                                  hT[:, b, k, :], start=k == 0, stop=k == 1)
                            x.then_inc(mid_full[b].sem, 1)

                        def mm(u):
                            b = u.c % 2
                            if uT is None:
                                lhs_full[b].take(te)
                                src_free[b].give(te)
                                lhs = hT
                            else:
                                act_full[b].take(te)
                                lhs = uT
                            s_add.wait(te, u.val + 1)
                            for k in range(2 * nsrc):
                                x = te.matmul(psO[b][:, 0:ncols], lhs[:, b, k, :], W[:, k, 0:ncols],
                                              start=k == 0, stop=k == 2 * nsrc - 1)
                            x.then_inc(res_full[b].sem, 1)
                        pipeline(te, NT, 8, [(0, trans), (1, mm)] if uT is None else [(0, trans), (1, midmm), (2, mm)])
                        for b in (0, 1):
                            src_free[b].take(te)

                    @block.vector
                    def _(v):
                        aux_full[0].take(v)
                        v.sem_inc(s_add.sem, 2)

                        def use(u):
                            b = u.c % 2
                            res_full[b].take(v)
                            post(v, u, psO[b], rows).then_inc(s_add.sem, 1)

                        def first(u):
                            prepare[0](v, u).then_inc(aux_free[1].sem, 1)

                        def second(u):
                            aux_free[1].take(v)
                            prepare[1](v, u).then_inc(aux_free[0].sem, 1)
                        stages = [(1, second), (0, first), (6, use)] if prepare else [(0, use)]
                        pipeline(v, NT, 8, stages + [(lag, lambda u, fn=fn: fn(v, u, rows)) for lag, fn in vector_stages])

                    if gpsimd:
                        @block.gpsimd
                        def _(g):
                            gpsimd(g, rows)
                s_add.base += NT + 2

        def ln_pre(view, keep=None):
            def pre(a, u, hs):
                scale, bias = rstd[:, bass.ds(u.val, 1)], nmr[:, bass.ds(u.val, 1)]
                if keep is not None:
                    a.activation(at_tile(keep, u.val), at_tile(view, u.val), ACT.Relu, bias=bias, scale=scale)
                return a.activation(hs[:, 0, :], at_tile(view, u.val), ACT.Relu, bias=bias, scale=scale)
            return pre

        def bcast_row(ap):
            return ap.rearrange("(a n) -> a n", a=1).partition_broadcast(P).rearrange("q a n -> q (a n)")

        def kchunks(w):
            return w.rearrange("(k p) n -> p k n", p=P)

        def segment_softmax(LG, logits, heads, room, last=None, peak=None, beside=None):
            H = 4
            RL, FW, BW = (part(room[0], k * 3584, [H, SB, P]) for k in range(3))
            fd, bd, first, final = (part(room[1], k * SB * P, [SB, P]) for k in range(4))
            tmp = part(room[1], 4 * SB * P, [SB, P])
            ends = part(room[1], 4500, [SB, 4, H])
            lastrow = part(room[1], 4700, [SB, P])
            TR = part(room[1], 5600, [4, SP_])[0:H]
            RT = part(room[1], 9200, [4, SP_])[0:H]
            with ExitStack() as ctx:
                carry = sb("carry", [P, SB, 3, H], F32, ctx)
                ps = [bank(f"ps_s{b}", ctx) for b in (0, 1)]
                for h0 in range(0, heads, H):
                    mine = logits[:, :, h0:h0 + H]
                    with phase() as block:
                        @block.tensor
                        def _(te):
                            for c in range(SB):
                                b = c % 2
                                res_free[b].take(te)
                                for h in range(H):
                                    x = te.transpose(ps[b][:, h * P:(h + 1) * P], mine[:, c * P:(c + 1) * P, h],
                                                     ident[:, :])
                                x.then_inc(res_full[b].sem, 1)
                            hot_full[0].take(te)
                            for c in range(SB):
                                b = c % 2
                                res_free[b].take(te)
                                for k in range(4):
                                    x = te.transpose(ps[b][0:H, k * P:(k + 1) * P], ends[:, c, k, :], ident[:, :])
                                x.then_inc(res_full[b].sem, 1)
                            hot_full[1].take(te)
                            for c in range(SB):
                                b = c % 2
                                res_free[b].take(te)
                                for k in range(3):
                                    x = te.transpose(ps[b][:, k * H:(k + 1) * H], RT[:, k, c * P:(c + 1) * P],
                                                     ident[0:H, 0:H])
                                x.then_inc(res_full[b].sem, 1)
                            hot_full[0].take(te)
                            for c in range(SB):
                                b = c % 2
                                res_free[b].take(te)
                                for h in range(H):
                                    x = te.transpose(ps[b][:, h * P:(h + 1) * P], RL[:, h, c, :], ident[:, :])
                                x.then_inc(res_full[b].sem, 1)
                            if last is not None:
                                for c in range(SB):
                                    b = (c + SB) % 2
                                    res_free[b].take(te)
                                    te.transpose(ps[b][:, 0:P], lastrow[:, c, :], ident[:, :])\
                                        .then_inc(res_full[b].sem, 1)

                        @block.vector
                        def _(v):
                            for b in (0, 1):
                                res_free[b].give(v)
                            d = dstrow
                            v.memset(fd[:, :, 0:1], -BIG)
                            v.memset(bd[:, :, P - 1:P], -BIG)
                            op(v.tensor_tensor(tmp[:, :, 1:P], d[:, :, 1:P], d[:, :, 0:P - 1], ALU.not_equal), v, "v")
                            v.tensor_scalar(fd[:, :, 1:P], tmp[:, :, 1:P], -BIG, None, ALU.mult)
                            v.tensor_scalar(bd[:, :, 0:P - 1], tmp[:, :, 1:P], -BIG, None, ALU.mult)
                            op(v.tensor_copy(lastrow[:, :, 0:P - 1], tmp[:, :, 1:P]), v, "v")
                            for mask, end in ((first, 0), (final, P - 1)):
                                op(v.tensor_tensor(mask, d[:, :, :], d[:, :, end:end + 1].to_broadcast([P, SB, P]),
                                                   ALU.not_equal), v, "v")
                                op(v.tensor_scalar(mask, mask, -BIG, None, ALU.mult), v, "v")
                            for c in range(SB):
                                b = c % 2
                                res_full[b].take(v)
                                op(v.tensor_copy(RL[:, :, c, :], ps[b][:, 0:512].rearrange("p (h e) -> p h e", e=P)), v, "v")
                                res_free[b].give(v)
                            flat = lambda x: x.rearrange("p c e -> p (c e)")
                            for h in range(H):
                                v.tensor_tensor_scan(flat(FW[:, h]), flat(fd), flat(RL[:, h]), -BIG, ALU.add, ALU.max)
                                op(v.tensor_tensor_scan(flat(BW[:, h])[:, ::-1], flat(bd)[:, ::-1], flat(RL[:, h])[:, ::-1],
                                                        -BIG, ALU.add, ALU.max), v, "v")
                            for h in range(H):
                                v.tensor_copy(ends[:, :, 0, h:h + 1], FW[:, h, :, P - 1:P])
                                v.tensor_copy(ends[:, :, 1, h:h + 1], BW[:, h, :, 0:1])
                                v.tensor_copy(ends[:, :, 2, h:h + 1], d[:, :, 0:1])
                                op(v.tensor_copy(ends[:, :, 3, h:h + 1], d[:, :, P - 1:P]), v, "v")
                            hot_full[0].give(v)
                            for c in range(SB):
                                b = c % 2
                                res_full[b].take(v)
                                op(v.tensor_copy(TR[:, :, c * P:(c + 1) * P],
                                                 ps[b][0:H, 0:512].rearrange("p (k s) -> p k s", s=P)), v, "v")
                                res_free[b].give(v)
                            fend, bst, d0, d1 = (TR[:, k, :] for k in range(4))
                            cf, cb, cont = (RT[:, k, :] for k in range(3))
                            op(v.memset(cont, 0.0), v, "v")
                            op(v.tensor_tensor(cont[:, 0:SP_ - 1], d0[:, 1:SP_], d1[:, 0:SP_ - 1], ALU.is_equal), v, "v")
                            op(v.tensor_tensor(d0, d0, d1, ALU.is_equal), v, "v")
                            op(v.memset(d1[:, 0:1], 0.0), v, "v")
                            op(v.tensor_tensor(d1[:, 1:SP_], d0[:, 1:SP_], cont[:, 0:SP_ - 1], ALU.mult), v, "v")
                            op(v.tensor_scalar(d1, d1, -1.0, BIG, ALU.add, ALU.mult), v, "v")
                            op(v.tensor_tensor_scan(fend, d1, fend, -BIG, ALU.add, ALU.max), v, "v")
                            op(v.tensor_tensor(d1, d0, cont, ALU.mult), v, "v")
                            op(v.tensor_scalar(d1, d1, -1.0, BIG, ALU.add, ALU.mult), v, "v")
                            op(v.tensor_tensor_scan(bst[:, ::-1], d1[:, ::-1], bst[:, ::-1], -BIG, ALU.add, ALU.max), v, "v")
                            op(v.tensor_scalar(d1, cont, -1.0, BIG, ALU.add, ALU.mult), v, "v")
                            v.memset(cf[:, 0:1], -BIG)
                            v.memset(cb[:, SP_ - 1:SP_], -BIG)
                            op(v.tensor_tensor(cf[:, 1:SP_], fend[:, 0:SP_ - 1], d1[:, 0:SP_ - 1], ALU.add), v, "v")
                            op(v.tensor_tensor(cb[:, 0:SP_ - 1], bst[:, 1:SP_], d1[:, 0:SP_ - 1], ALU.add), v, "v")
                            hot_full[1].give(v)
                            for c in range(SB):
                                b = c % 2
                                res_full[b].take(v)
                                op(v.tensor_copy(carry[:, c, :, :], ps[b][:, 0:3 * H].rearrange("p (k h) -> p k h", h=H)), v, "v")
                                res_free[b].give(v)
                            for h in range(H):
                                op(v.tensor_tensor(RL[:, h], FW[:, h], BW[:, h], ALU.max), v, "v")
                                for k, mask in ((0, first), (1, final)):
                                    op(v.tensor_tensor(tmp, mask, carry[:, :, k, h:h + 1].to_broadcast([P, SB, P]),
                                                       ALU.add), v, "v")
                                    op(v.tensor_tensor(RL[:, h], RL[:, h], tmp, ALU.max), v, "v")
                            op(v.tensor_scalar(lastrow[:, :, P - 1:P], carry[:, :, 2, 0:1], -1.0, 1.0, ALU.mult, ALU.add), v, "v")
                            hot_full[0].give(v)
                            MX = part(room[0], 3584, [SB, P, H])
                            for c in range(SB):
                                b = c % 2
                                res_full[b].take(v)
                                op(v.tensor_copy(MX[:, c], ps[b][:, 0:512].rearrange("p (h s) -> p s h", s=P)), v, "v")
                                res_free[b].give(v)
                            mx = MX.rearrange("p c s h -> p (c s) h")
                            if last is not None:
                                for c in range(SB):
                                    b = (c + SB) % 2
                                    res_full[b].take(v)
                                    op(v.tensor_copy(last[:, c * P:(c + 1) * P], ps[b][:, 0:P]), v, "v")
                                    res_free[b].give(v)
                                v.tensor_tensor(peak[:, :, :], mx, last[:, :].unsqueeze(2).to_broadcast([P, SP_, H]), ALU.mult)
                            op(v.tensor_tensor(mine, mine, mx, ALU.subtract), v, "v")
                            ping.give(v)
                            for b in (0, 1):
                                res_free[b].take(v)

                        @block.scalar
                        def _(a):
                            if beside:
                                beside(a)
                            ping.take(a)
                            op(a.activation(mine, mine, ACT.Exp), a, "a")


        def one_hot(v, hot, j, s, weighted):
            if weighted:
                return v.tensor_scalar(hot[:, j, :], iota[:, :], rel[:, bass.ds(s, 1)], wgt[:, bass.ds(s, 1)],
                                       ALU.is_equal, ALU.mult)
            return v.tensor_scalar(hot[:, j, :], iota[:, :], rel[:, bass.ds(s, 1)], None, ALU.is_equal)

        def rows_count(name, n=2):
            return [Count(sem(f"s_rows_{name}{b}")) for b in range(n)]

        def add_steps(v, u, regs, acc, ps, width, nbank):
            nt = ntile(v, u, regs)
            for j in range(GS):
                add_step(v, u, j, nt[j], acc, ps, width, nbank)

        def add_step(v, u, j, nt, acc, ps, width, nbank):
            step_full.take(v)
            s_add.wait(v, u.val * GS + (j + nbank))
            dst_ = at_tile(acc, nt)
            v.tensor_tensor(dst_, dst_, ps[(u.c * GS + j) % nbank][:, 0:width], ALU.add).then_inc(s_add.sem, 1)

        def zero_acc(v, acc_flat, nbank):
            op(v.memset(acc_flat, 0.0), v, "v")
            s_add_start(v, nbank)

        def s_add_start(v, nbank):
            v.sem_inc(s_add.sem, nbank)

        def copy_idx(a, idx, u, b):
            return a.activation(idx[:, b, :], gidx[:, bass.ds(u.val * GS, GS)], ACT.Copy)

        def plain_pass(name, table, acc, acc_flat, width, weighted, fold=None, own=None):
            NB = 4
            s_rows = rows_count(name)
            with ExitStack() as ctx:
                G = sb("rows_in", [P, 2, GS, width], F32, ctx)
                hot = sb("hot", [P, 2, GS, P], F32, ctx)
                idx = sb("idx", [P, 2, GS], I32, ctx)
                ps = [bank(f"ps_p{i}", ctx) for i in range(NB)]
                if fold:
                    parts = part(fold[1], 0, [2, CHAINS + 1, D])
                    total = part(fold[1], 2 * (CHAINS + 1) * D, [D])
                if own:
                    W = sb("own_weights", [P, 2, D], F32, ctx)
                    ownb = sb("own_bias", [P, D], F32, ctx)
                    h_tile = sb("own_tile", [P, D], F32, ctx)
                    hT = sb("own_T", [P, 2, P], F32, ctx)
                    psH = bank("ps_own_T", ctx)
                    psW = bank("ps_own", ctx)

                def beside(u):
                    return u.c % 2 == 0 and (not isinstance(u.val, int) or u.val // 2 < NT)
                with phase() as block:
                    if fold:
                        @block.sync
                        def _(sp):
                            for b in (0, 1):
                                load(sp, parts[:, b, CHAINS, :], bcast_row(fold[0]))
                            loaded(sp)
                            aux_full[0].give(sp)

                            def sums_in(u):
                                b = u.c % 2
                                src_free[b].take(sp)
                                sp.dma_start(parts[:, b, 0:CHAINS, :], scat.rearrange("(k n) c -> n k c", k=CHAINS)
                                             [bass.ds(u.val * P, P), :, :]).then_inc(s_load[b].sem, 16)
                            pipeline(sp, NT, 2, [(0, sums_in)])
                    if own:
                        @block.sync
                        def _(sp):
                            load(sp, W[:, :, :], kchunks(t[own[1]]))
                            load(sp, ownb[:, :], bcast_row(t[own[2]]))
                            loaded(sp)
                            aux_full[0].give(sp)
                            aux_full[1].give(sp)

                    @block.scalar
                    def _(a):
                        def index(u):
                            b = u.c % 2
                            slot_free[b].take(a)
                            copy_idx(a, idx, u, b).then_inc(idx_full[b].sem, 1)

                        def own_fill(u):
                            if beside(u):
                                a.activation(h_tile[:, :], at_tile(own[0], u.val // 2), ACT.Copy).then_inc(mid_full[0].sem, 1)

                        def own_copyT(u):
                            if beside(u):
                                tr_full[0].take(a)
                                a.activation(hT[:, :, :].rearrange("p k n -> p (k n)"), psH[:, 0:2 * P], ACT.Copy)\
                                    .then_inc(lhs_full[0].sem, 1)
                        if own:
                            pipeline(a, NG, 2, [(0, index), (0, own_fill), (1, own_copyT)], steady=2 * (NT - 1))
                        else:
                            pipeline(a, NG, 2, [(0, index)])

                    @block.gpsimd
                    def _(g):
                        top_row = g.to_reg(NP - 1)

                        def fetch(u):
                            b = u.c % 2
                            idx_full[b].take(g)
                            for j in range(GS):
                                g.indirect_dma_start(out=G[:, b, j, 0:D], out_offset=None, in_=table,
                                                     in_offset=bass.IndirectOffsetOnAxis(ap=idx[:, b, j:j + 1], axis=0),
                                                     bounds_check=top_row, oob_is_err=True).then_inc(s_rows[b].sem, 16)
                        pipeline(g, NG, 2, [(0, fetch)])

                    @block.tensor
                    def _(te):
                        def multiply(u):
                            b, turn = u.c % 2, u.c // 2
                            hot_full[b].take(te)
                            s_rows[b].wait(te, (u.val - b) * (16 * GS // 2) + 16 * GS)
                            for j in range(GS):
                                s_add.wait(te, u.val * GS + (j + 1))
                                te.matmul(ps[(u.c * GS + j) % NB][:, 0:width], hot[:, b, j, :], G[:, b, j, :],
                                          start=True, stop=True).then_inc(step_full.sem, 1)

                        def own_trans(u):
                            if beside(u):
                                mid_full[0].take(te)
                                for k in (0, 1):
                                    x = te.transpose(psH[:, k * P:(k + 1) * P], h_tile[:, k * P:(k + 1) * P], ident[:, :])
                                x.then_inc(tr_full[0].sem, 1)

                        def own_mm(u):
                            if beside(u):
                                lhs_full[0].take(te)
                                for k in (0, 1):
                                    x = te.matmul(psW[:, 0:D], hT[:, k, :], W[:, k, :], start=k == 0, stop=k == 1)
                                x.then_inc(res_full[0].sem, 1)
                        if own:
                            aux_full[1].take(te)
                            pipeline(te, NG, 2, [(0, own_trans), (0, multiply), (0, own_mm)], steady=2 * (NT - 1))
                        else:
                            pipeline(te, NG, 2, [(0, multiply)])

                    @block.vector
                    def _(v):
                        regs = [v.alloc_register(f"nt_{name}{j}") for j in range(GS)]
                        if width > D:
                            op(v.memset(G[:, :, :, D:width], 1.0), v, "v")
                        for b in (0, 1):
                            slot_free[b].give(v)
                        if fold:
                            aux_full[0].take(v)
                            s_add_start(v, NB)
                        else:
                            zero_acc(v, acc_flat, NB)

                        def hots(u):
                            b = u.c % 2
                            for j in range(GS):
                                x = one_hot(v, hot[:, b], j, u.val * GS + j, weighted)
                            x.then_inc(hot_full[b].sem, 1)

                        def adds(u):
                            add_steps(v, u, regs, acc, ps, width, NB)
                            slot_free[u.c % 2].give(v)

                        def own_out(u):
                            if beside(u):
                                res_full[0].take(v)
                                v.tensor_tensor(at_tile(own[0], u.val // 2), psW[:, 0:D], ownb[:, :], ALU.add)

                        def fold_sum(u):
                            b = u.c // 2 % 2
                            if beside(u):
                                s_load[b].wait(v, u.val // 4 * 16 + 16)
                                v.tensor_reduce(total, parts[:, b].rearrange("p k c -> p c k"), AX.X, ALU.add)\
                                    .then_inc(link["v"].sem, 1)

                        def fold_add(u):
                            if beside(u):
                                link["v"].take(v)
                                src_free[u.c // 2 % 2].give(v)
                                s_add.wait(v, u.val * GS + NB)
                                x = at_tile(acc, u.val // 2)
                                op(v.tensor_tensor(x, x, total, ALU.add), v, "v")
                        if fold:
                            for b in (0, 1):
                                src_free[b].give(v)
                            pipeline(v, NG, 4, [(0, hots), (0, fold_sum), (1, adds), (0, fold_add)], steady=2 * (NT - 1))
                            for b in (0, 1):
                                src_free[b].take(v)
                        elif own:
                            aux_full[0].take(v)
                            pipeline(v, NG, 2, [(0, hots), (1, adds), (1, own_out)], steady=2 * (NT - 1))
                        else:
                            pipeline(v, NG, 2, [(0, hots), (1, adds)])
                        for b in (0, 1):
                            slot_free[b].take(v)
            s_add.base += S + NB
            if fold:
                for b in (0, 1):
                    s_load[b].base += 16 * len(range(b, NT, 2))

        def attention_fetch0(LG, attc, room):
            PAIRS = S // 2
            G = part(room, 0, [RING, GS * D])
            s_rows = rows_count("att0_", RING)
            with ExitStack() as ctx:
                hot = sb("hot", [P, 2, 2, P], F32, ctx)
                hotT = sb("hotT", [P, 2, 2, P], F32, ctx)
                feat = sb("feat", [P, 2, 2 * D], F32, ctx)
                featT = sb("featT", [P, 2, 4, P], F32, ctx)
                idx = sb("idx", [P, RING, GS], I32, ctx)
                psT = [bank(f"psT{b}", ctx) for b in (0, 1)]
                psX = [bank(f"psX{b}", ctx) for b in (0, 1)]
                psF = [bank(f"psF{b}", ctx) for b in (0, 1)]
                psL = [bank(f"psL{b}", ctx) for b in (0, 1)]
                QP = GS // 2
                with phase() as block:
                    @block.sync
                    def _(sp):
                        def keep(u):
                            b = u.c % RING
                            s_rows[b].wait(sp, (u.val - b) * (16 * GS // RING) + 16 * GS)
                            sp.dma_start(Eb[bass.ds(u.val, 1), :, :].rearrange("a p c -> p (a c)"),
                                         G[:, b, :]).then_inc(s_keep[b].sem, 16)
                            s_keep[b].wait(sp, (u.val - b) * (16 // RING) + 16)
                            slot_kept[b].give(sp)
                        for b in range(RING):
                            slot_kept[b].give(sp)
                        ping.take(sp)
                        for h in range(HEADS0):
                            load(sp, attc[h % 2 * 64:h % 2 * 64 + 64, h // 2, h:h + 1],
                                 t["L0_gnn_att"][h:h + 1, :].rearrange("a c -> c a"), allow_slow_non_contiguous=True)
                        loaded(sp)
                        pong.give(sp)
                        pipeline(sp, NG, RING, [(0, keep)])
                        for b in range(RING):
                            slot_kept[b].take(sp)

                    @block.gpsimd
                    def _(g):
                        top_row = g.to_reg(NP - 1)

                        def fetch(u):
                            b = u.c % RING
                            idx_full[b].take(g)
                            for j in range(GS):
                                g.indirect_dma_start(out=G[:, b, j * D:(j + 1) * D], out_offset=None, in_=T0,
                                                     in_offset=bass.IndirectOffsetOnAxis(ap=idx[:, b, j:j + 1], axis=0),
                                                     bounds_check=top_row, oob_is_err=True).then_inc(s_rows[b].sem, 16)
                        pipeline(g, NG, RING, [(0, fetch)])

                    @block.scalar
                    def _(a):
                        def index(u):
                            if u.c % QP:
                                return
                            b = u.c // QP % RING
                            slot_free[b].take(a)
                            slot_kept[b].take(a)
                            a.activation(idx[:, b, :], gidx[:, bass.ds(u.val * 2, GS)], ACT.Copy)\
                                .then_inc(idx_full[b].sem, 1)

                        def copyT(u):
                            b = u.c % 2
                            tr_full[b].take(a)
                            hot_free[b].give(a)
                            a.activation(hotT[:, b].rearrange("p k n -> p (k n)"), psT[b][:, 0:2 * P], ACT.Copy)\
                                .then_inc(lhs_full[b].sem, 1)


                        def copyF(u):
                            b = u.c % 2
                            mid_full[b].take(a)
                            a.activation(featT[:, b].rearrange("p k n -> p (k n)"), psF[b][:, :], ACT.Copy)\
                                .then_inc(act_full[b].sem, 1)
                        pipeline(a, PAIRS, RING * QP, [(6, copyT), (9, copyF), (0, index)])

                    @block.tensor
                    def _(te):
                        regs = [te.alloc_register(f"nt_att0{j}") for j in range(GS)]

                        def trans(u):
                            b = u.c % 2
                            hot_full[b].take(te)
                            for k in (0, 1):
                                x = te.transpose(psT[b][:, k * P:(k + 1) * P], hot[:, b, k, :], ident[:, :])
                            x.then_inc(tr_full[b].sem, 1)

                        def fetch_xr(u):
                            b = u.c % 2
                            q = u.c % QP * 2
                            nt = [te.snap(r, min_val=0, max_val=NT - 1) for r in regs[q:q + 2]]
                            lhs_full[b].take(te)
                            for k in (0, 1):
                                x = te.matmul(psX[b][:, k * D:(k + 1) * D], hotT[:, b, k, :], at_tile(A256, nt[k]),
                                              start=True, stop=True)
                            x.then_inc(res_full[b].sem, 1)

                        def load_nt(u):
                            if u.c % QP == 0:
                                te.load(regs, ntab[0:1, bass.ds(u.val * 2, GS)])

                        def transF(u):
                            b = u.c % 2
                            src_full[b].take(te)
                            for k in range(4):
                                x = te.transpose(psF[b][:, k * P:(k + 1) * P], feat[:, b, k * P:(k + 1) * P], ident[:, :])
                            x.then_inc(mid_full[b].sem, 1)

                        def logit(u):
                            b, gb = u.c % 2, u.c // QP % 2
                            act_full[b].take(te)
                            if u.c % QP == 0:
                                aux_free[gb].take(te)
                            for k in (0, 1):
                                col = (u.c % QP * 2 + k) * HEADS0
                                for c in (0, 1):
                                    x = te.matmul(psL[gb][:, col:col + HEADS0], featT[:, b, 2 * k + c, :], attc[:, c, :],
                                                  start=c == 0, stop=c == 1)
                            if u.c % QP == QP - 1:
                                x.then_inc(aux_full[gb].sem, 1)
                        pong.take(te)
                        pipeline(te, PAIRS, RING * QP, [(1, trans), (6, logit), (4, transF), (2, load_nt), (2, fetch_xr)])

                    @block.vector
                    def _(v):
                        for b in range(RING):
                            slot_free[b].give(v)
                        op(v.memset(attc[:, :, :], 0.0), v, "v")
                        ping.give(v)
                        op(v.memset(LG[:, :, :], 0.0), v, "v")
                        for b in (0, 1):
                            aux_free[b].give(v)
                            hot_free[b].give(v)

                        def hots(u):
                            b = u.c % 2
                            hot_free[b].take(v)
                            for k in (0, 1):
                                x = one_hot(v, hot[:, b], k, u.val * 2 + k, False)
                            x.then_inc(hot_full[b].sem, 1)

                        def feats(u):
                            b, gb = u.c % 2, u.c // QP % RING
                            if u.c % QP == 0:
                                s_rows[gb].wait(v, (u.val - (u.c % (RING * QP))) * (16 * GS // (RING * QP)) + 16 * GS)
                            res_full[b].take(v)
                            v.tensor_tensor(feat[:, b, :], G[:, gb, u.c % QP * 2 * D:(u.c % QP + 1) * 2 * D],
                                            psX[b][:, :], ALU.add).then_inc(link["v"].sem, 1)

                        def leak(u):
                            b = u.c % 2
                            link["v"].take(v)
                            if u.c % QP == QP - 1:
                                slot_free[u.c // QP % RING].give(v)
                            v.scalar_tensor_tensor(out=feat[:, b, :], in0=feat[:, b, :], scalar=0.2, in1=feat[:, b, :],
                                                   op0=ALU.mult, op1=ALU.max).then_inc(src_full[b].sem, 1)

                        def logits_out(u):
                            gb = u.c // QP % 2
                            if u.c % QP != QP - 1:
                                return
                            aux_full[gb].take(v)
                            v.tensor_copy(LG[:, bass.ds((u.val - (QP - 1)) * 2, GS), :],
                                          psL[gb][:, 0:GS * HEADS0].rearrange("p (s h) -> p s h", h=HEADS0))\
                                .then_inc(aux_free[gb].sem, 1)
                        pipeline(v, PAIRS, RING * QP, [(3, feats), (0, hots), (3, leak), (7, logits_out)])
                        for b in range(RING):
                            slot_free[b].take(v)
                        for b in (0, 1):
                            aux_free[b].take(v)
                            hot_free[b].take(v)
            for b in range(RING):
                s_keep[b].base += 16 * NG // RING

        def attention_sum(name, LG, heads, head_major, extras, acc, acc_flat, room):
            NB = 4
            width = D + heads + sum(k for _, k in extras)
            GL = part(room, 0, [2, GS, D])
            Gs = part(room, 2 * GS * D, [2 * GS, width])
            hot = part(room, 2 * GS * (D + width), [2 * GS, P])
            with ExitStack() as ctx:
                ps = [bank(f"ps_p{i}", ctx) for i in range(NB)]
                with phase() as block:
                    @block.sync
                    def _(sp):
                        def back(u):
                            b = u.c % 2
                            src_free[b].take(sp)
                            sp.dma_start(GL[:, b].rearrange("p s c -> p (s c)"),
                                         Eb[bass.ds(u.val, 1), :, :].rearrange("a p c -> p (a c)"))\
                                .then_inc(s_load[b].sem, 16)
                        pipeline(sp, NG, 2, [(0, back)])

                    @block.gpsimd
                    def _(g):
                        for b in (0, 1):
                            src_free[b].give(g)

                        def scale(u):
                            b = u.c % 2
                            s_load[b].wait(g, (u.val - b) * 8 + 16)
                            slot_free[b].take(g)
                            w = LG[:, bass.ds(u.val * GS, GS), :]
                            out_ = Gs[:, b * GS:(b + 1) * GS, 0:D]
                            if head_major:
                                o = out_.rearrange("p s (h c) -> p s h c", h=heads)
                                i = GL[:, b].rearrange("p s (h c) -> p s h c", h=heads)
                                w = w.unsqueeze(3).to_broadcast([P, GS, heads, D // heads])
                            else:
                                o = out_.rearrange("p s (c h) -> p s c h", h=heads)
                                i = GL[:, b].rearrange("p s (c h) -> p s c h", h=heads)
                                w = w.unsqueeze(2).to_broadcast([P, GS, D // heads, heads])
                            op(g.tensor_tensor(o, i, w, ALU.mult), g, "p")
                            aux_full[b].give(g)
                            src_free[b].give(g)
                        pipeline(g, NG, 2, [(0, scale)])
                        for b in (0, 1):
                            src_free[b].take(g)

                    @block.scalar
                    def _(a):
                        def more(u):
                            b = u.c % 2
                            slot_kept[b].take(a)
                            at = D
                            for table, k in [(LG, heads)] + extras:
                                x = a.activation(Gs[:, b * GS:(b + 1) * GS, at:at + k],
                                                 table[:, bass.ds(u.val * GS, GS), :], ACT.Copy)
                                at += k
                            x.then_inc(lhs_full[b].sem, 1)
                        pipeline(a, NG, 2, [(0, more)])

                    @block.tensor
                    def _(te):
                        def multiply(u):
                            b = u.c % 2
                            aux_full[b].take(te)
                            lhs_full[b].take(te)
                            for j in range(GS):
                                if j % (GS // 2) == 0:
                                    hot_full[b].take(te)
                                s_add.wait(te, u.val * GS + (j + 1))
                                te.matmul(ps[(u.c * GS + j) % NB][:, 0:width], hot[:, b * GS + j, :],
                                          Gs[:, b * GS + j, :], start=True, stop=True).then_inc(step_full.sem, 1)
                        pipeline(te, NG, 2, [(0, multiply)])

                    @block.vector
                    def _(v):
                        regs = [v.alloc_register(f"nt_{name}{j}") for j in range(GS)]
                        for b in (0, 1):
                            slot_free[b].give(v)
                            slot_kept[b].give(v)
                        zero_acc(v, acc_flat, NB)

                        def hot_step(u, j):
                            b = u.c % 2
                            x = one_hot(v, hot[:, b * GS:(b + 1) * GS], j, u.val * GS + j, False)
                            if (j + 1) % (GS // 2) == 0:
                                x.then_inc(hot_full[b].sem, 1)

                        def turn(u):
                            nt = ntile(v, u, regs)
                            for j in range(GS):
                                if not isinstance(u.val, int) or u.val + 1 < NG:
                                    hot_step(U(u.val + 1, u.c + 1), j)
                                add_step(v, u, j, nt[j], acc, ps, width, NB)
                            slot_free[u.c % 2].give(v)
                            slot_kept[u.c % 2].give(v)
                        for j in range(GS):
                            hot_step(U(0, 0), j)
                        pipeline(v, NG, 2, [(0, turn)], steady=NG - 2)
                        for b in (0, 1):
                            slot_free[b].take(v)
                            slot_kept[b].take(v)
            s_add.base += S + NB
            for b in (0, 1):
                s_load[b].base += 16 * NG // 2

        def grp(view, u, n=GT):
            return view[:, bass.ds(u.val * n, n), :]

        def column_norm(Y, gamma, beta, finish, scale_, gb, beside=None):
            with ExitStack() as ctx:
                ones = sb("ones", [P, 2, P], F32, ctx)
                sq = sb("squares", [P, 2, GT, D], F32, ctx)
                mean = scale_
                psS = bank("ps_sum", ctx)
                psQ = bank("ps_sq", ctx)
                with phase() as block:
                    @block.sync
                    def _(sp):
                        load(sp, gb[:, 0, :], bcast_row(gamma))
                        load(sp, gb[:, 1, :], bcast_row(beta))
                        if beside:
                            beside(sp)
                        sp.wait_ge(s_in.sem, s_in.base)
                        aux_full[0].give(sp)

                    @block.gpsimd
                    def _(g):
                        op(g.memset(ones[:, 0, :], 1.0), g, "p")
                        op(g.affine_select(out=ones[:, 1, :], in_=ones[:, 0, :], compare_op=ALU.is_ge, fill=0.0,
                                           base=TAIL - 1, pattern=[[0, P]], channel_multiplier=-1), g, "p")
                        hot_full[0].give(g)

                    def sums(te, rhs_of, ps, before=None):
                        def one(u):
                            if before:
                                before(u)
                            last_ = isinstance(u.val, int) and u.val == NT - 1
                            x = te.matmul(ps[:, 0:D], ones[:, 1 if last_ else 0, :], rhs_of(u),
                                          start=isinstance(u.val, int) and u.val == 0, stop=last_)
                            return x
                        return one

                    @block.tensor
                    def _(te):
                        hot_full[0].take(te)
                        one = sums(te, lambda u: at_tile(Y, u.val), psS)
                        one(U(0, 0))
                        with te.Fori(1, NT - 1) as i:
                            one(U(i, 1))
                        one(U(NT - 1, 0)).then_inc(ping.sem, 1)

                        def square_group(u):
                            b = u.c % 2
                            src_full[b].take(te)
                            for j in range(GT):
                                first = u.c == 0 and isinstance(u.val, int) and u.val == 0 and j == 0
                                last_ = isinstance(u.val, int) and u.val == GT - 1 and j == GT - 1
                                x = te.matmul(psQ[:, 0:D], ones[:, 1 if last_ else 0, :], sq[:, b, j, :],
                                              start=first, stop=last_)
                            x.then_inc(src_free[b].sem, 1)
                        square_group(U(0, 0))
                        with te.Fori(0, 2) as i:
                            square_group(U(i * 2 + 1, 1))
                            square_group(U(i * 2 + 2, 2))
                        square_group(U(GT - 2, GT - 2))
                        square_group(U(GT - 1, GT - 1))

                    @block.scalar
                    def _(a):
                        for b in (0, 1):
                            src_free[b].give(a)

                        def square(u):
                            b = u.c % 2
                            res_full[0].take(a)
                            src_free[b].take(a)
                            a.activation(sq[:, b], grp(Y, u), ACT.Square).then_inc(src_full[b].sem, 1)
                        pipeline(a, GT, 2, [(0, square)])
                        for b in (0, 1):
                            src_free[b].take(a)
                        pong.give(a)
                        stats_done.take(a)
                        a.activation(mean[:, :], mean[:, :], ACT.Sqrt, bias=eps[:, 0:1]).then_inc(mid_full[0].sem, 1)

                    @block.vector
                    def _(v):
                        ping.take(v)
                        op(v.tensor_scalar(mean[:, :], psS[:, 0:D], 1.0 / N, None, ALU.mult), v, "v")

                        def center(u):
                            y = grp(Y, u)
                            op(v.tensor_tensor(y, y, mean[:, :].unsqueeze(1).to_broadcast([P, GT, D]), ALU.subtract), v, "v")
                            res_full[0].give(v)
                        pipeline(v, GT, 2, [(0, center)])
                        pong.take(v)
                        aux_full[0].take(v)
                        v.drain()
                        op(v.tensor_scalar(mean[:, :], psQ[:, 0:D], 1.0 / N, None, ALU.mult), v, "v")
                        stats_done.give(v)
                        mid_full[0].take(v)
                        op(v.reciprocal(mean[:, :], mean[:, :]), v, "v")
                        op(v.tensor_tensor(mean[:, :], mean[:, :], gb[:, 0, :], ALU.mult), v, "v")

                        def scale(u):
                            y = grp(Y, u)
                            op(v.tensor_tensor(y, y, mean[:, :].unsqueeze(1).to_broadcast([P, GT, D]), ALU.mult), v, "v")
                            op(v.tensor_tensor(y, y, gb[:, 1, :].unsqueeze(1).to_broadcast([P, GT, D]), ALU.add), v, "v")
                            finish(v, u, y)
                        if finish:
                            pipeline(v, GT, GT, [(0, scale)])

        def scatter_pass(SUP, room, table):
            Q = 4
            NQ = S // Q
            RB = 4
            at = 0

            def take(shape):
                nonlocal at
                v = part(room, at, shape)
                at += int(np.prod(shape))
                return v
            hot, same, srow, pairs = (take([2 * Q, P]) for _ in range(4))
            sums = take([RB, Q, D])
            source, row, away = (take([S]) for _ in range(3))
            lower, marked = take([P]), take([Q, P])
            with ExitStack() as ctx:
                dump_row = sb("dump_row", [P, 1], F32, ctx)
                start = sb("accumulator_start", [P, CHAINS], F32, ctx)
                earlier = sb("earlier", [P, 2, Q], F32, ctx)
                idx = sb("idx", [P, RB, Q], I32, ctx)
                psC = [bank(f"psC{b}", ctx) for b in (0, 1)]
                psO = [bank(f"psO{i}", ctx) for i in range(4)]
                s_scat = [Count(sem(f"s_scat{k}")) for k in range(CHAINS)]
                sums_full = [token(f"s_sums_full{b}") for b in range(RB)]
                with phase() as block:
                    @block.sync
                    def _(sp):
                        for g in range(GT):
                            sp.dma_start(table[g * GT * P:(g + 1) * GT * P, :].rearrange("(t p) c -> p t c", p=P),
                                         SUP[:, g * GT:(g + 1) * GT, :]).then_inc(s_st.sem, 16)
                            s_st.base += 16

                        def rows_in(u):
                            b = u.c % 2
                            src_free[b].take(sp)
                            sp.dma_start(srow[:, b * Q:(b + 1) * Q, :].rearrange("p q e -> p (q e)"),
                                         srcrow_d[bass.ds(u.val * Q, Q), :].rearrange("(a q) e -> a (q e)", a=1)
                                         .partition_broadcast(P).rearrange("p a e -> p (a e)")).then_inc(s_load[b].sem, 16)
                        pipeline(sp, NQ, 2, [(0, rows_in)])
                        sp.wait_ge(s_st.sem, s_st.base)

                    @block.gpsimd
                    def _(g):
                        op(g.memset(lower, 1.0), g, "p")
                        g.iota(dump_row[:, :], [[0, 1]], base=NP, channel_multiplier=1,
                               allow_small_or_imprecise_dtypes=True)
                        g.iota(start[:, :], [[ND, CHAINS]], base=0, channel_multiplier=0,
                               allow_small_or_imprecise_dtypes=True)
                        op(g.affine_select(out=lower, in_=lower, compare_op=ALU.is_gt, fill=0.0,
                                           base=0, pattern=[[-1, P]], channel_multiplier=1), g, "p")
                        aux_full[0].give(g)
                        g.wait_ge(s_zero.sem, s_zero.base)
                        nought, bound = g.alloc_register("nought"), g.alloc_register("last_row")
                        g.reg_mov(nought, 0)

                        def scatter(u):
                            b, half = u.c % RB, u.c % 2
                            idx_full[b].take(g)
                            sums_full[b].take(g)
                            for j in range(Q):
                                k = half * Q + j
                                if not isinstance(u.val, int) or u.val >= 2:
                                    s_scat[k].wait(g, (u.val - half) * (16 // 2))
                                g.reg_add(bound, nought, CHAINS * ND - 1)
                                g.indirect_dma_start(out=scat, out_offset=bass.IndirectOffsetOnAxis(ap=idx[:, b, j:j + 1], axis=0),
                                                     in_=sums[:, b, j, :], in_offset=None, bounds_check=bound,
                                                     oob_is_err=True, compute_op=ALU.add).then_inc(s_scat[k].sem, 16)

                        def landed(u):
                            b, half = u.c % RB, u.c % 2
                            if isinstance(u.val, int) and u.val >= NQ - 2:
                                for k in range(half * Q, half * Q + Q):
                                    s_scat[k].wait(g, NQ // 2 * 16)
                            slot_free[b].give(g)
                            slot_kept[b].give(g)
                        for b in range(RB):
                            slot_free[b].give(g)
                            slot_kept[b].give(g)
                        pipeline(g, NQ, RB, [(0, scatter), (2, landed)])
                        for b in range(RB):
                            slot_free[b].take(g)
                            slot_kept[b].take(g)

                    @block.scalar
                    def _(a):
                        def copyC(u):
                            b = u.c % 2
                            tr_full[b].take(a)
                            hot_free[b].give(a)
                            src_free[b].give(a)
                            a.activation(pairs[:, b * Q:(b + 1) * Q, :].rearrange("p q e -> p (q e)"), psC[b][:, :], ACT.Copy)\
                                .then_inc(lhs_full[b].sem, 1)

                        def copyO(u):
                            b = u.c % 2
                            slot_free[u.c % RB].take(a)
                            for j in range(2):
                                res_full[j].take(a)
                                op(a.activation(sums[:, u.c % RB, 2 * j:2 * j + 2, :].rearrange("p q c -> p (q c)"),
                                                psO[2 * b + j][:, :], ACT.Copy), a, "a")
                                res_free[j].give(a)
                            sums_full[u.c % RB].give(a)
                        for b in (0, 1):
                            hot_free[b].give(a)
                            src_free[b].give(a)
                            res_free[b].give(a)
                            res_free[b].give(a)
                        pipeline(a, NQ, RB, [(0, copyC), (1, copyO)])
                        for b in (0, 1):
                            hot_free[b].take(a)
                            src_free[b].take(a)
                            res_free[b].take(a, 2)

                    @block.tensor
                    def _(te):
                        regs = [te.alloc_register(f"nt_sc{j}") for j in range(Q)]

                        def pairmm(u):
                            b = u.c % 2
                            hot_full[b].take(te)
                            for j in range(Q):
                                x = te.matmul(psC[b][:, j * P:(j + 1) * P], hot[:, b * Q + j, :], same[:, b * Q + j, :],
                                              start=True, stop=True)
                            x.then_inc(tr_full[b].sem, 1)

                        def summm(u):
                            b = u.c % 2
                            te.load(regs, ntab[0:1, bass.ds(u.val * Q, Q)])
                            nt = [te.snap(r, min_val=0, max_val=NT - 1) for r in regs]
                            lhs_full[b].take(te)
                            for j in range(Q):
                                if j % 2 == 0:
                                    res_free[j // 2].take(te)
                                x = te.matmul(psO[2 * b + j // 2][:, j % 2 * D:(j % 2 + 1) * D], pairs[:, b * Q + j, :],
                                              at_tile(SUP, nt[j]), start=True, stop=True)
                                if j % 2:
                                    x.then_inc(res_full[j // 2].sem, 1)
                        pipeline(te, NQ, 2, [(0, pairmm), (1, summm)])

                    @block.vector
                    def _(v):
                        aux_full[0].take(v)
                        op(v.tensor_copy(source, gidx[:, :]), v, "v")
                        v.tensor_tensor(row.rearrange("p (n k) -> p n k", k=CHAINS),
                                        source.rearrange("p (n k) -> p n k", k=CHAINS),
                                        start[:, :].unsqueeze(1).to_broadcast([P, S // CHAINS, CHAINS]), ALU.add)
                        op(v.tensor_scalar(away, source, -1.0, dump_row[:, 0:1], ALU.mult, ALU.add), v, "v")

                        def marks(u):
                            b, rb = u.c % 2, u.c % RB
                            hot_free[b].take(v)
                            src = [source[:, bass.ds(u.val * Q + j, 1)] for j in range(Q)]
                            steps = bass.ds(u.val * Q, Q)
                            for j in range(Q):
                                one_hot(v, hot[:, b * Q:(b + 1) * Q], j, u.val * Q + j, True)
                            s_load[b].wait(v, (u.val - b) * (16 // 2) + 16)
                            for j in range(Q):
                                x = v.scalar_tensor_tensor(out=marked[:, j, :], in0=srow[:, b * Q + j, :], scalar=src[j], in1=lower,
                                                           op0=ALU.is_equal, op1=ALU.mult, accum_out=earlier[:, b, j:j + 1])
                            x.then_inc(link["v"].sem, 1)
                            for j in range(Q):
                                x = v.tensor_scalar(same[:, b * Q + j, :], srow[:, b * Q + j, :], src[j], None, ALU.is_equal)
                            x.then_inc(hot_full[b].sem, 1)
                            link["v"].take(v)
                            op(v.scalar_tensor_tensor(out=earlier[:, b, :], in0=earlier[:, b, :], scalar=0.0, in1=away[:, steps],
                                                      op0=ALU.is_gt, op1=ALU.mult), v, "v")
                            slot_kept[rb].take(v)
                            v.tensor_tensor(idx[:, rb, :], earlier[:, b, :], row[:, steps], ALU.add)\
                                .then_inc(idx_full[rb].sem, 1)
                        pipeline(v, NQ, RB, [(0, marks)])
            for b in (0, 1):
                s_load[b].base += 16 * NQ // 2

        def attention_fetch3(LG, SV, rows_room, T_room):
            G = part(rows_room, 0, [RING, GS, WT])
            s_rows = rows_count("att3_", RING)
            with ExitStack() as ctx:
                hot = part(T_room, 0, [2 * GS, P])
                hotT = part(T_room, 2 * GS * P, [2 * GS, P])
                raw = sb("raw_logits", [P, GS, HEADS3], F32, ctx)
                idx = sb("idx", [P, RING, GS], I32, ctx)
                psT = [[bank(f"psT{b}{k}", ctx) for k in (0, 1)] for b in (0, 1)]
                psS = [bank(f"psS{b}", ctx) for b in (0, 1)]
                with phase() as block:
                    @block.sync
                    def _(sp):
                        def keep(u):
                            b = u.c % RING
                            s_rows[b].wait(sp, (u.val - b) * (16 * GS // RING) + 16 * GS)
                            sp.dma_start(Eb[bass.ds(u.val, 1), :, :].rearrange("a p (s c) -> p (a s) c", c=D),
                                         G[:, b, :, 0:D]).then_inc(s_keep[b].sem, 16)
                            s_keep[b].wait(sp, (u.val - b) * (16 // RING) + 16)
                            slot_kept[b].give(sp)
                        for b in range(RING):
                            slot_kept[b].give(sp)
                        pipeline(sp, NG, RING, [(0, keep)])
                        for b in range(RING):
                            slot_kept[b].take(sp)

                    @block.gpsimd
                    def _(g):
                        top_row = g.to_reg(NP - 1)

                        def fetch(u):
                            b = u.c % RING
                            idx_full[b].take(g)
                            for j in range(GS):
                                g.indirect_dma_start(out=G[:, b, j, :], out_offset=None, in_=T4,
                                                     in_offset=bass.IndirectOffsetOnAxis(ap=idx[:, b, j:j + 1], axis=0),
                                                     bounds_check=top_row, oob_is_err=True).then_inc(s_rows[b].sem, 16)
                        pipeline(g, NG, RING, [(0, fetch)])

                    @block.scalar
                    def _(a):
                        def index(u):
                            b = u.c % RING
                            slot_free[b].take(a)
                            slot_kept[b].take(a)
                            a.activation(idx[:, b, :], gidx[:, bass.ds(u.val * GS, GS)], ACT.Copy)\
                                .then_inc(idx_full[b].sem, 1)

                        def copyT(u):
                            b = u.c % 2
                            tr_full[b].take(a)
                            for k in (0, 1):
                                x = a.activation(hotT[:, b * GS + 4 * k:b * GS + 4 * k + 4, :].rearrange("p j n -> p (j n)"),
                                                 psT[b][k][:, :], ACT.Copy)
                            x.then_inc(lhs_full[b].sem, 1)
                        pipeline(a, NG, RING, [(0, index), (2, copyT)])

                    @block.tensor
                    def _(te):
                        regs = [te.alloc_register(f"nt_att3{j}") for j in range(GS)]

                        def trans(u):
                            b = u.c % 2
                            hot_full[b].take(te)
                            for j in range(GS):
                                x = te.transpose(psT[b][j // 4][:, j % 4 * P:(j % 4 + 1) * P], hot[:, b * GS + j, :], ident[:, :])
                            x.then_inc(tr_full[b].sem, 1)

                        def scores(u):
                            b = u.c % 2
                            nt = ntile(te, u, regs)
                            lhs_full[b].take(te)
                            res_free[b].take(te)
                            for j in range(GS):
                                x = te.matmul(psS[b][:, j * HEADS3:(j + 1) * HEADS3], hotT[:, b * GS + j, :],
                                              at_tile(SV, nt[j]), start=True, stop=True)
                            x.then_inc(res_full[b].sem, 1)
                        pipeline(te, NG, RING, [(2, trans), (3, scores)])

                    @block.vector
                    def _(v):
                        op(v.memset(LG[:, :, :], 0.0), v, "v")
                        for b in range(RING):
                            slot_free[b].give(v)
                        for b in (0, 1):
                            res_free[b].give(v)

                        def hots(u):
                            b = u.c % 2
                            for j in range(GS):
                                x = one_hot(v, hot[:, b * GS:(b + 1) * GS], j, u.val * GS + j, False)
                            x.then_inc(hot_full[b].sem, 1)

                        def logits(u):
                            b, gb = u.c % 2, u.c % RING
                            s_rows[gb].wait(v, (u.val - gb) * (16 * GS // RING) + 16 * GS)
                            res_full[b].take(v)
                            op(v.tensor_tensor(raw[:, :, :], G[:, gb, :, D:WT],
                                               psS[b][:, 0:GS * HEADS3].rearrange("p (s h) -> p s h", h=HEADS3), ALU.add), v, "v")
                            slot_free[gb].give(v)
                            res_free[b].give(v)
                            op(v.scalar_tensor_tensor(out=LG[:, bass.ds(u.val * GS, GS), :], in0=raw[:, :, :], scalar=0.2,
                                                      in1=raw[:, :, :], op0=ALU.mult, op1=ALU.max), v, "v")
                        pipeline(v, NG, RING, [(2, logits), (0, hots)])
                        for b in range(RING):
                            slot_free[b].take(v)
                        for b in (0, 1):
                            res_free[b].take(v)
            for b in range(RING):
                s_keep[b].base += 16 * NG // RING

        ln_stats(B256)
        XL, XR, H0 = B256, A256, C256

        def w0(sp, W, rows, mb):
            load(sp, W[:, 0:2, 0:D], kchunks(t["L0_gnn_W_l"]))
            load(sp, W[:, 0:2, D:2 * D], kchunks(t["L0_gnn_W_r"]))
            load(sp, rows[:, 0, :], bcast_row(t["L0_gnn_bias"]))
            load(sp, rows[:, 1, :], bcast_row(t["L0_gnn_att"].rearrange("h c -> (h c)")))

        def post0(v, u, ps, rows):
            v.tensor_copy(at_tile(XL, u.val), ps[:, 0:D])
            return v.tensor_copy(at_tile(XR, u.val), ps[:, D:2 * D])

        SL = sb("self_logits", [P, NT, HEADS0])
        with ExitStack() as ctx:
            f = sb("self_feat", [P, 4, D], F32, ctx)

            def self_sum(v, u, rows):
                b = u.c % 4
                s_add.wait(v, u.val + 3)
                v.tensor_tensor(f[:, b, :], at_tile(XL, u.val), at_tile(XR, u.val), ALU.add)\
                    .then_inc(link["v"].sem, 1)

            def self_leak(v, u, rows):
                b = u.c % 4
                link["v"].take(v)
                v.scalar_tensor_tensor(out=f[:, b, :], in0=f[:, b, :], scalar=0.2, in1=f[:, b, :],
                                       op0=ALU.mult, op1=ALU.max).then_inc(slot_free[b].sem, 1)

            def self_weigh(g, rows):
                def one(u):
                    b = u.c % 4
                    slot_free[b].take(g)
                    h = at_tile(H0, u.val)
                    g.tensor_tensor(h, h, rows[:, 0, :], ALU.add)
                    g.tensor_tensor(f[:, b, :], f[:, b, :], rows[:, 1, :], ALU.mult).then_inc(slot_kept[b].sem, 1)
                pipeline(g, NT, 8, [(0, one)])

            def self_logit(v, u, rows):
                b = u.c % 4
                slot_kept[b].take(v)
                v.tensor_reduce(at_tile(SL, u.val), f[:, b, :].rearrange("p (h c) -> p h c", h=HEADS0), AX.X, ALU.add)

            dense_loop(1, 2 * D, w0, ln_pre(B256, H0), post0, nrows=2, save=[(T0, XL)],
                       beside=lambda a: zero_sums(a, range(0, 3)),
                       vector_stages=[(2, self_leak), (1, self_sum), (3, self_logit)], gpsimd=self_weigh)

        with ExitStack() as L0:
            LG = sb("logits0", [P, SP_, HEADS0], F32, L0)
            attc = sb("att_cols", [P, 2, HEADS0], F32, L0)
            attention_fetch0(LG, attc, B)
            PK = sb("peaks", [P, SP_, HEADS0], F32, L0)
            LS = sb("last_marks", [P, SP_], F32, L0)
            segment_softmax(LG, LG[:, :, :], HEADS0, (A, B), last=LS[:, :], peak=PK,
                            beside=lambda a: zero_sums(a, range(3, CHAINS)))
            WB = D + 2 * HEADS0 + 1
            ACCB = tiles(B, WB)
            attention_sum("a0", LG, HEADS0, True, [(PK, HEADS0), (LS[:, :].unsqueeze(2), 1)],
                          ACCB, B[:, 0:NT * WB], A)
            with ExitStack() as ctx:
                xl = part(A, 0, [GT, D])
                sm = [sb(f"small{k}", [P, GT, HEADS0], F32, ctx) for k in range(4)]
                with phase() as block:
                    @block.sync
                    def _(sp):
                        def group(u):
                            src_free[0].take(sp)
                            sp.dma_start(xl[:, :, :], T0[bass.ds(u.val * (GT * P), GT * P), :].rearrange("(t p) c -> p t c", p=P))\
                                .then_inc(s_load[0].sem, 16)
                        pipeline(sp, GT, GT, [(0, group)])

                    @block.scalar
                    def _(a):
                        def exps(u):
                            src_full[0].take(a)
                            op(a.activation(sm[0][:, :, :], sm[0][:, :, :], ACT.Exp), a, "a")
                            a.activation(sm[1][:, :, :], sm[1][:, :, :], ACT.Exp).then_inc(src_full[1].sem, 1)
                        pipeline(a, GT, GT, [(0, exps)])

                    @block.vector
                    def _(v):
                        src_free[0].give(v)

                        def join(u):
                            acc = ACCB[:, bass.ds(u.val * GT, GT), :]
                            wsum, peak, hit = acc[:, :, D:D + 4], acc[:, :, D + 4:D + 8], acc[:, :, D + 8:D + 9]
                            e, s_, x2, x3 = (k[:, :, :] for k in sm)
                            sl = SL[:, bass.ds(u.val * GT, GT), :]
                            bw = [P, GT, HEADS0]
                            op(v.tensor_scalar(x2[:, :, 0:1], hit, -1.0, BIG, ALU.add, ALU.mult), v, "v")
                            op(v.tensor_tensor(e, peak, x2[:, :, 0:1].to_broadcast(bw), ALU.add), v, "v")
                            op(v.tensor_tensor(x3, e, sl, ALU.max), v, "v")
                            op(v.tensor_tensor(e, e, x3, ALU.subtract), v, "v")
                            op(v.tensor_tensor(s_, sl, x3, ALU.subtract), v, "v")
                            src_full[0].give(v)
                            src_full[1].take(v)
                            op(v.tensor_tensor(x2, wsum, e, ALU.mult), v, "v")
                            op(v.tensor_tensor(x2, x2, s_, ALU.add), v, "v")
                            op(v.tensor_scalar(x2, x2, 1e-16, None, ALU.add), v, "v")
                            op(v.reciprocal(x2, x2), v, "v")
                            op(v.tensor_tensor(e, e, x2, ALU.mult), v, "v")
                            op(v.tensor_tensor(s_, s_, x2, ALU.mult), v, "v")
                            heads_of = lambda z: z.rearrange("p t (h c) -> p t h c", h=HEADS0)
                            wide = [P, GT, HEADS0, D // HEADS0]
                            rows_ = acc[:, :, 0:D]
                            op(v.tensor_tensor(heads_of(rows_), heads_of(rows_), e.unsqueeze(3).to_broadcast(wide), ALU.mult), v, "v")
                            s_load[0].wait(v, u.val * 16 + 16)
                            op(v.tensor_tensor(heads_of(xl[:, :, :]), heads_of(xl[:, :, :]), s_.unsqueeze(3).to_broadcast(wide),
                                               ALU.mult), v, "v")
                            op(v.tensor_tensor(rows_, rows_, xl[:, :, :], ALU.add), v, "v")
                            src_free[0].give(v)
                            h = grp(C256, u)
                            op(v.tensor_tensor(h, h, rows_, ALU.add), v, "v")
                        pipeline(v, GT, GT, [(0, join)])
                        src_free[0].take(v)
                        v.memset(B256[:, NT - 1, :], 0.0)
                s_load[0].base += 16 * GT

        def reload(sp):
            sp.dma_start(B256[:, 0:NT - 1, :], t["x"][0:(NT - 1) * P, :].rearrange("(t p) c -> p t c", p=P))\
                .then_inc(s_back.sem, 16)
            sp.dma_start(B256[0:TAIL, NT - 1, :], t["x"][(NT - 1) * P:N, :]).then_inc(s_back.sem, 16)
            s_back.base += 32

        norm_ctx = top.enter_context(ExitStack())
        scale_ = sb("norm_scale", [P, D], F32, norm_ctx)
        gamma_beta = sb("gamma_beta", [P, 2, D], F32, norm_ctx)
        column_norm(C256, t["L0_gnn_gamma1"], t["L0_gnn_beta1"], None, scale_, gamma_beta, reload)

        def w_ffn(sp, W, rows, mb):
            load(sp, W[:, 2:4, :], kchunks(t["L0_gnn_W1"]))
            load(sp, W[:, 0:2, :], kchunks(t["L0_gnn_W2"]))
            load(sp, rows[:, 0, :], bcast_row(t["L0_gnn_b2"]))
            load(sp, mb[:, :], t["L0_gnn_b1"].rearrange("(k p) -> p k", p=P), allow_slow_non_contiguous=True)

        def copy_pre(a, u, hs):
            return a.activation(hs[:, 0, :], at_tile(C256, u.val), ACT.Copy)

        def post_ffn(v, u, ps, rows):
            y = at_tile(C256, u.val)
            op(v.tensor_tensor(y, y, ps[:, 0:D], ALU.add), v, "v")
            return v.tensor_tensor(y, y, rows[:, 0, :], ALU.add)

        def norm_mult(v, u):
            y = at_tile(C256, u.val)
            return v.tensor_tensor(y, y, scale_[:, :], ALU.mult)

        def norm_shift(v, u):
            y = at_tile(C256, u.val)
            return v.tensor_tensor(y, y, gamma_beta[:, 1, :], ALU.add)

        dense_loop(1, D, w_ffn, copy_pre, post_ffn, mid_bias=True, nrows=1, prepare=(norm_mult, norm_shift))
        def add_residual(v, u, y):
            x = grp(B256, u)
            if isinstance(u.val, int) and u.val == 0:
                v.wait_ge(s_back.sem, s_back.base)
            op(v.tensor_tensor(x, x, y, ALU.add), v, "v")

        column_norm(C256, t["L0_gnn_gamma2"], t["L0_gnn_beta2"], add_residual, scale_, gamma_beta)
        norm_ctx.close()

        ln_stats(B256)

        def w_one(name):
            def w(sp, W, rows, mb):
                load(sp, W[:, 0:2, :], kchunks(t[name]))
            return w

        def post_support(v, u, ps, rows):
            return v.tensor_copy(at_tile(A256, u.val), ps[:, 0:D])

        dense_loop(1, D, w_one("L1_gnn_weight"), ln_pre(B256), post_support)
        scatter_pass(A256, C, T1)
        plain_pass("l1", T1, B256, None, D, True, fold=(t["L1_gnn_bias"], A))

        ln_stats(B256)
        with phase() as block:
            @block.scalar
            def _(a):
                def norm(u):
                    x = a.activation(at_tile(A256, u.val), at_tile(B256, u.val), ACT.Relu,
                                     bias=nmr[:, bass.ds(u.val, 1)], scale=rstd[:, bass.ds(u.val, 1)])
                    if u.c % GT == GT - 1:
                        x.then_inc(res_full[0].sem, 1)
                pipeline(a, NT, GT, [(0, norm)])

            @block.sync
            def _(sp):
                for g in range(GT):
                    res_full[0].take(sp)
                    sp.dma_start(T2[g * GT * P:(g + 1) * GT * P, :].rearrange("(t p) c -> p t c", p=P),
                                 A256[:, g * GT:(g + 1) * GT, :]).then_inc(s_st.sem, 16)
                    s_st.base += 16
                sp.wait_ge(s_st.sem, s_st.base)
        WC = D + 1
        ACC1 = tiles(C, WC)
        plain_pass("l2a", T2, ACC1, C[:, 0:NT * WC], WC, False, own=(A256, "L2_gnn_W1_self", "L2_gnn_b1_self"))

        def conv_weights(k):
            def w(sp, W, rows, mb):
                load(sp, W[:, 0:2, :], kchunks(t[f"L2_gnn_W{k}_msg"]))
                load(sp, rows[:, 0, :], bcast_row(t[f"L2_gnn_b{k}_msg"]))
            return w

        def sums_pre(acc):
            def pre(a, u, hs):
                return a.activation(hs[:, 0, :], acc[:, bass.ds(u.val, 1), 0:D].rearrange("p a c -> p (a c)"), ACT.Copy)
            return pre

        def post_conv1(v, u, ps, rows):
            y = at_tile(A256, u.val)
            dg = ACC1[:, bass.ds(u.val, 1), D:D + 1].rearrange("p a c -> p (a c)")
            v.tensor_copy(deg[:, bass.ds(u.val, 1)], dg)
            op(v.tensor_tensor(y, y, ps[:, 0:D], ALU.add), v, "v")
            op(v.scalar_tensor_tensor(out=y, in0=rows[:, 0, :], scalar=dg, in1=y, op0=ALU.mult, op1=ALU.add), v, "v")
            return v.scalar_tensor_tensor(out=y, in0=y, scalar=0.1, in1=y, op0=ALU.mult, op1=ALU.max)

        dense_loop(1, D, conv_weights(1), sums_pre(ACC1), post_conv1, nrows=1, save=[(T3, A256)])
        plain_pass("l2b", T3, C256, C[:, 0:NT * D], D, False, own=(A256, "L2_gnn_W2_self", "L2_gnn_b2_self"))

        def post_conv2(v, u, ps, rows):
            x = at_tile(B256, u.val)
            op(v.tensor_tensor(x, x, at_tile(A256, u.val), ALU.add), v, "v")
            op(v.scalar_tensor_tensor(out=x, in0=rows[:, 0, :], scalar=deg[:, bass.ds(u.val, 1)], in1=x,
                                      op0=ALU.mult, op1=ALU.add), v, "v")
            return v.tensor_tensor(x, x, ps[:, 0:D], ALU.add)

        dense_loop(1, D, conv_weights(2), sums_pre(C256), post_conv2, nrows=1)

        ln_stats(B256)
        H4 = tiles(A, WT)
        with ExitStack() as L3:
            LG3 = sb("logits3", [P, SP_, HEADS3], F32, L3)
            SV = sb("dst_scores", [P, NT, HEADS3], F32, L3)

            def w_uv(sp, W, rows, mb):
                load(sp, W[:, 0:2, 0:2 * HEADS3], kchunks(t["W_uv"]))
                load(sp, rows[:, 0, 0:HEADS3], bcast_row(t["L3_gnn_b_u"]))

            def pre_uv(a, u, hs):
                scale, bias = rstd[:, bass.ds(u.val, 1)], nmr[:, bass.ds(u.val, 1)]
                a.activation(H4[:, bass.ds(u.val, 1), 0:D].rearrange("p a c -> p (a c)"), at_tile(B256, u.val),
                             ACT.Relu, bias=bias, scale=scale)
                return a.activation(hs[:, 0, :], at_tile(B256, u.val), ACT.Relu, bias=bias, scale=scale)

            def post_uv(v, u, ps, rows):
                v.tensor_tensor(H4[:, bass.ds(u.val, 1), D:WT].rearrange("p a c -> p (a c)"), ps[:, 0:HEADS3],
                                rows[:, 0, 0:HEADS3], ALU.add)
                return v.tensor_copy(at_tile(SV, u.val), ps[:, HEADS3:2 * HEADS3])

            dense_loop(1, 2 * HEADS3, w_uv, pre_uv, post_uv, nrows=1, save=[(T4, H4)])
            attention_fetch3(LG3, SV, C, A)
            segment_softmax(LG3, LG3[:, :, :], HEADS3, (A, C))
            ACC3 = tiles(C, WT)
            attention_sum("a3", LG3, HEADS3, False, [], ACC3, C[:, 0:NT * WT], A)
            with ExitStack() as ctx:
                rd = sb("denominators", [P, GT, HEADS3], F32, ctx)
                with phase() as block:
                    @block.vector
                    def _(v):
                        def final(u):
                            acc = ACC3[:, bass.ds(u.val * GT, GT), :]
                            op(v.tensor_scalar(rd[:, :, :], acc[:, :, D:WT], 0.5, None, ALU.max), v, "v")
                            op(v.reciprocal(rd[:, :, :], rd[:, :, :]), v, "v")
                            rows_ = acc[:, :, 0:D].rearrange("p t (c h) -> p t c h", h=HEADS3)
                            op(v.tensor_tensor(rows_, rows_, rd[:, :, :].unsqueeze(2).to_broadcast([P, GT, D // HEADS3, HEADS3]),
                                               ALU.mult), v, "v")
                            x = grp(B256, u)
                            op(v.tensor_tensor(x, x, acc[:, :, 0:D], ALU.add), v, "v")
                            res_full[0].give(v)
                        pipeline(v, GT, GT, [(0, final)])

                    @block.sync
                    def _(sp):
                        for g in range(GT - 1):
                            res_full[0].take(sp)
                            sp.dma_start(out[g * GT * P:(g + 1) * GT * P, :].rearrange("(t p) c -> p t c", p=P),
                                         B256[:, g * GT:(g + 1) * GT, :]).then_inc(s_st.sem, 16)
                        res_full[0].take(sp)
                        g = GT - 1
                        sp.dma_start(out[g * GT * P:(NT - 1) * P, :].rearrange("(t p) c -> p t c", p=P),
                                     B256[:, g * GT:NT - 1, :]).then_inc(s_st.sem, 16)
                        sp.dma_start(out[(NT - 1) * P:N, :], B256[0:TAIL, NT - 1, :]).then_inc(s_st.sem, 16)
                        s_st.base += 16 * (GT + 1)
                        sp.wait_ge(s_st.sem, s_st.base)


_INS = ['x', 'L0_gnn_W_l', 'L0_gnn_W_r', 'L0_gnn_att', 'L0_gnn_bias', 'L0_gnn_W1', 'L0_gnn_b1', 'L0_gnn_W2',
        'L0_gnn_b2', 'L0_gnn_gamma1', 'L0_gnn_beta1', 'L0_gnn_gamma2', 'L0_gnn_beta2', 'L1_gnn_weight',
        'L1_gnn_bias', 'L1_gnn_alpha', 'L2_gnn_W1_msg', 'L2_gnn_b1_msg', 'L2_gnn_W1_self', 'L2_gnn_b1_self',
        'L2_gnn_W2_msg', 'L2_gnn_b2_msg', 'L2_gnn_W2_self', 'L2_gnn_b2_self', 'L3_gnn_b_u']


def kernel(**inputs):
    import concourse.bacc as bacc
    from concourse.bass_utils import run_bass_kernel_spmd as run

    nc = bacc.Bacc("TRN2", target_bir_lowering=False, num_devices=1)
    arrays, t = {}, {}

    def give(name, a):
        a = np.ascontiguousarray(a)
        arrays[f"in_{name}"] = a
        t[name] = nc.dram_tensor(f"in_{name}", a.shape, mybir.dt.from_np(a.dtype), kind="ExternalInput").ap()

    for name in _INS:
        give(name, inputs[name])
    pad = EP - E
    dst = np.pad(np.asarray(inputs["dst"]), (0, pad), constant_values=N).reshape(ET, P)
    src = np.pad(np.asarray(inputs["src"]), (0, pad)).reshape(ET, P)
    typ = np.pad(np.asarray(inputs["edge_type_11"]), (0, pad), constant_values=RELS).reshape(ET, P)
    give("edge_tiles", np.concatenate([dst, src, typ], axis=1))
    give("dst_last", dst[:, P - 1])
    give("W_uv", np.concatenate([np.asarray(inputs["L3_gnn_W_u"]).T, np.asarray(inputs["L3_gnn_W_v"]).T], axis=1))
    out = nc.dram_tensor("out0", (N, D), F32, kind="ExternalOutput").ap()
    build(nc, t, out)
    r = run(nc, [arrays], core_ids=[0])
    return r.results[0]["out0"]
```
